# Optimizing a Trainium2 kernel written in Bass

```python
import numpy as np
import jax
import jax.numpy as jnp

def _softmax(x, axis=-1):
    return jax.nn.softmax(x, axis=axis)

def _gelu(x):
    return jax.nn.gelu(x, approximate=True)

def _silu(x):
    return jax.nn.silu(x)

def _sigmoid(x):
    return jax.nn.sigmoid(x)

def _layernorm(x, axis=-1, eps=1e-05):
    m = jnp.mean(x, axis=axis, keepdims=True)
    v = jnp.var(x, axis=axis, keepdims=True)
    return (x - m) / jnp.sqrt(v + eps)

def _scatter_add(tgt, idx, src, axis=0):
    return tgt.at[idx].add(src)

def _segment_sum(src, seg, n):
    return jax.ops.segment_sum(src, seg, n)
kernel_name = 'mk_prb_d2_jaxref_r4_4eaf77'

def setup_inputs(seed: int=0):
    np.random.seed(seed)
    _w = jnp.asarray

    def _L0_attn_setup():
        import jax, jax.numpy as jnp
        import numpy as np
        NUM_HEADS = 16
        key = jax.random.key(seed)
        k1, k2, k3 = jax.random.split(key, 3)
        B, D, N = (2, 512, 256)
        x = jax.random.normal(k1, (B, D, N), dtype=jnp.float32)
        W_qkv = jax.random.normal(k2, (N, 3 * N), dtype=jnp.float32) * (1.0 / np.sqrt(N))
        b_qkv = jax.random.normal(k3, (3 * N,), dtype=jnp.float32) * 0.01
        return {'x': x, 'W_qkv': W_qkv, 'b_qkv': b_qkv}
    _L0_attn_in = _L0_attn_setup()

    def _L0_ffn_setup():
        import jax, jax.numpy as jnp
        import numpy as np
        E, D, F = (8, 256, 1024)
        B, S = (4, 512)

        def _layernorm(x, g, b, eps=1e-05):
            mu = jnp.mean(x, axis=-1, keepdims=True)
            var = jnp.var(x, axis=-1, keepdims=True)
            return (x - mu) * jax.lax.rsqrt(var + eps) * g + b
        key = jax.random.key(seed)
        ks = jax.random.split(key, 5)
        return {'input_features': jax.random.normal(ks[0], (B, S, D), jnp.float32), 'centroids': jax.random.normal(ks[1], (E, D), jnp.float32) * 0.1, 'ln_g': jnp.ones((E, D), jnp.float32), 'ln_b': jnp.zeros((E, D), jnp.float32), 'w1': jax.random.normal(ks[2], (E, F, D), jnp.float32) * (1.0 / np.sqrt(D).astype(np.float32)), 'b1': jnp.zeros((E, F), jnp.float32), 'w2': jax.random.normal(ks[3], (E, D, F), jnp.float32) * (1.0 / np.sqrt(F).astype(np.float32)), 'b2': jnp.zeros((E, D), jnp.float32)}
    _L0_ffn_in = _L0_ffn_setup()

    def _L1_attn_setup():
        import jax, jax.numpy as jnp
        import numpy as np
        import math
        D_MODEL = 256
        NUM_HEADS = 16
        HEAD_DIM = D_MODEL // NUM_HEADS
        B, S = (2, 512)

        def _causal_attn(q, k, v):
            scale = 1.0 / math.sqrt(q.shape[-1])
            scores = jnp.einsum('bthd,bshd->bhts', q, k) * scale
            t = q.shape[1]
            mask = jnp.tril(jnp.ones((t, t), dtype=bool))
            scores = jnp.where(mask, scores, -jnp.inf)
            attn = jax.nn.softmax(scores, axis=-1)
            return jnp.einsum('bhts,bshd->bthd', attn, v)
        key = jax.random.key(seed)
        ks = jax.random.split(key, 7)
        sc = 0.02
        return {'x': jax.random.normal(ks[0], (B, S, D_MODEL), dtype=jnp.float32), 'Wqkv_w': jax.random.normal(ks[1], (3 * D_MODEL, D_MODEL), dtype=jnp.float32) * sc, 'Wqkv_b': jnp.zeros((3 * D_MODEL,), dtype=jnp.float32), 'conv_w': jax.random.normal(ks[2], (D_MODEL, D_MODEL, 3), dtype=jnp.float32) * sc, 'conv_b': jnp.zeros((D_MODEL,), dtype=jnp.float32), 'out_w': jax.random.normal(ks[3], (D_MODEL, D_MODEL), dtype=jnp.float32) * sc, 'out_b': jnp.zeros((D_MODEL,), dtype=jnp.float32)}
    _L1_attn_in = _L1_attn_setup()

    def _L1_ffn_setup():
        import jax, jax.numpy as jnp
        import numpy as np
        D_MODEL, D_FF, RANK = (256, 1024, 64)
        B, S = (4, 1024)
        key = jax.random.key(seed)
        ks = jax.random.split(key, 7)
        return {'x': jax.random.normal(ks[0], (B, S, D_MODEL), dtype=jnp.float32), 'U1': jax.random.normal(ks[1], (D_MODEL, RANK), dtype=jnp.float32) * 0.02, 'V1': jax.random.normal(ks[2], (RANK, D_FF), dtype=jnp.float32) * 0.02, 'b1': jnp.zeros((D_FF,), dtype=jnp.float32), 'U2': jax.random.normal(ks[3], (D_FF, RANK), dtype=jnp.float32) * 0.02, 'V2': jax.random.normal(ks[4], (RANK, D_MODEL), dtype=jnp.float32) * 0.02, 'b2': jnp.zeros((D_MODEL,), dtype=jnp.float32)}
    _L1_ffn_in = _L1_ffn_setup()
    _d = {'L0_attn_x': _L0_attn_in['x'], 'L0_attn_W_qkv': _L0_attn_in['W_qkv'], 'L0_attn_b_qkv': _L0_attn_in['b_qkv'], 'L0_ffn_centroids': _L0_ffn_in['centroids'], 'L0_ffn_ln_g': _L0_ffn_in['ln_g'], 'L0_ffn_ln_b': _L0_ffn_in['ln_b'], 'L0_ffn_w1': _L0_ffn_in['w1'], 'L0_ffn_b1': _L0_ffn_in['b1'], 'L0_ffn_w2': _L0_ffn_in['w2'], 'L0_ffn_b2': _L0_ffn_in['b2'], 'L1_attn_Wqkv_w': _L1_attn_in['Wqkv_w'], 'L1_attn_Wqkv_b': _L1_attn_in['Wqkv_b'], 'L1_attn_conv_w': _L1_attn_in['conv_w'], 'L1_attn_conv_b': _L1_attn_in['conv_b'], 'L1_attn_out_w': _L1_attn_in['out_w'], 'L1_attn_out_b': _L1_attn_in['out_b'], 'L1_ffn_U1': _L1_ffn_in['U1'], 'L1_ffn_V1': _L1_ffn_in['V1'], 'L1_ffn_b1': _L1_ffn_in['b1'], 'L1_ffn_U2': _L1_ffn_in['U2'], 'L1_ffn_V2': _L1_ffn_in['V2'], 'L1_ffn_b2': _L1_ffn_in['b2']}
    _x0 = _d['L0_attn_x']
    _d['L0_attn_x'] = jax.random.normal(jax.random.fold_in(jax.random.key(seed), 1), (8, 512, 256), dtype=_x0.dtype)
    del _x0
    return _d

def reference(L0_attn_x, L0_attn_W_qkv, L0_attn_b_qkv, L0_ffn_centroids, L0_ffn_ln_g, L0_ffn_ln_b, L0_ffn_w1, L0_ffn_b1, L0_ffn_w2, L0_ffn_b2, L1_attn_Wqkv_w, L1_attn_Wqkv_b, L1_attn_conv_w, L1_attn_conv_b, L1_attn_out_w, L1_attn_out_b, L1_ffn_U1, L1_ffn_V1, L1_ffn_b1, L1_ffn_U2, L1_ffn_V2, L1_ffn_b2):

    def _L0_attn_ref(x, W_qkv, b_qkv):
        import jax, jax.numpy as jnp
        import numpy as np
        NUM_HEADS = 16
        B, D, N = x.shape
        H = NUM_HEADS
        p = N // H
        qkv = (x @ W_qkv + b_qkv).reshape(B, D, 3, H, p).transpose(2, 0, 3, 1, 4)
        q, k, v = (qkv[0], qkv[1], qkv[2])
        scores = jax.nn.softmax(jnp.einsum('bhip,bhjp->bhij', q, k), axis=-1)
        out = jnp.einsum('bhij,bhjp->bhip', scores, v)
        return out.reshape(B, D, N)

    def _L0_ffn_ref(input_features, centroids, ln_g, ln_b, w1, b1, w2, b2):
        import jax, jax.numpy as jnp
        import numpy as np
        E, D, F = (8, 256, 1024)
        B, S = (4, 512)

        def _layernorm(x, g, b, eps=1e-05):
            mu = jnp.mean(x, axis=-1, keepdims=True)
            var = jnp.var(x, axis=-1, keepdims=True)
            return (x - mu) * jax.lax.rsqrt(var + eps) * g + b
        Bf, Sf, Df = input_features.shape
        x = input_features.reshape(-1, Df)
        aff = x @ centroids.T
        assign = jnp.argmax(aff, axis=1)
        order = jnp.argsort(assign)
        xs = x[order]
        es = assign[order]
        alpha = jax.nn.sigmoid(jnp.take_along_axis(aff[order], es[:, None], axis=1))
        nE = centroids.shape[0]
        y = jnp.zeros_like(xs)
        for e in range(nE):
            h = _layernorm(xs, ln_g[e], ln_b[e])
            h = jax.nn.relu(h @ w1[e].T + b1[e])
            ye = xs + h @ w2[e].T + b2[e]
            y = y + jnp.where((es == e)[:, None], ye, 0.0)
        out_sorted = alpha * y + (1.0 - alpha) * xs
        inv = jnp.argsort(order)
        return out_sorted[inv].reshape(Bf, Sf, Df)

    def _L1_attn_ref(x, Wqkv_w, Wqkv_b, conv_w, conv_b, out_w, out_b):
        import jax, jax.numpy as jnp
        import numpy as np
        import math
        D_MODEL = 256
        NUM_HEADS = 16
        HEAD_DIM = D_MODEL // NUM_HEADS
        B, S = (2, 512)

        def _causal_attn(q, k, v):
            scale = 1.0 / math.sqrt(q.shape[-1])
            scores = jnp.einsum('bthd,bshd->bhts', q, k) * scale
            t = q.shape[1]
            mask = jnp.tril(jnp.ones((t, t), dtype=bool))
            scores = jnp.where(mask, scores, -jnp.inf)
            attn = jax.nn.softmax(scores, axis=-1)
            return jnp.einsum('bhts,bshd->bthd', attn, v)
        b, s, d = x.shape
        qkv = x @ Wqkv_w.T + Wqkv_b
        qkv = qkv.reshape(b, s, 3, NUM_HEADS, HEAD_DIM)
        q, k, v = (qkv[:, :, 0], qkv[:, :, 1], qkv[:, :, 2])
        ctx = _causal_attn(q, k, v)
        ctx_c = ctx.reshape(b, s, d).transpose(0, 2, 1)
        conv_out = jax.lax.conv_general_dilated(ctx_c, conv_w, window_strides=(1,), padding=[(1, 1)], dimension_numbers=('NCH', 'OIH', 'NCH')) + conv_b[None, :, None]
        q2 = conv_out.transpose(0, 2, 1).reshape(b, s, NUM_HEADS, HEAD_DIM)
        ctx2 = _causal_attn(q2, k, v)
        out = ctx2.reshape(b, s, d) @ out_w.T + out_b
        return out

    def _L1_ffn_ref(x, U1, V1, b1, U2, V2, b2):
        import jax, jax.numpy as jnp
        import numpy as np
        D_MODEL, D_FF, RANK = (256, 1024, 64)
        B, S = (4, 1024)
        P = jnp.einsum('bsd,dr->bsr', x, U1)
        H = jax.nn.gelu(jnp.einsum('bsr,rf->bsf', P, V1) + b1)
        Q = jnp.einsum('bsf,fr->bsr', H, U2)
        return jnp.einsum('bsr,rd->bsd', Q, V2) + b2
    x = L0_attn_x
    xn = _layernorm(x, axis=-1)
    x = x + _L0_attn_ref(xn, L0_attn_W_qkv, L0_attn_b_qkv) + _L0_ffn_ref(xn, L0_ffn_centroids, L0_ffn_ln_g, L0_ffn_ln_b, L0_ffn_w1, L0_ffn_b1, L0_ffn_w2, L0_ffn_b2)
    xn = _layernorm(x, axis=-1)
    x = x + _L1_attn_ref(xn, L1_attn_Wqkv_w, L1_attn_Wqkv_b, L1_attn_conv_w, L1_attn_conv_b, L1_attn_out_w, L1_attn_out_b) + _L1_ffn_ref(xn, L1_ffn_U1, L1_ffn_V1, L1_ffn_b1, L1_ffn_U2, L1_ffn_V2, L1_ffn_b2)
    return x

_drawn_inputs = setup_inputs


def setup_inputs(seed=0):
    import zlib

    import numpy as np

    out = dict(_drawn_inputs(seed))
    spreads = {'L0_ffn_ln_g': (1.0, 0.2),
     'L0_ffn_ln_b': (0.0, 0.281),
     'L0_ffn_b1': (0.0, 0.277),
     'L0_ffn_b2': (0.0, 0.1),
     'L1_attn_Wqkv_b': (0.0, 0.558),
     'L1_attn_conv_b': (0.0, 0.8),
     'L1_attn_out_b': (0.0, 0.8),
     'L1_ffn_b1': (0.0, 0.8),
     'L1_ffn_b2': (0.0, 0.8)}
    factors = {'L0_attn_b_qkv': 7.923,
     'L1_attn_Wqkv_w': 8.0,
     'L1_attn_conv_w': 8.0,
     'L1_attn_out_w': 3.492,
     'L1_ffn_U1': 8.0,
     'L1_ffn_V1': 8.0,
     'L1_ffn_U2': 8.0,
     'L1_ffn_V2': 8.0}
    for name, (base, spread) in spreads.items():
        noise = np.random.default_rng([zlib.crc32(name.encode()), seed]).standard_normal(out[name].shape)
        drawn = base * np.exp(spread * noise) if base else spread * noise
        out[name] = jnp.asarray(drawn.astype(out[name].dtype))
    for name, factor in factors.items():
        out[name] = (out[name] * factor).astype(out[name].dtype)
    return out
```

```python
import concourse.bass as bass
from concourse import mybir
from contextlib import ExitStack

F32 = mybir.dt.float32
BF = mybir.dt.bfloat16
I32 = mybir.dt.int32
U32 = mybir.dt.uint32
ALU = mybir.AluOpType
ACT = mybir.ActivationFunctionType
AX = mybir.AxisListType

NB = 8
NT = 32
NE = 8
TM = 39
EPS = 1e-5
NEG = -(2.0 ** 127)
ENGINES = ("tensor", "vector", "scalar", "gpsimd", "sync")


class Queues:

    def __init__(self, nc, ctx):
        self.nc, self.ctx = nc, ctx
        self.items = {e: [] for e in ENGINES}
        self.sems, self.count = {}, {}
        self.seen = {e: {} for e in ENGINES}
        self.last = {}

    def sem(self, name):
        if name not in self.sems:
            self.sems[name] = self.ctx.enter_context(self.nc.semaphore(name))
            self.count[name] = 0
        return name

    def _wait(self, eng, after):
        need = {}
        for m in after:
            if m is not None and m[1] > self.seen[eng].get(m[0], 0):
                need[m[0]] = max(need.get(m[0], 0), m[1])
        for s, v in need.items():
            self.seen[eng][s] = v
            self.items[eng].append(("wait", s, v))

    def op(self, eng, fn, after=(), mark=True):
        self._wait(eng, after)
        if mark:
            s = self.sem("s_" + eng)
            self.count[s] += 1
            self.items[eng].append(("op", fn, s, 1))
            self.last[eng] = (s, self.count[s])
            return self.last[eng]
        self.items[eng].append(("op", fn, None, 0))
        return None

    def dma(self, name, fn, after=(), eng="sync"):
        self._wait(eng, after)
        s = self.sem(name)
        self.count[s] += 16
        self.items[eng].append(("op", fn, s, 16))
        return (s, self.count[s])

    def emit(self, block):
        for e in ENGINES:
            def body(handle, e=e):
                for it in self.items[e]:
                    if it[0] == "wait":
                        handle.wait_ge(self.sems[it[1]], it[2])
                    else:
                        r = it[1](handle)
                        if it[2] is not None:
                            r.then_inc(self.sems[it[2]], it[3])
            register = {"tensor": block.tensor, "vector": block.vector, "scalar": block.scalar,
                            "gpsimd": block.gpsimd, "sync": block.sync}
            register[e](body)


def build(nc, x, wqkv0, bqk0, bv0, cent, gb, w1, b1, w2, b2, wqkv1, bqk1, bv1, convw, convb,
          outw, outb, u1, v1, fb1, u2, v2, fb2, out):
    ctx = ExitStack()
    with ctx:
        Q = Queues(nc, ctx)
        op, dma = Q.op, Q.dma

        def sb(name, shape, dt=F32):
            return ctx.enter_context(nc.sbuf_tensor("t_" + name, shape, dt))

        def ps(name, shape):
            return ctx.enter_context(nc.psum_tensor("p_" + name, shape, F32))

        X = sb("X", [128, NT, 256])
        R1 = sb("R1", [128, 16384])
        R2 = sb("R2", [128, 16384])
        R3 = sb("R3", [128, 1632])
        r2b = R2[:, :].bitcast(BF)
        QA = [r2b[:, i * 4096:(i + 1) * 4096].rearrange("p (h n) -> p h n", h=8) for i in range(3)]
        KA = [r2b[:, (3 + i) * 4096:(4 + i) * 4096].rearrange("p (h n) -> p h n", h=8) for i in range(3)]
        P = [R2[:, 12288 + i * 2048:12288 + (i + 1) * 2048].rearrange("p (h n) -> p h n", h=4) for i in range(2)]
        V0 = [R3[:, i * 544:(i + 1) * 544].rearrange("p (k h d) -> p k h d", k=4, h=8) for i in range(3)]
        W1 = R1[:, :].rearrange("p (e n) -> p e n", e=NE)
        W2 = R2[:, 0:16384].rearrange("p (e n) -> p e n", e=NE)
        XT = R1[:, 0:8192].rearrange("p (c n) -> p c n", c=2)
        V1S = [R1[:, 8192 + i * 544:8192 + (i + 1) * 544].rearrange("p (k h d) -> p k h d", k=4, h=8)
               for i in range(8)]

        S1 = [ps("S1a", [128, 512]), ps("S1b", [128, 512])]
        S2 = [ps("S2a", [128, 2, 512]), ps("S2b", [128, 2, 512])]
        PV = ps("PV", [128, 512])
        M = ps("M", [128, 512])

        ident = sb("ident", [128, 128])
        identb = sb("identb", [128, 128], BF)
        maskq = sb("maskq", [128, 128], BF)
        maskk = sb("maskk", [128, 128], BF)
        G = "gpsimd"
        V = "vector"
        A = "scalar"
        T = "tensor"

        zi = op(G, lambda e: nc.gpsimd.memset(ident[:, :], 0.0))
        zb = op(G, lambda e: nc.gpsimd.memset(identb[:, :], 0.0))
        zq = op(G, lambda e: nc.gpsimd.memset(maskq[:, :], 0.0))
        zk = op(G, lambda e: nc.gpsimd.memset(maskk[:, :], 0.0))
        mident = op(G, lambda e: nc.gpsimd.affine_select(out=ident[:, :], in_=ident[:, :], compare_op=ALU.not_equal,
                    fill=1.0, base=0, pattern=[[-1, 128]], channel_multiplier=1), [zi])
        op(G, lambda e: nc.gpsimd.affine_select(out=identb[:, :], in_=identb[:, :], compare_op=ALU.not_equal,
                    fill=1.0, base=0, pattern=[[-1, 128]], channel_multiplier=1), [zb])
        op(G, lambda e: nc.gpsimd.affine_select(out=maskq[:, :], in_=maskq[:, :], compare_op=ALU.is_ge,
                    fill=1.0, base=0, pattern=[[-1, 128]], channel_multiplier=1), [zq])
        mconst = op(G, lambda e: nc.gpsimd.affine_select(out=maskk[:, :], in_=maskk[:, :], compare_op=ALU.is_ge,
                    fill=1.0, base=0, pattern=[[1, 128]], channel_multiplier=-1), [zk])

        m_ = op(V, lambda e: nc.vector.tensor_scalar(maskq[:, :], maskq[:, :], NEG, None, ALU.mult), [mconst])
        mconst = op(V, lambda e: nc.vector.tensor_scalar(maskk[:, :], maskk[:, :], NEG, None, ALU.mult), [m_])

        xv = x.rearrange("(t p) d -> p t d", p=128)
        ov = out.rearrange("(t p) d -> p t d", p=128)
        mx_in = [dma(f"d_x{b}", lambda e, b=b: e.dma_start(X[:, 4 * b:4 * b + 4, :], xv[:, 4 * b:4 * b + 4, :]))
                 for b in range(NB)]

        def load(name, shape, src, dt=F32):
            t = sb(name, shape, dt)
            m = dma("d_w", lambda e: e.dma_start(t[:], src))
            return t, m

        WQ, _ = load("WQ", [128, 2, 768], wqkv0)
        BQK, _ = load("BQK", [128, 4], bqk0)
        BV, _ = load("BV", [128, 256], bv0.rearrange("(o n) -> o n", o=1).to_broadcast([128, 256]))
        CT, _ = load("CT", [128, 2, NE], cent)
        GB, mw = load("GB", [128, NE, 4], gb)
        mw1 = [dma("d_w1", lambda e, i=i: e.dma_start(W1[:, i, :], w1[:, i, :])) for i in range(NE)][-1]

        st = sb("st", [128, 4, 6])
        mv = sb("mv", [128, NT, 2])
        rs = sb("rs", [128, NT])
        mv2 = sb("mv2", [128, NT, 2])
        rs2 = sb("rs2", [128, NT])
        nt_ = sb("nt_", [128, NT])
        nu_ = sb("nu_", [128, NT])
        xnb = sb("xnb", [128, 4, 256])
        cT = sb("cT", [128, 2, 514])
        h0b = cT[:, :, :].rearrange("p a n -> p (a n)")[:, 0:1024].rearrange("p (k n) -> p k n", k=4)
        xTb = sb("xTb", [128, 2, 512])
        AF = sb("AF", [128, NT, NE])
        spl = sb("spl", [128, 2, 3, 512], BF)
        rr = sb("rr", [128, 512])
        mx = sb("mx", [128, 2, 16])
        msp = sb("msp", [16, 3, 128], BF)
        mrr = sb("mrr", [16, 128])
        O = sb("O", [128, 512])
        OW = R3[:, 0:512].rearrange("p (c n) -> p c n", c=2)
        rc = sb("rc", [128, 4, 4])
        rc0 = sb("rc0", [128, 16])
        on = sb("on", [128, 256])
        on0 = on[:, :].rearrange("p (r d) -> p r d", r=16)

        qs = nc.dram_tensor("qs", (48, 128, 3, 512), BF).ap()
        ks = nc.dram_tensor("ks", (32, 128, 3, 512), BF).ap()
        msd = nc.dram_tensor("msd", (96, 16, 3, 128), BF).ap()
        h0d = nc.dram_tensor("h0d", (4096, 256), F32).ap()
        ysd = nc.dram_tensor("ysd", (TM * 128, 256), F32).ap()
        idd = nc.dram_tensor("idd", (TM * 128, 1), I32).ap()

        free = {"M": None, "rr": None, "S1": [None, None], "S2": [None, None], "PV": None, "P": [None, None],
                "O": None, "on": None, "spl": [None, None], "xnb": None, "h0b": None, "xTb": None,
                "mx": [None, None], "msp": None, "QA": [[], [], []], "KA": [[], [], []]}

        def rstd(var, dst, cols, first):
            a = slice(*cols)
            t1 = op(V, lambda e: nc.vector.tensor_scalar(nu_[:, a], var, EPS, None, ALU.add), first)
            t2 = op(A, lambda e: nc.scalar.activation(nt_[:, a], nu_[:, a], ACT.Sqrt), [t1])
            t3 = op(V, lambda e: nc.vector.reciprocal(dst, nt_[:, a]), [t2])
            t4 = op(V, lambda e: nc.vector.tensor_tensor(nt_[:, a], dst, dst, ALU.mult), [t3])
            t5 = op(V, lambda e: nc.vector.tensor_tensor(nt_[:, a], nt_[:, a], nu_[:, a], ALU.mult), [t4])
            t6 = op(V, lambda e: nc.vector.tensor_scalar(nt_[:, a], nt_[:, a], -0.5, 1.5, ALU.mult, ALU.add), [t5])
            return op(V, lambda e: nc.vector.tensor_tensor(dst, dst, nt_[:, a], ALU.mult), [t6])

        sts = sb("sts", [128, NT, 6])

        def stats(t, src, m, after):
            s = op(V, lambda e: nc.vector.bn_stats(sts[:, t, :], src), after)
            return op(V, lambda e: nc.vector.bn_aggr(m[:, t, :], sts[:, t, :]), [s])

        ms = None
        for t in range(NT):
            ms = stats(t, X[:, t, :], mv, [mx_in[t // 4]])
        mr = rstd(mv[:, :, 1], rs[:, :], (0, NT), [ms])
        for t in range(NT):
            k = t % 4
            a = op(V, lambda e, t=t, k=k: nc.vector.tensor_scalar(xnb[:, k, :], X[:, t, :], mv[:, t, 0:1], rs[:, t:t + 1],
                                                                  ALU.subtract, ALU.mult), [mr, free["xnb"]])
            free["xnb"] = stats(t, xnb[:, k, :], mv2, [a, ms])
        mr2 = rstd(mv2[:, :, 1], rs2[:, :], (0, NT), [free["xnb"], mr])

        def ln_batch(b, after):
            m = None
            for k in range(4):
                t = 4 * b + k
                m = op(V, lambda e, t=t, k=k: nc.vector.tensor_scalar(
                    xnb[:, k, :], X[:, t, :], mv[:, t, 0:1], rs[:, t:t + 1], ALU.subtract, ALU.mult),
                    [free["xnb"], *after])
            return m

        def transposes(src, dst, src_ready, dst_free, eng=A):
            m = None
            for c in range(2):
                for k in range(4):
                    t = op(T, lambda e, c=c, k=k: nc.tensor.transpose(
                        M[:, k * 128:(k + 1) * 128], src[:, k, c * 128:(c + 1) * 128], ident[:, :]),
                        [src_ready, free["M"], mident], mark=(k == 3))
                m = op(A, lambda e, c=c: nc.scalar.copy(dst[:, c, :], M[:, :]), [t, dst_free])
                free["M"] = m
                yield m

        def split_out(z, bias, after_mm, name, dram, bw):
            a1 = op(A, lambda e: nc.scalar.activation(spl[:, z, 0, :], M[:, :], ACT.Identity, bias=bias),
                    [after_mm, free["spl"][z], bw])
            a2 = op(V, lambda e: nc.vector.scalar_tensor_tensor(out=rr[:, :], in0=M[:, :], scalar=bias,
                    in1=spl[:, z, 0, :], op0=ALU.add, op1=ALU.subtract), [a1, free["rr"]])
            free["M"] = a2
            a3 = op(V, lambda e: nc.vector.tensor_copy(spl[:, z, 1, :], rr[:, :]), [a2])
            a4 = op(G, lambda e: nc.gpsimd.tensor_tensor(spl[:, z, 2, :], rr[:, :], spl[:, z, 1, :], ALU.subtract), [a3])
            free["rr"] = a4
            d = dma(name, lambda e: e.dma_start(dram, spl[:, z, :, :]), [a4])
            free["spl"][z] = d
            return d

        def fan(dst, dram, parts, name, after):
            m = None
            for j, s in enumerate(parts):
                m = dma(name, lambda e, j=j, s=s: e.dma_start(
                    dst[16 * j:16 * j + 16, :, :], dram[:, s, :].rearrange("(h d) n -> d h n", d=16)), after)
            return m

        QP, KP = (0, 0, 0, 1, 1, 2), (0, 1, 2, 0, 1, 0)

        class Unit:

            def __init__(self, n, kind, b, c):
                self.n, self.kind, self.b, self.c = n, kind, b, c
                self.causal = kind > 0
                self.buf = n % 3
                self.qready = self.kready = self.vready = None
                self.mready = [None, None]
                self.tail = None

        xt_ready = {}
        kdram = {}
        vready = {}
        vfree = {}
        ctxT_ready = {}
        cnt = {"s1": 0, "s2": 0, "p": 0, "mg": 0}

        def vtile(u):
            if u.kind == 0:
                return V0[u.n % 3], ("v0", u.n % 3)
            i = (2 * u.b + u.c) % 8
            return V1S[i], ("v1", i)

        def project(u, xT, wt, bt, bvt, wm, xm):
            c = u.c
            for z, (off, parts) in enumerate(((0, QP), (256, KP))):
                for cc in range(2):
                    t = op(T, lambda e, cc=cc, off=off: nc.tensor.matmul(
                        M[:, :], wt[:, cc, off + c * 128:off + c * 128 + 128], xT[:, cc, :],
                        start=(cc == 0), stop=(cc == 1)), [xm, free["M"], wm], mark=(cc == 1))
                dram = qs[u.n] if z == 0 else ks[(0 if u.kind == 0 else 16) + 2 * u.b + c]
                d = split_out(z, bt[:, 2 * z + c:2 * z + c + 1], t, f"d_sp{z}", dram, wm)
                buf = (QA if z == 0 else KA)[u.buf]
                fr = free["QA" if z == 0 else "KA"][u.buf]
                m = fan(buf, dram, parts, f"d_f{z}{u.buf}", [d, *fr])
                if z == 0:
                    u.qready = m
                else:
                    u.kready = m
                    kdram[(u.kind, u.b, c)] = dram
                yield
            vt, key = vtile(u)
            for k in range(4):
                for cc in range(2):
                    t = op(T, lambda e, cc=cc, k=k: nc.tensor.matmul(
                        M[:, k * 128:(k + 1) * 128], xT[:, cc, k * 128:(k + 1) * 128],
                        wt[:, cc, 512 + c * 128:512 + c * 128 + 128], start=(cc == 0), stop=(cc == 1)),
                        [xm, free["M"], wm], mark=(k == 3 and cc == 1))
            a = op(V, lambda e: nc.vector.tensor_tensor(
                vt[:, :, :, 0:16], M[:, :].rearrange("p (k h d) -> p k h d", k=4, h=8),
                bvt[:, c * 128:c * 128 + 128].rearrange("p (o h d) -> p o h d", o=1, h=8).to_broadcast([128, 4, 8, 16]),
                ALU.add), [t, vfree.get(key), wm])
            free["M"] = a
            u.vready = vready[(u.kind, u.b, c)] = a
            yield

        def pre0(u):
            b = u.b
            if u.c == 0:
                m = ln_batch(b, [mr2])
                yield
                mh = None
                for k in range(4):
                    t = 4 * b + k
                    mh = op(V, lambda e, t=t, k=k: nc.vector.tensor_scalar(
                        h0b[:, k, :], xnb[:, k, :], mv2[:, t, 0:1], rs2[:, t:t + 1], ALU.subtract, ALU.mult),
                        [m, free["h0b"]])
                d = dma("d_h0", lambda e: e.dma_start(
                    h0d.rearrange("(t p) d -> p t d", p=128)[:, 4 * b:4 * b + 4, :], h0b[:, :, :]), [mh])
                free["h0b"] = d
                for xm in transposes(xnb, xTb, m, free["xTb"]):
                    yield
                g = op(G, lambda e: nc.gpsimd.tensor_tensor(
                    X[:, 4 * b:4 * b + 4, :], X[:, 4 * b:4 * b + 4, :], xnb[:, :, :], ALU.add), [m])
                xadd[b] = g
                for k in range(4):
                    for cc in range(2):
                        t = op(T, lambda e, k=k, cc=cc: nc.tensor.matmul(
                            M[:, k * 8:k * 8 + 8], xTb[:, cc, k * 128:(k + 1) * 128], CT[:, cc, :],
                            start=(cc == 0), stop=(cc == 1)), [xm, free["M"], mw], mark=(k == 3 and cc == 1))
                a = op(V, lambda e: nc.vector.tensor_copy(
                    AF[:, 4 * b:4 * b + 4, :], M[:, 0:32].rearrange("p (k e) -> p k e", k=4)), [t])
                free["M"] = a
                free["xnb"] = g
                afready.append(a)
                xt_ready[b] = xm
                yield
            yield from project(u, xTb, WQ, BQK, BV, mw, xt_ready[b])
            free["xTb"] = Q.last[T]

        xadd, afready = {}, []

        def maxp(u):
            qa, ka = QA[u.buf], KA[u.buf]
            for g in range(2):
                gi = cnt["mg"] % 2
                cnt["mg"] += 1
                r = None
                for j in range(4):
                    h = 4 * g + j
                    for qb in range(4):
                        n = 128 * (qb + 1) if u.causal else 512
                        s = cnt["s1"] % 2
                        cnt["s1"] += 1
                        t = op(T, lambda e, s=s, h=h, qb=qb, n=n: nc.tensor.matmul(
                            S1[s][:, 0:n], qa[0:96, h, qb * 128:(qb + 1) * 128], ka[0:96, h, 0:n],
                            start=True, stop=not u.causal), [u.qready, u.kready, free["S1"][s]], mark=not u.causal)
                        if u.causal:
                            t = op(T, lambda e, s=s, n=n: nc.tensor.matmul(
                                S1[s][:, n - 128:n], identb[:, :], maskq[:, :], start=False, stop=True), [mconst])
                        r = op(V, lambda e, s=s, n=n, i=4 * j + qb, gi=gi: nc.vector.tensor_reduce(
                            mx[:, gi, i:i + 1], S1[s][:, 0:n], AX.X, ALU.max), [t, free["mx"][gi]])
                        free["S1"][s] = r
                        yield
                t = op(T, lambda e, gi=gi: nc.tensor.transpose(M[0:16, 0:128], mx[:, gi, :], ident[:, :]),
                       [r, free["M"], mident])
                free["mx"][gi] = t
                a1 = op(V, lambda e, gi=gi: nc.vector.tensor_scalar(msp[:, 0, :], M[0:16, 0:128], -1.0, None, ALU.mult),
                        [t, free["msp"]])
                a2 = op(V, lambda e: nc.vector.scalar_tensor_tensor(
                    out=mrr[:, :], in0=M[0:16, 0:128], scalar=-1.0, in1=msp[:, 0, :],
                    op0=ALU.mult, op1=ALU.subtract), [a1])
                free["M"] = a2
                a3 = op(V, lambda e, gi=gi: nc.vector.tensor_copy(msp[:, 1, :], mrr[:, :]), [a2])
                a4 = op(V, lambda e, gi=gi: nc.vector.tensor_tensor(
                    msp[:, 2, :], mrr[:, :], msp[:, 1, :], ALU.subtract), [a3])
                i = 2 * u.n + g
                d1 = dma("d_m", lambda e, gi=gi, i=i: e.dma_start(msd[i], msp[:, :, :]), [a4])
                free["msp"] = d1
                u.mready[g] = dma(f"d_mq{u.buf}{g}", lambda e, g=g, i=i: e.dma_start(
                    qa[96:99, 4 * g:4 * g + 4, :], msd[i].rearrange("a s p -> s a p")), [d1, *free["QA"][u.buf]])
                yield

        def pv(u, g, kb, slot, e_ready):
            vt, _ = vtile(u)
            n0 = 128 * kb if u.causal else 0
            t = None
            for j in range(4):
                t = op(T, lambda e, j=j: nc.tensor.matmul(
                    PV[32 * j:32 * j + 17, n0:512], vt[:, kb, 4 * g + j, :], P[slot][:, j, 0:512 - n0],
                    start=(kb == 0), stop=(kb == 3), skip_group_check=True),
                    [e_ready, u.vready, free["PV"] if kb == 0 else None], mark=(j == 3))
            free["P"][slot] = t
            return t

        def expp(u, done):
            qa, ka = QA[u.buf], KA[u.buf]
            pend = None

            def close(g, t):
                if u.kind == 0:
                    a = op(V, lambda e: nc.vector.transpose(
                        O[:, :].rearrange("p (r d) -> p r d", r=16), PV[:, :].rearrange("p (n r) -> p r n", r=16)),
                        [t, free["O"]])
                    free["PV"] = a
                    yield
                    od = O[:, :].rearrange("p (r d) -> p r d", r=16)
                    r = op(V, lambda e: nc.vector.reciprocal(rc0[:, :], od[:, :, 16]), [a, free["on"]])
                    a = op(V, lambda e: nc.vector.tensor_tensor(
                        on0, od[:, :, 0:16], rc0[:, :].rearrange("p (r o) -> p r o", o=1).to_broadcast([128, 16, 16]),
                        ALU.mult), [r])
                    free["O"] = a
                    tgt = X[:, 4 * u.b + 2 * u.c + g, :].rearrange("p (r d) -> p r d", r=16)
                    free["on"] = op(G, lambda e: nc.gpsimd.tensor_tensor(tgt, tgt, on0, ALU.add), [a, xadd[u.b]])
                    return
                a = op(A, lambda e: nc.scalar.copy(O[:, :], PV[:, :]), [t, free["O"]])
                free["PV"] = a
                yield
                for k in range(4):
                    t = op(T, lambda e, k=k: nc.tensor.transpose(
                        M[:, k * 128:(k + 1) * 128], O[:, k * 128:(k + 1) * 128], ident[:, :]),
                        [a, free["M"], mident], mark=(k == 3))
                free["O"] = t
                mo = M[:, :].rearrange("p (k j d) -> p k j d", k=4, j=4)
                r = op(V, lambda e: nc.vector.reciprocal(rc[:, :, :], mo[:, :, :, 16]), [t, free["on"]])
                rb = rc[:, :, :].rearrange("p k (j o) -> p k j o", o=1).to_broadcast([128, 4, 4, 16])
                done(u, g, mo[:, :, :, 0:16], rb, r)

            for g in range(2):
                for kb in range(4):
                    n0 = 128 * kb if u.causal else 0
                    n = 512 - n0
                    slot = cnt["p"] % 2
                    cnt["p"] += 1
                    ex = None
                    for pr in range(2):
                        s = cnt["s2"] % 2
                        cnt["s2"] += 1
                        for i in range(2):
                            h = 4 * g + 2 * pr + i
                            t = op(T, lambda e, s=s, i=i, h=h, n=n, n0=n0, kb=kb: nc.tensor.matmul(
                                S2[s][:, i, 0:n], ka[0:99, h, kb * 128:(kb + 1) * 128], qa[0:99, h, n0:512],
                                start=True, stop=not u.causal),
                                [u.qready, u.kready, u.mready[g], free["S2"][s], mones[0]],
                                mark=(i == 1 and not u.causal))
                            if u.causal:
                                t = op(T, lambda e, s=s, i=i: nc.tensor.matmul(
                                    S2[s][:, i, 0:128], identb[:, :], maskk[:, :], start=False, stop=True),
                                    [mconst], mark=(i == 1))
                        ex = op(A, lambda e, s=s, pr=pr, n=n, slot=slot: nc.scalar.activation(
                            P[slot][:, 2 * pr:2 * pr + 2, 0:n], S2[s][:, :, 0:n], ACT.Exp,
                            scale=0.25 if u.causal else 1.0), [t, free["P"][slot]])
                        free["S2"][s] = ex
                        if pr == 1 and pend is not None:
                            t = pv(*pend)
                            if pend[2] == 3:
                                yield
                                yield from close(pend[1], t)
                        yield
                    pend = (u, g, kb, slot, ex)
            t = pv(*pend)
            free["QA"][u.buf] = [t]
            free["KA"][u.buf] = [t]
            vt, key = vtile(u)
            if u.kind != 1:
                vfree[key] = t
            yield
            yield from close(1, t)

        def run(units, pre, done, fin):
            def gen(f, i):
                return f(units[i]) if 0 <= i < len(units) else iter(())
            for i in range(-2, len(units) + 1):
                lanes = [(expp(units[i], done) if 0 <= i < len(units) else iter(()), 4),
                         (gen(maxp, i + 1), 2), (gen(pre, i + 2), 4)]
                if fin is not None and i >= 1 and i - 1 < len(units):
                    lanes.append((fin(units[i - 1]), 4))
                live = [True] * len(lanes)
                k = 0
                while any(live):
                    for z, (g, every) in enumerate(lanes):
                        if live[z] and k % every == 0:
                            try:
                                next(g)
                            except StopIteration:
                                live[z] = False
                    k += 1

        mones = [None]

        def init_attention(after, vt):
            for i in range(3):
                op(V, lambda e, i=i: nc.vector.memset(KA[i][96:99, :, :], 1.0), after)
            for t in vt:
                op(V, lambda e, t=t: nc.vector.memset(t[:, :, :, 16:17], 1.0), after)
            w = op(V, lambda e: nc.vector.memset(PV[:, :], 0.0), after)
            m = op(G, lambda e: nc.gpsimd.memset(rr[:, 0:1], 0.0), [Q.last[G], w])
            mones[0] = m
            free["rr"] = m

        init_attention([], V0)

        units = [Unit(n, 0, n // 2, n % 2) for n in range(16)]
        run(units, pre0, None, None)

        def barrier():
            return [Q.last[e] for e in (T, V, A, G)] + [(s, Q.count[s]) for s in Q.sems if s.startswith("d_")]

        bar = barrier()
        mw2 = [dma("d_w2", lambda e, i=i: e.dma_start(W2[:, i, :], w2[:, i, :]), bar) for i in range(NE)][-1]
        B2 = R3[0:3, 0:1024].bitcast(BF).rearrange("p (e n) -> p e n", e=NE)
        cTv = cT[:, :, :].rearrange("p a n -> p (a n)")
        WQv = WQ[:, :, :].rearrange("p a n -> p (a n)")

        def wq8(i):
            return WQv[:, i * 256:(i + 1) * 256].rearrange("p (t e) -> p t e", e=NE)

        B1T = sb("B1T", [128, NE, 8])
        bd2 = nc.dram_tensor("bd2", (3, 2048), BF).ap()
        bt = sb("bt", [128, 16])
        br = sb("br", [128, 16])
        bs = sb("bs", [128, 3, 16], BF)
        ones3 = sb("ones3", [3, 128], BF)
        on3 = op(V, lambda e: nc.vector.memset(ones3[:, :], 1.0))
        mb1 = dma("d_b1", lambda e: e.dma_start(B1T[:, :, :], b1))
        m = dma("d_b", lambda e: e.dma_start(bt[:, :], b2.rearrange("(p n) -> p n", p=128)))
        m = op(V, lambda e: nc.vector.tensor_copy(bs[:, 0, :], bt[:, :]), [m])
        m = op(V, lambda e: nc.vector.tensor_tensor(br[:, :], bt[:, :], bs[:, 0, :], ALU.subtract), [m])
        m = op(V, lambda e: nc.vector.tensor_copy(bs[:, 1, :], br[:, :]), [m])
        m = op(V, lambda e: nc.vector.tensor_tensor(bs[:, 2, :], br[:, :], bs[:, 1, :], ALU.subtract), [m])
        m = dma("d_b", lambda e: e.dma_start(bd2.rearrange("s (p n) -> p s n", p=128), bs[:, :, :]), [m])
        mbias = dma("d_b2", lambda e: e.dma_start(B2.rearrange("s e n -> s (e n)"), bd2), [m, *bar])

        tri = sb("tri", [128, 128])
        onesf = sb("onesf", [128, 128])
        io8 = sb("io8", [128, NE])
        ioT = sb("ioT", [128, TM])
        tok = sb("tok", [128, NT], I32)
        z39 = sb("z39", [128, TM], I32)
        g1 = op(G, lambda e: nc.gpsimd.memset(tri[:, :], 0.0))
        op(G, lambda e: nc.gpsimd.memset(onesf[:, :], 1.0))
        op(G, lambda e: nc.gpsimd.affine_select(out=tri[:, :], in_=tri[:, :], compare_op=ALU.is_ge, fill=1.0,
                                                base=0, pattern=[[-1, 128]], channel_multiplier=1), [g1])
        op(G, lambda e: nc.gpsimd.iota(io8[:, :], pattern=[[1, NE]], base=0, channel_multiplier=0,
                                       allow_small_or_imprecise_dtypes=True))
        op(G, lambda e: nc.gpsimd.iota(ioT[:, :], pattern=[[1, TM]], base=0, channel_multiplier=0,
                                       allow_small_or_imprecise_dtypes=True))
        op(G, lambda e: nc.gpsimd.iota(tok[:, :], pattern=[[128, NT]], base=0, channel_multiplier=1))
        mg = op(G, lambda e: nc.gpsimd.memset(z39[:, :], 0))
        mzid = dma("d_z", lambda e: e.dma_start(idd.rearrange("(p t) o -> p (t o)", p=128), z39[:, :]), [mg])

        def bc(ap, shape):
            return ap.to_broadcast(shape)

        amax = sb("amax", [128, NT])
        alpha = sb("alpha", [128, NT])
        eq = wq8(0)
        oh = wq8(1)
        emin = sb("emin", [128, NT])
        wi = wq8(2)
        tt = [wq8(3), wq8(4)]
        tot = wq8(5)
        te_ = [sb("tea", [128, NE]), sb("teb", [128, NE])]
        tl = sb("tl", [128, NE])
        tli = sb("tli", [128, NE], I32)
        slotf = sb("slotf", [128, NT])
        sloti = sb("sloti", [128, NT], I32)
        lo7 = sb("lo7", [128, NT], I32)
        hi7 = sb("hi7", [128, NT], I32)
        lof = sb("lof", [128, NT])
        hif = sb("hif", [128, NT])
        sidx = sb("sidx", [128, NT], I32)
        tcm = R3[:, 1024:1024 + TM * NE].rearrange("p (t e) -> p t e", e=NE)
        texf = sb("texf", [128, TM])
        texp = sb("texp", [128, TM], I32)
        gidx = sb("gidx", [128, TM], I32)

        def v(f, *after):
            return op(V, f, list(after))

        s8 = [128, NT, NE]
        m = v(lambda e: nc.vector.tensor_reduce(amax[:, :], AF[:, :, :], AX.X, ALU.max), afready[-1])
        ma = op(A, lambda e: nc.scalar.activation(alpha[:, :], amax[:, :], ACT.Exp, scale=-1.0), [m])
        ma = v(lambda e: nc.vector.tensor_scalar(alpha[:, :], alpha[:, :], 1.0, None, ALU.add), ma)
        malpha = v(lambda e: nc.vector.reciprocal(alpha[:, :], alpha[:, :]), ma)
        m = v(lambda e: nc.vector.tensor_tensor(eq[:, :, :], AF[:, :, :],
              bc(amax[:, :].rearrange("p (t o) -> p t o", o=1), s8), ALU.is_ge), m, *bar)
        m = v(lambda e: nc.vector.scalar_tensor_tensor(out=eq[:, :, :], in0=eq[:, :, :], scalar=-8.0,
              in1=bc(io8[:, :].rearrange("p (o e) -> p o e", o=1), s8), op0=ALU.mult, op1=ALU.add), m, mg)
        m = v(lambda e: nc.vector.tensor_reduce(emin[:, :], eq[:, :, :], AX.X, ALU.min), m)
        m = v(lambda e: nc.vector.tensor_tensor(oh[:, :, :], eq[:, :, :],
              bc(emin[:, :].rearrange("p (t o) -> p t o", o=1), s8), ALU.is_equal), m)
        ohf = oh[:, :, :].rearrange("p t e -> p (t e)")
        op(T, lambda e: nc.tensor.matmul(M[:, 0:256], tri[:, :], ohf, start=True, stop=True), [m, mg, *bar], mark=False)
        t = op(T, lambda e: nc.tensor.matmul(M[:, 256:512], onesf[:, :], ohf, start=True, stop=True))
        m1 = v(lambda e: nc.vector.tensor_copy(wi[:, :, :].rearrange("p t e -> p (t e)"), M[:, 0:256]), t)
        m = v(lambda e: nc.vector.tensor_copy(tot[:, :, :].rearrange("p t e -> p (t e)"), M[:, 256:512]), t)
        free["M"] = m
        src = tot
        for i, s in enumerate((1, 2, 4, 8, 16)):
            dst = tt[i % 2]
            m2 = v(lambda e, src=src, dst=dst, s=s: nc.vector.tensor_copy(dst[:, 0:s, :], src[:, 0:s, :]), m)
            m = v(lambda e, src=src, dst=dst, s=s: nc.vector.tensor_tensor(
                dst[:, s:NT, :], src[:, s:NT, :], src[:, 0:NT - s, :], ALU.add), m2)
            src = dst
        inc = src
        m = v(lambda e: nc.vector.tensor_scalar(tl[:, :], inc[:, NT - 1, :], 127.0, None, ALU.add), m)
        m = v(lambda e: nc.vector.tensor_copy(tli[:, :], tl[:, :]), m)
        m = v(lambda e: nc.vector.tensor_scalar(tli[:, :], tli[:, :], 7, None, ALU.arith_shift_right), m)
        m = v(lambda e: nc.vector.tensor_copy(tl[:, :], tli[:, :]), m)
        src = tl
        for i, s in enumerate((1, 2, 4)):
            dst = te_[i % 2]
            m2 = v(lambda e, src=src, dst=dst, s=s: nc.vector.tensor_copy(dst[:, 0:s], src[:, 0:s]), m)
            m = v(lambda e, src=src, dst=dst, s=s: nc.vector.tensor_tensor(
                dst[:, s:NE], src[:, s:NE], src[:, 0:NE - s], ALU.add), m2)
            src = dst
        ends, base = te_[0], te_[1]
        m2 = v(lambda e: nc.vector.tensor_tensor(base[:, :], ends[:, :], tl[:, :], ALU.subtract), m)
        m2 = v(lambda e: nc.vector.tensor_scalar(base[:, :], base[:, :], 128.0, None, ALU.mult), m2)
        m3 = v(lambda e: nc.vector.tensor_tensor(wi[:, :, :], wi[:, :, :], inc[:, :, :], ALU.add), m2, m1)
        m3 = v(lambda e: nc.vector.tensor_tensor(wi[:, :, :], wi[:, :, :], tot[:, :, :], ALU.subtract), m3)
        m3 = v(lambda e: nc.vector.tensor_tensor(wi[:, :, :], wi[:, :, :],
               bc(base[:, :].rearrange("p (o e) -> p o e", o=1), s8), ALU.add), m3)
        m3 = v(lambda e: nc.vector.tensor_tensor(wi[:, :, :], wi[:, :, :], oh[:, :, :], ALU.mult), m3)
        m3 = v(lambda e: nc.vector.tensor_reduce(slotf[:, :], wi[:, :, :], AX.X, ALU.add), m3)
        m3 = v(lambda e: nc.vector.tensor_copy(sloti[:, :], slotf[:, :]), m3)
        mslot = m3
        m3 = v(lambda e: nc.vector.tensor_scalar(lo7[:, :], sloti[:, :], 127, None, ALU.bitwise_and), m3)
        m3 = v(lambda e: nc.vector.tensor_scalar(hi7[:, :], sloti[:, :], 7, None, ALU.arith_shift_right), m3)
        m3 = v(lambda e: nc.vector.tensor_copy(lof[:, :], lo7[:, :]), m3)
        m3 = v(lambda e: nc.vector.tensor_copy(hif[:, :], hi7[:, :]), m3)
        m3 = v(lambda e: nc.vector.scalar_tensor_tensor(out=lof[:, :], in0=lof[:, :], scalar=float(TM), in1=hif[:, :],
               op0=ALU.mult, op1=ALU.add), m3)
        midx = v(lambda e: nc.vector.tensor_copy(sidx[:, :], lof[:, :]), m3)
        s39 = [128, TM, NE]
        m = v(lambda e: nc.vector.tensor_tensor(tcm[:, :, :], bc(ends[:, :].rearrange("p (o e) -> p o e", o=1), s39),
              bc(ioT[:, :].rearrange("p (t o) -> p t o", o=1), s39), ALU.is_le), m)
        m = v(lambda e: nc.vector.tensor_reduce(texf[:, :], tcm[:, :, :], AX.X, ALU.add), m)
        m = v(lambda e: nc.vector.tensor_scalar(texf[:, :], texf[:, :], float(NE - 1), None, ALU.min), m)
        mtex = v(lambda e: nc.vector.tensor_copy(texp[:, :], texf[:, :]), m)

        m = None
        for t in range(NT):
            m = dma("d_sc", lambda e, t=t: nc.gpsimd.indirect_dma_start(
                idd, bass.IndirectOffsetOnAxis(ap=sidx[:, t:t + 1].bitcast(U32), axis=0), tok[:, t:t + 1], None),
                [midx, mzid, mg], eng=G)
        mgi = dma("d_gi", lambda e: e.dma_start(gidx[:, :], idd.rearrange("(p t) o -> p (t o)", p=128)), [m])

        hs = [O[:, 0:256], O[:, 256:512], on[:, :]]
        hT = [cTv[:, i * 256:(i + 1) * 256].rearrange("p (c n) -> p c n", c=2) for i in range(2)]
        AA = [xnb[:, :, :].rearrange("p a n -> p (a n)"), xTb[:, :, :].rearrange("p a n -> p (a n)")]
        AT = spl[:, :, :, :].rearrange("p a b n -> p (a b n)").bitcast(F32)[:, 0:1024].rearrange("p (k n) -> p k n", k=8)
        Y = [cTv[:, 512 + i * 256:768 + i * 256] for i in range(2)]
        ef = {"hs": [None] * 3, "hT": [None] * 2, "AA": [None] * 2, "AT": [None, None], "Y": [None] * 2,
              "S2": [bar[0], bar[0]], "S1": [None, None], "PV": None}
        gath = {}
        regs = {}

        def gather(t):
            gath[t] = dma(f"d_hs{t % 3}", lambda e: nc.gpsimd.indirect_dma_start(
                hs[t % 3], None, h0d, bass.IndirectOffsetOnAxis(ap=gidx[:, t:t + 1].bitcast(U32), axis=0)),
                [mgi, ef["hs"][t % 3], *bar], eng=G)

        def expert(eng, t):
            def f(e):
                regs[(eng, t)] = e.value_load(texp[0:1, t:t + 1], min_val=0, max_val=NE - 1)
            return f

        aready = {}

        def first(t):
            i = t % 2
            Q._wait(T, [mtex])
            Q.items[T].append(("op", expert(T, t), None, 0))
            Q._wait(V, [mtex])
            Q.items[V].append(("op", expert(V, t), None, 0))
            for c in range(2):
                x_ = op(T, lambda e, c=c: nc.tensor.transpose(M[:, c * 128:(c + 1) * 128],
                        hs[t % 3][:, c * 128:(c + 1) * 128], ident[:, :]), [gath[t], free["M"]], mark=(c == 1))
            ef["hs"][t % 3] = x_
            for c in range(2):
                y_ = op(V, lambda e, c=c: nc.vector.tensor_scalar(
                    hT[i][:, c, :], M[:, c * 128:(c + 1) * 128],
                    GB[:, bass.ds(regs[(V, t)], 1), c:c + 1], GB[:, bass.ds(regs[(V, t)], 1), 2 + c:3 + c],
                    ALU.mult, ALU.add), [x_, ef["hT"][i]])
            free["M"] = y_
            for f in range(2):
                for c in range(2):
                    z_ = op(T, lambda e, f=f, c=c: nc.tensor.matmul(
                        S2[i][:, f, :], hT[i][:, c, :],
                        W1[:, bass.ds(regs[(T, t)], 1), c * 1024 + f * 512:c * 1024 + f * 512 + 512],
                        start=(c == 0), stop=(c == 1)), [y_, ef["S2"][i], mw1], mark=(c == 1))
                a_ = op(A, lambda e, f=f: nc.scalar.copy(AA[i][:, f * 512:(f + 1) * 512], S2[i][:, f, :]),
                        [z_, ef["AA"][i]])
            ef["hT"][i] = z_
            ef["S2"][i] = a_
            aready[t] = a_

        def second(t):
            i = t % 2
            cp = [None, None]
            for f in range(2):
                for k in range(4):
                    t_ = op(T, lambda e, f=f, k=k: nc.tensor.transpose(
                        S1[f][:, k * 128:(k + 1) * 128], AA[i][:, (4 * f + k) * 128:(4 * f + k + 1) * 128], ident[:, :]),
                        [aready[t], ef["S1"][f]], mark=(k == 3))
                for k in range(4):
                    cp[f] = op(V, lambda e, f=f, k=k: nc.vector.tensor_scalar(
                        AT[:, 4 * f + k, :], S1[f][:, k * 128:(k + 1) * 128],
                        B1T[:, bass.ds(regs[(V, t)], 1), 4 * f + k:4 * f + k + 1], 0.0, ALU.add, ALU.max),
                        [t_, ef["AT"][f], mb1])
                ef["S1"][f] = cp[f]
            ef["AA"][i] = t_
            for k in range(8):
                t_ = op(T, lambda e, k=k: nc.tensor.matmul(
                    PV[:, 0:256], AT[:, k, :], W2[:, bass.ds(regs[(T, t)], 1), k * 256:k * 256 + 256],
                    start=(k == 0), stop=False), [cp[k // 4], ef["PV"], mw2], mark=(k in (3, 7)))
                if k in (3, 7):
                    ef["AT"][k // 4] = t_
            t_ = op(T, lambda e: nc.tensor.matmul(
                PV[:, 0:256], ones3[:, :], B2[:, bass.ds(regs[(T, t)], 1), :], start=False, stop=True), [mbias, on3])
            a_ = op(A, lambda e: nc.scalar.copy(Y[i], PV[:, 0:256]), [t_, ef["Y"][i]])
            ef["PV"] = a_
            ef["Y"][i] = dma(f"d_y{i}", lambda e: e.dma_start(ysd[t * 128:(t + 1) * 128, :], Y[i]), [a_])

        gather(0)
        gather(1)
        first(0)
        for t in range(TM):
            if t + 2 < TM:
                gather(t + 2)
            if t + 1 < TM:
                first(t + 1)
            second(t)

        bar = barrier()
        gy = [R2[:, 12288 + i * 256:12544 + i * 256] for i in range(4)]
        gyf = [None] * 4
        WQ1 = WQ
        m = dma("d_l1", lambda e: e.dma_start(WQ1[:], wqkv1), bar)
        dma("d_l1", lambda e: e.dma_start(BQK[:], bqk1))
        dma("d_l1", lambda e: e.dma_start(BV[:], bv1.rearrange("(o n) -> o n", o=1).to_broadcast([128, 256])))

        def loadl(view, src):
            return dma("d_l1", lambda e: e.dma_start(view, src))

        CW = R1[:, 12544:14080].rearrange("p (a n) -> p a n", a=6)
        OB = R3[:, 512:768]
        FB = R3[:, 768:1024]
        CB = sb("CB", [128, 2])
        U1 = R3[:, 1024:1280].rearrange("p (c n) -> p c n", c=2)
        V1f = R2[:, 0:1024]
        V1r = R2[:, 1024:2048]
        r2c = R2[:, :].bitcast(BF)
        V1a = r2c[:, 4096:5120]
        V1b = r2c[:, 5120:6144]
        V1c = r2c[:, 6144:7168]
        VA = r2c[:, 7168:8192]
        VB = r2c[:, 8192:9216]
        U2 = R2[:, 5120:5632].rearrange("p (k n) -> p k n", k=8)
        V2 = R2[:, 5632:5888]
        PT = r2c[:, 12288:12288 + 1536].rearrange("p (a n) -> p a n", a=3)
        Pr = R2[:, 7168:7680]
        HT = [R2[:, 7680 + i * 512:8192 + i * 512] for i in range(4)]
        QS = [R2[:, 9728 + i * 512:10240 + i * 512] for i in range(2)]
        FBI = sb("FBI", [128, 8])
        loadl(CW[:, :, :], convw)
        loadl(OW[:], outw)
        loadl(OB[:], outb.rearrange("(o n) -> o n", o=1).to_broadcast([128, 256]))
        loadl(FB[:], fb2.rearrange("(o n) -> o n", o=1).to_broadcast([128, 256]))
        loadl(CB[:], convb)
        loadl(U1[:], u1)
        loadl(V1f[0:64], v1)
        loadl(V1f[64:128], v1)
        loadl(U2, u2)
        loadl(V2[0:64], v2)
        loadl(V2[64:128], v2)
        ml1 = loadl(FBI[:], fb1)

        ms = None
        for t in range(NT):
            k = t % 4
            d = dma(f"d_gy{k}", lambda e, t=t, k=k: nc.gpsimd.indirect_dma_start(
                gy[k], None, ysd, bass.IndirectOffsetOnAxis(ap=sloti[:, t:t + 1].bitcast(U32), axis=0)),
                [gyf[k], mslot, *bar], eng=G)
            a = v(lambda e, t=t, k=k: nc.vector.scalar_tensor_tensor(
                out=X[:, t, :], in0=gy[k], scalar=alpha[:, t:t + 1], in1=X[:, t, :], op0=ALU.mult, op1=ALU.add),
                d, malpha, *bar)
            gyf[k] = a
            ms = stats(t, X[:, t, :], mv, [a])
        mr = rstd(mv[:, :, 1], rs[:, :], (0, NT), [ms])
        mbb = op(G, lambda e: nc.gpsimd.tensor_tensor(OB[:, :], OB[:, :], FB[:, :], ALU.add), [ml1])

        m = v(lambda e: nc.vector.tensor_copy(V1a, V1f), ml1)
        m = v(lambda e: nc.vector.tensor_tensor(V1r, V1f, V1a, ALU.subtract), m)
        m = v(lambda e: nc.vector.tensor_copy(V1b, V1r), m)
        m = v(lambda e: nc.vector.tensor_tensor(V1c, V1r, V1b, ALU.subtract), m)
        v(lambda e: nc.vector.tensor_copy(VA[0:64], V1a[0:64]), m)
        v(lambda e: nc.vector.tensor_copy(VA[64:128], V1b[64:128]), m)
        v(lambda e: nc.vector.tensor_copy(VB[0:64], V1a[0:64]), m)
        mva = v(lambda e: nc.vector.tensor_copy(VB[64:128], V1c[64:128]), m)

        ff = {"PT": None, "HT": [None] * 4, "QS": [None] * 2, "hb": [bar[0]] * 4, "qb": [None, None], "yb": None}
        hbank = [S2[0][:, 0, :], S2[0][:, 1, :], S2[1][:, 0, :], S2[1][:, 1, :]]
        hc = 0
        for b in range(NB):
            m = ln_batch(b, [mr, *bar])
            xm = None
            for xm in transposes(xnb, XT[:, :, 512 * b:512 * b + 512], m, None):
                pass
            free["xnb"] = Q.last[T]
            xt_ready[("l1", b)] = xm
            for cc in range(2):
                t = op(T, lambda e, cc=cc, b=b: nc.tensor.matmul(
                    M[:, :], U1[:, cc, :], XT[:, cc, 512 * b:512 * b + 512], start=(cc == 0), stop=(cc == 1)),
                    [xm, free["M"], ml1], mark=(cc == 1))
            a1 = op(A, lambda e: nc.scalar.copy(PT[:, 0, :], M[:, :]), [t, ff["PT"]])
            a2 = v(lambda e: nc.vector.tensor_tensor(Pr, M[:, :], PT[:, 0, :], ALU.subtract), a1)
            a3 = v(lambda e: nc.vector.tensor_copy(PT[:, 1, :], Pr), a2)
            a4 = v(lambda e: nc.vector.tensor_tensor(PT[0:64, 2, :], Pr[0:64], PT[0:64, 1, :], ALU.subtract), a3)
            a5 = op(A, lambda e: nc.scalar.copy(PT[64:128, 2, :], PT[64:128, 0, :]), [a1, a2])
            free["M"] = a2
            qb = (PV, S1[0])[b % 2]
            qm = None
            pend = []

            def u2mm(j, qb=qb, b=b):
                q = None
                for f, hm in j:
                    h = f % 2
                    q = op(T, lambda e, f=f, h=h, hm=hm: nc.tensor.matmul(
                        qb[64 * h:64 * h + 64, :], U2[:, f, :], HT[hm[1]], start=(f < 2), stop=(f >= 6),
                        skip_group_check=True), [hm[0], ff["qb"][b % 2]], mark=True)
                    ff["HT"][hm[1]] = q
                return q

            for f in range(8):
                hb = hbank[hc % 4]
                hi = hc % 4
                for z, (vv, pp) in enumerate(((VA, 0), (VA, 1), (VB, 2))):
                    t = op(T, lambda e, z=z, vv=vv, pp=pp, f=f, hb=hb: nc.tensor.matmul(
                        hb, vv[:, f * 128:(f + 1) * 128], PT[:, pp, :], start=(z == 0), stop=(z == 2)),
                        [a4, a5, mva, ff["hb"][hi]], mark=(z == 2))
                g_ = op(A, lambda e, f=f, hb=hb, hi=hi: nc.scalar.activation(
                    HT[hi], hb, ACT.Gelu_apprx_tanh, bias=FBI[:, f:f + 1]), [t, ff["HT"][hi]])
                ff["hb"][hi] = g_
                pend.append((f, (g_, hi)))
                hc += 1
                if f % 2 == 1 and f >= 3:
                    qm = u2mm(pend[:2])
                    pend = pend[2:]
            ff["PT"] = t
            qm = u2mm(pend)
            a = op(A, lambda e, b=b, qb=qb: nc.scalar.copy(QS[b % 2], qb[:, :]), [qm, ff["QS"][b % 2]])
            ff["qb"][b % 2] = a
            for h in range(2):
                for k in range(2):
                    t = op(T, lambda e, h=h, k=k, b=b: nc.tensor.matmul(
                        S1[1][:, k * 256:(k + 1) * 256], QS[b % 2][:, (2 * h + k) * 128:(2 * h + k + 1) * 128], V2,
                        start=True, stop=True), [a, ff["yb"]], mark=(k == 1))
                tg = X[:, 4 * b + 2 * h:4 * b + 2 * h + 2, :]
                y_ = v(lambda e, tg=tg: nc.vector.tensor_tensor(
                    tg, tg, S1[1][:, :].rearrange("p (k n) -> p k n", k=2), ALU.add), t, m)
                ff["yb"] = y_
            ff["QS"][b % 2] = t
            tg = X[:, 4 * b:4 * b + 4, :]
            xadd[b] = op(G, lambda e, tg=tg: nc.gpsimd.tensor_tensor(
                tg, tg, OB[:, :].rearrange("p (o n) -> p o n", o=1).to_broadcast([128, 4, 256]), ALU.add), [y_, mbb])

        bar = barrier()
        CTX = [R1[:, 14080:15104].rearrange("p (k n) -> p k n", k=4),
               R1[:, 15104:16128].rearrange("p (k n) -> p k n", k=4), xnb]
        c2T = xTb
        init_attention(bar, V1S)
        for k in (0, 513):
            mpad = op(V, lambda e, k=k: nc.vector.memset(cT[:, :, k:k + 1], 0.0))
        for key in ("M", "PV", "O", "on", "xTb", "xnb"):
            free[key] = mones[0]
        free["S1"] = [mones[0]] * 2
        free["S2"] = [mones[0]] * 2
        free["P"] = [mones[0]] * 2
        free["QA"] = [[mones[0]] for _ in range(3)]
        free["KA"] = [[mones[0]] for _ in range(3)]
        vfree.clear()

        ctxm = {}
        ctxf = [None] * 3

        def cslot(kind, b):
            return b % 2 if kind == 1 else 2

        cTf = [None]

        def pre1(u):
            b, c = u.b, u.c
            if u.kind == 1:
                yield from project(u, XT[:, :, 512 * b:512 * b + 512], WQ1, BQK, BV, ml1, xt_ready[("l1", b)])
                return
            if c == 0:
                cx = CTX[cslot(1, b)]
                for m in transposes(cx, cT[:, :, 1:513], ctxm[(1, b)], cTf[0]):
                    yield
                ctxf[cslot(1, b)] = Q.last[T]
                ctxT_ready[b] = m
            for i in range(6):
                k, cc = i // 2, i % 2
                t = op(T, lambda e, i=i, k=k, cc=cc: nc.tensor.matmul(
                    M[:, :], CW[:, i, c * 128:c * 128 + 128], cT[:, cc, k:k + 512], start=(i == 0), stop=(i == 5)),
                    [ctxT_ready[b], mpad, free["M"]], mark=(i == 5))
            cTf[0] = t
            d = split_out(0, CB[:, c:c + 1], t, "d_sp0", qs[u.n], ml1)
            u.qready = fan(QA[u.buf], qs[u.n], QP, f"d_f0{u.buf}", [d, *free["QA"][u.buf]])
            yield
            u.kready = fan(KA[u.buf], kdram[(1, b, c)], KP, f"d_f1{u.buf}", [*free["KA"][u.buf]])
            u.vready = vready[(1, b, c)]
            yield

        def done1(u, g, vals, rb, r):
            key = (u.kind, u.b)
            s = cslot(*key)
            lo = u.c * 128 + g * 64
            tg = CTX[s][:, :, lo:lo + 64].rearrange("p k (j d) -> p k j d", j=4)
            a = op(V, lambda e: nc.vector.tensor_tensor(tg, vals, rb, ALU.mult), [r, ctxf[s]])
            free["M"] = a
            free["on"] = a
            ctxm[key] = a

        def fin1(u):
            if u.kind != 2 or u.c != 1:
                return
            b = u.b
            cx = CTX[cslot(2, b)]
            for m in transposes(cx, c2T, ctxm[(2, b)], free["xTb"]):
                yield
            ctxf[cslot(2, b)] = Q.last[T]
            for h in range(2):
                for k in range(2):
                    for cc in range(2):
                        t = op(T, lambda e, h=h, k=k, cc=cc: nc.tensor.matmul(
                            M[:, k * 256:(k + 1) * 256], c2T[:, cc, (2 * h + k) * 128:(2 * h + k + 1) * 128],
                            OW[:, cc, :], start=(cc == 0), stop=(cc == 1)), [m, free["M"], ml1], mark=(k == 1 and cc == 1))
                tg = X[:, 4 * b + 2 * h:4 * b + 2 * h + 2, :]
                y_ = v(lambda e, tg=tg: nc.vector.tensor_tensor(
                    tg, tg, M[:, :].rearrange("p (k n) -> p k n", k=2), ALU.add), t, xadd[b])
                free["M"] = y_
                yield
            free["xTb"] = t
            dma("d_out", lambda e: e.dma_start(ov[:, 4 * b:4 * b + 4, :], X[:, 4 * b:4 * b + 4, :]), [y_])

        order, a1, a2 = [], 0, 0
        while a2 < NB:
            if a1 < NB and a1 < a2 + 2:
                order += [(1, a1, 0), (1, a1, 1)]
                a1 += 1
            else:
                order += [(2, a2, 0), (2, a2, 1)]
                a2 += 1
        units = [Unit(n, kind, b, c) for n, (kind, b, c) in enumerate(order, 16)]
        run(units, pre1, done1, fin1)

        ends_ = [(s, Q.count[s]) for s in Q.sems if s.startswith("d_")]
        Q._wait("sync", ends_)
        block = ctx.enter_context(nc.Block())
        Q.emit(block)


_ARGS = ["x", "wqkv0", "bqk0", "bv0", "cent", "gb", "w1", "b1", "w2", "b2", "wqkv1", "bqk1", "bv1", "convw", "convb",
         "outw", "outb", "u1", "v1", "fb1", "u2", "v2", "fb2"]


def kernel(**inputs):
    import numpy as np
    import concourse.bacc as bacc
    from concourse.bass_utils import run_bass_kernel_spmd

    i = {k: np.asarray(v) for k, v in inputs.items()}

    def rows(w):
        return w.reshape(2, 128, -1).transpose(1, 0, 2)

    g, b = i["L0_ffn_ln_g"].reshape(8, 2, 128), i["L0_ffn_ln_b"].reshape(8, 2, 128)
    a = {
        "x": i["L0_attn_x"].reshape(4096, 256),
        "wqkv0": rows(i["L0_attn_W_qkv"]),
        "bqk0": i["L0_attn_b_qkv"][0:512].reshape(4, 128).T,
        "bv0": i["L0_attn_b_qkv"][512:768],
        "cent": rows(i["L0_ffn_centroids"].T),
        "gb": np.concatenate([g, b], axis=1).transpose(2, 0, 1),
        "w1": i["L0_ffn_w1"].transpose(0, 2, 1).reshape(8, 2, 128, 1024).transpose(2, 0, 1, 3).reshape(128, 8, 2048),
        "b1": i["L0_ffn_b1"].reshape(8, 8, 128).transpose(2, 0, 1),
        "w2": i["L0_ffn_w2"].transpose(0, 2, 1).reshape(8, 8, 128, 256).transpose(2, 0, 1, 3).reshape(128, 8, 2048),
        "b2": i["L0_ffn_b2"].reshape(-1),
        "wqkv1": rows(i["L1_attn_Wqkv_w"].T),
        "bqk1": i["L1_attn_Wqkv_b"][0:512].reshape(4, 128).T,
        "bv1": i["L1_attn_Wqkv_b"][512:768],
        "convw": i["L1_attn_conv_w"].transpose(2, 1, 0).reshape(3, 2, 128, 256).transpose(2, 0, 1, 3).reshape(128, 6, 256),
        "convb": i["L1_attn_conv_b"].reshape(2, 128).T,
        "outw": rows(i["L1_attn_out_w"].T),
        "outb": i["L1_attn_out_b"],
        "u1": np.concatenate([rows(i["L1_ffn_U1"])] * 2, axis=2),
        "v1": i["L1_ffn_V1"],
        "fb1": i["L1_ffn_b1"].reshape(8, 128).T,
        "u2": i["L1_ffn_U2"].reshape(8, 128, 64).transpose(1, 0, 2),
        "v2": i["L1_ffn_V2"],
        "fb2": i["L1_ffn_b2"],
    }
    nc = bacc.Bacc("TRN2", target_bir_lowering=False, num_devices=1)
    arrays, args = {}, []
    for name in _ARGS:
        arrays[f"in_{name}"] = np.ascontiguousarray(a[name])
        args.append(nc.dram_tensor(f"in_{name}", a[name].shape, F32, kind="ExternalInput").ap())
    args.append(nc.dram_tensor("out", (4096, 256), F32, kind="ExternalOutput").ap())
    build(nc, *args)
    r = run_bass_kernel_spmd(nc, [arrays], core_ids=[0])
    return r.results[0]["out"].reshape(8, 512, 256)
```

```python
import concourse.bass as bass
from concourse import mybir
from contextlib import ExitStack

F32 = mybir.dt.float32
BF = mybir.dt.bfloat16
I32 = mybir.dt.int32
U32 = mybir.dt.uint32
ALU = mybir.AluOpType
ACT = mybir.ActivationFunctionType
AX = mybir.AxisListType

NB = 8
NT = 32
NE = 8
TM = 39
EPS = 1e-5
NEG = -(2.0 ** 127)
ENGINES = ("tensor", "vector", "scalar", "gpsimd", "sync")


class Queues:

    def __init__(self, nc, ctx):
        self.nc, self.ctx = nc, ctx
        self.items = {e: [] for e in ENGINES}
        self.sems, self.count = {}, {}
        self.seen = {e: {} for e in ENGINES}
        self.last = {}

    def sem(self, name):
        if name not in self.sems:
            self.sems[name] = self.ctx.enter_context(self.nc.semaphore(name))
            self.count[name] = 0
        return name

    def _wait(self, eng, after):
        need = {}
        for m in after:
            if m is not None and m[1] > self.seen[eng].get(m[0], 0):
                need[m[0]] = max(need.get(m[0], 0), m[1])
        for s, v in need.items():
            self.seen[eng][s] = v
            self.items[eng].append(("wait", s, v))

    def op(self, eng, fn, after=(), mark=True):
        self._wait(eng, after)
        if mark:
            s = self.sem("s_" + eng)
            self.count[s] += 1
            self.items[eng].append(("op", fn, s, 1))
            self.last[eng] = (s, self.count[s])
            return self.last[eng]
        self.items[eng].append(("op", fn, None, 0))
        return None

    def dma(self, name, fn, after=(), eng="sync"):
        self._wait(eng, after)
        s = self.sem(name)
        self.count[s] += 16
        self.items[eng].append(("op", fn, s, 16))
        return (s, self.count[s])

    def emit(self, block):
        for e in ENGINES:
            def body(handle, e=e):
                for it in self.items[e]:
                    if it[0] == "wait":
                        handle.wait_ge(self.sems[it[1]], it[2])
                    else:
                        r = it[1](handle)
                        if it[2] is not None:
                            r.then_inc(self.sems[it[2]], it[3])
            register = {"tensor": block.tensor, "vector": block.vector, "scalar": block.scalar,
                            "gpsimd": block.gpsimd, "sync": block.sync}
            register[e](body)


def build(nc, x, wqkv0, bqk0, bv0, cent, gb, w1, b1, w2, b2, wqkv1, bqk1, bv1, convw, convb,
          outw, outb, u1, v1, fb1, u2, v2, fb2, out):
    ctx = ExitStack()
    with ctx:
        Q = Queues(nc, ctx)
        op, dma = Q.op, Q.dma

        def sb(name, shape, dt=F32):
            return ctx.enter_context(nc.sbuf_tensor("t_" + name, shape, dt))

        def ps(name, shape):
            return ctx.enter_context(nc.psum_tensor("p_" + name, shape, F32))

        X = sb("X", [128, NT, 256])
        R1 = sb("R1", [128, 16384])
        R2 = sb("R2", [128, 16384])
        R3 = sb("R3", [128, 1632])
        r2b = R2[:, :].bitcast(BF)
        QA = [r2b[:, i * 4096:(i + 1) * 4096].rearrange("p (h n) -> p h n", h=8) for i in (4, 0, 2)]
        KA = [r2b[:, i * 4096:(i + 1) * 4096].rearrange("p (h n) -> p h n", h=8) for i in (5, 1, 3)]
        P = [R2[:, 12288 + i * 2048:12288 + (i + 1) * 2048].rearrange("p (h n) -> p h n", h=4) for i in range(2)]
        V0 = [R3[:, i * 544:(i + 1) * 544].rearrange("p (k h d) -> p k h d", k=4, h=8) for i in range(3)]
        W1 = R1[:, :].rearrange("p (e n) -> p e n", e=NE)
        W2 = R2[:, 0:16384].rearrange("p (e n) -> p e n", e=NE)
        XT = R1[:, 0:8192].rearrange("p (c n) -> p c n", c=2)
        V1S = [R1[:, 8192 + i * 544:8192 + (i + 1) * 544].rearrange("p (k h d) -> p k h d", k=4, h=8)
               for i in range(8)]

        S1 = [ps(f"S1{i}", [128, 512]) for i in range(3)]
        S2 = [ps(f"S2{i}", [128, 512]) for i in range(3)]
        PV = ps("PV", [128, 512])
        M = ps("M", [128, 512])

        ident = sb("ident", [128, 128])
        identb = sb("identb", [128, 128], BF)
        maskq = sb("maskq", [128, 128], BF)
        maskk = sb("maskk", [128, 128], BF)
        G = "gpsimd"
        V = "vector"
        A = "scalar"
        T = "tensor"

        zi = op(G, lambda e: nc.gpsimd.memset(ident[:, :], 0.0))
        zb = op(G, lambda e: nc.gpsimd.memset(identb[:, :], 0.0))
        zq = op(G, lambda e: nc.gpsimd.memset(maskq[:, :], 0.0))
        zk = op(G, lambda e: nc.gpsimd.memset(maskk[:, :], 0.0))
        mident = op(G, lambda e: nc.gpsimd.affine_select(out=ident[:, :], in_=ident[:, :], compare_op=ALU.not_equal,
                    fill=1.0, base=0, pattern=[[-1, 128]], channel_multiplier=1), [zi])
        op(G, lambda e: nc.gpsimd.affine_select(out=identb[:, :], in_=identb[:, :], compare_op=ALU.not_equal,
                    fill=1.0, base=0, pattern=[[-1, 128]], channel_multiplier=1), [zb])
        mconst = op(G, lambda e: nc.gpsimd.affine_select(out=maskq[:, :], in_=maskq[:, :], compare_op=ALU.is_ge,
                    fill=1.0, base=0, pattern=[[-1, 128]], channel_multiplier=1), [zq])
        mconst = op(G, lambda e: nc.gpsimd.affine_select(out=maskk[:, :], in_=maskk[:, :], compare_op=ALU.is_ge,
                    fill=1.0, base=0, pattern=[[1, 128]], channel_multiplier=-1), [zk])
        mconst = op(V, lambda e: nc.vector.tensor_scalar(maskk[:, :], maskk[:, :], NEG, None, ALU.mult), [mconst])
        mconst = op(V, lambda e: nc.vector.tensor_scalar(maskq[:, :], maskq[:, :], NEG, None, ALU.mult), [mconst])

        xv = x.rearrange("(t p) d -> p t d", p=128)
        ov = out.rearrange("(t p) d -> p t d", p=128)
        mx_in = [dma(f"d_x{b}", lambda e, b=b: e.dma_start(X[:, 4 * b:4 * b + 4, :], xv[:, 4 * b:4 * b + 4, :]))
                 for b in range(NB)]

        def load(name, shape, src, dt=F32):
            t = sb(name, shape, dt)
            m = dma("d_w", lambda e: e.dma_start(t[:], src))
            return t, m

        WQ, _ = load("WQ", [128, 2, 768], wqkv0)
        BQK, _ = load("BQK", [128, 4], bqk0)
        BV, _ = load("BV", [128, 256], bv0.rearrange("(o n) -> o n", o=1).to_broadcast([128, 256]))
        CT, _ = load("CT", [128, 2, NE], cent)
        GB, mw = load("GB", [128, NE, 4], gb)
        mw1 = [dma("d_w1", lambda e, i=i: e.dma_start(W1[:, i, :], w1[:, i, :])) for i in range(NE)][-1]

        st = sb("st", [128, 4, 6])
        mv = sb("mv", [128, NT, 2])
        rs = sb("rs", [128, NT])
        mv2 = sb("mv2", [128, NT, 2])
        rs2 = sb("rs2", [128, NT])
        nt_ = sb("nt_", [128, NT])
        nu_ = sb("nu_", [128, NT])
        nw_ = sb("nw_", [128, NT])
        xnb = sb("xnb", [128, 4, 256])
        cT = sb("cT", [128, 2, 514])
        h0b = cT[:, :, :].rearrange("p a n -> p (a n)")[:, 0:1024].rearrange("p (k n) -> p k n", k=4)
        xTb = sb("xTb", [128, 2, 512])
        AF = sb("AF", [128, NT, NE])
        spl = sb("spl", [128, 2, 3, 512], BF)
        rr = sb("rr", [128, 512])
        mx = sb("mx", [128, 2, 16])
        msp = sb("msp", [16, 3, 128], BF)
        mrr = sb("mrr", [16, 128])
        O = sb("O", [128, 512])
        OW = R3[:, 0:512].rearrange("p (c n) -> p c n", c=2)
        rc = sb("rc", [128, 4, 4])
        rc0 = sb("rc0", [128, 16])
        on = sb("on", [128, 256])
        on0 = on[:, :].rearrange("p (r d) -> p r d", r=16)

        qs = nc.dram_tensor("qs", (48, 128, 3, 512), BF).ap()
        ks = nc.dram_tensor("ks", (32, 128, 3, 512), BF).ap()
        msd = nc.dram_tensor("msd", (96, 16, 3, 128), BF).ap()
        h0d = nc.dram_tensor("h0d", (4096, 256), F32).ap()
        ysd = nc.dram_tensor("ysd", (TM * 128, 256), F32).ap()
        idd = nc.dram_tensor("idd", (TM * 128, 1), I32).ap()

        free = {"M": None, "rr": None, "S1": [None] * 3, "S2": [None] * 3, "PV": None, "P": [None, None],
                "O": None, "on": None, "spl": [None, None], "xnb": [], "h0b": None, "xTb": None,
                "mx": [None, None], "msp": None, "QA": [[], [], []], "KA": [[], [], []]}

        def rstd(var, dst, lo, hi, after):
            a = slice(lo, hi)
            nu, y, w, w2 = nu_[:, a], dst, nt_[:, a], nw_[:, a]
            m = op(V, lambda e: nc.vector.tensor_scalar(nu, var, EPS, None, ALU.add), after)
            yield
            m = op(V, lambda e: nc.vector.tensor_scalar(w.bitcast(I32), nu.bitcast(I32), 1, None,
                                                        ALU.arith_shift_right), [m])
            yield
            m = op(V, lambda e: nc.vector.tensor_scalar(y.bitcast(I32), w.bitcast(I32), -1.0, 1597463007.0,
                                                        ALU.mult, ALU.add), [m])
            yield
            for _ in range(3):
                m = op(G, lambda e: nc.gpsimd.tensor_tensor(w, y, y, ALU.mult), [m])
                m = op(G, lambda e: nc.gpsimd.tensor_tensor(w2, w, nu, ALU.mult), [m])
                m = op(G, lambda e: nc.gpsimd.tensor_scalar(w, w2, -0.5, 1.5, ALU.mult, ALU.add), [m])
                m = op(G, lambda e: nc.gpsimd.tensor_tensor(y, y, w, ALU.mult), [m])
                yield
            rsm[0] = m

        rsm = [None]
        sts = sb("sts", [128, NT, 6])

        def stats(t, src, m, after):
            s = op(V, lambda e: nc.vector.bn_stats(sts[:, t, :], src), after)
            return op(V, lambda e: nc.vector.bn_aggr(m[:, t, :], sts[:, t, :]), [s])

        xnm, h0m = {}, {}

        def norm(b, ready):
            ms = None
            for k in range(4):
                t = 4 * b + k
                ms = stats(t, X[:, t, :], mv, [ready])
                yield
            yield from rstd(mv[:, 4 * b:4 * b + 4, 1], rs[:, 4 * b:4 * b + 4], 4 * b, 4 * b + 4, [ms])
            mr, m = rsm[0], None
            for k in range(4):
                t = 4 * b + k
                m = op(V, lambda e, t=t, k=k: nc.vector.tensor_scalar(
                    xnb[:, k, :], X[:, t, :], mv[:, t, 0:1], rs[:, t:t + 1], ALU.subtract, ALU.mult),
                    [mr, *free["xnb"]])
                yield
            xnm[b] = m

        def norm0(u):
            b = u.b
            if u.c:
                return
            yield from norm(b, mx_in[b])
            ms = None
            for k in range(4):
                ms = stats(4 * b + k, xnb[:, k, :], mv2, [xnm[b]])
                yield
            yield from rstd(mv2[:, 4 * b:4 * b + 4, 1], rs2[:, 4 * b:4 * b + 4], 4 * b, 4 * b + 4, [ms])
            mr = rsm[0]
            for k in range(4):
                t = 4 * b + k
                mh = op(G, lambda e, t=t, k=k: nc.gpsimd.tensor_scalar(
                    h0b[:, k, :], xnb[:, k, :], mv2[:, t, 0:1], rs2[:, t:t + 1], ALU.subtract, ALU.mult),
                    [mr, free["h0b"]])
            d = dma("d_h0", lambda e: e.dma_start(
                h0d.rearrange("(t p) d -> p t d", p=128)[:, 4 * b:4 * b + 4, :], h0b[:, :, :]), [mh])
            free["h0b"] = d
            h0m[b] = mh

        def transposes(src, dst, src_ready, dst_free, eng=A):
            m = None
            for c in range(2):
                for k in range(4):
                    t = op(T, lambda e, c=c, k=k: nc.tensor.transpose(
                        M[:, k * 128:(k + 1) * 128], src[:, k, c * 128:(c + 1) * 128], ident[:, :]),
                        [src_ready, free["M"], mident], mark=(k == 3))
                m = op(A, lambda e, c=c: nc.scalar.copy(dst[:, c, :], M[:, :]), [t, dst_free])
                free["M"] = m
                yield m

        def split_out(z, bias, after_mm, name, dram, bw):
            a1 = op(A, lambda e: nc.scalar.activation(spl[:, z, 0, :], M[:, :], ACT.Identity, bias=bias),
                    [after_mm, free["spl"][z], bw])
            a2 = op(V, lambda e: nc.vector.scalar_tensor_tensor(out=rr[:, :], in0=M[:, :], scalar=bias,
                    in1=spl[:, z, 0, :], op0=ALU.add, op1=ALU.subtract), [a1, free["rr"]])
            free["M"] = a2
            a3 = op(G, lambda e: nc.gpsimd.tensor_copy(spl[:, z, 1, :], rr[:, :]), [a2])
            a4 = op(G, lambda e: nc.gpsimd.tensor_tensor(spl[:, z, 2, :], rr[:, :], spl[:, z, 1, :], ALU.subtract), [a3])
            free["rr"] = a4
            d = dma(name, lambda e: e.dma_start(dram, spl[:, z, :, :]), [a4])
            free["spl"][z] = d
            return d

        def fan(dst, dram, parts, name, after):
            m = None
            for j, s in enumerate(parts):
                m = dma(name, lambda e, j=j, s=s: e.dma_start(
                    dst[16 * j:16 * j + 16, :, :], dram[:, s, :].rearrange("(h d) n -> d h n", d=16)), after)
            return m

        QP, KP = (0, 0, 0, 1, 1, 2), (0, 1, 2, 0, 1, 0)

        class Unit:

            def __init__(self, n, kind, b, c):
                self.n, self.kind, self.b, self.c = n, kind, b, c
                self.causal = kind > 0
                self.buf = n % 3
                self.qready = self.kready = self.vready = None
                self.mready = [None, None]
                self.tail = None

        xt_ready = {}
        kdram = {}
        vready = {}
        vfree = {}
        ctxT_ready = {}
        cnt = {"s1": 0, "s2": 0, "p": 0, "mg": 0}

        def vtile(u):
            if u.kind == 0:
                return V0[u.n % 3], ("v0", u.n % 3)
            i = (2 * u.b + u.c) % 8
            return V1S[i], ("v1", i)

        def project(u, xT, wt, bt, bvt, wm, xm):
            c = u.c
            for z, (off, parts) in enumerate(((0, QP), (256, KP))):
                for cc in range(2):
                    t = op(T, lambda e, cc=cc, off=off: nc.tensor.matmul(
                        M[:, :], wt[:, cc, off + c * 128:off + c * 128 + 128], xT[:, cc, :],
                        start=(cc == 0), stop=(cc == 1)), [xm, free["M"], wm], mark=(cc == 1))
                dram = qs[u.n] if z == 0 else ks[(0 if u.kind == 0 else 16) + 2 * u.b + c]
                d = split_out(z, bt[:, 2 * z + c:2 * z + c + 1], t, f"d_sp{z}", dram, wm)
                buf = (QA if z == 0 else KA)[u.buf]
                fr = free["QA" if z == 0 else "KA"][u.buf]
                m = fan(buf, dram, parts, f"d_f{z}{u.buf}", [d, *fr])
                if z == 0:
                    u.qready = m
                else:
                    u.kready = m
                    kdram[(u.kind, u.b, c)] = dram
                yield
            vt, key = vtile(u)
            for k in range(4):
                for cc in range(2):
                    t = op(T, lambda e, cc=cc, k=k: nc.tensor.matmul(
                        M[:, k * 128:(k + 1) * 128], xT[:, cc, k * 128:(k + 1) * 128],
                        wt[:, cc, 512 + c * 128:512 + c * 128 + 128], start=(cc == 0), stop=(cc == 1)),
                        [xm, free["M"], wm], mark=(k == 3 and cc == 1))
            a = op(V, lambda e: nc.vector.tensor_tensor(
                vt[:, :, :, 0:16], M[:, :].rearrange("p (k h d) -> p k h d", k=4, h=8),
                bvt[:, c * 128:c * 128 + 128].rearrange("p (o h d) -> p o h d", o=1, h=8).to_broadcast([128, 4, 8, 16]),
                ALU.add), [t, vfree.get(key), wm])
            free["M"] = a
            u.vready = vready[(u.kind, u.b, c)] = a
            yield

        def pre0(u):
            b = u.b
            if u.c == 0:
                for xm in transposes(xnb, xTb, xnm[b], free["xTb"]):
                    yield
                g = op(G, lambda e: nc.gpsimd.tensor_tensor(
                    X[:, 4 * b:4 * b + 4, :], X[:, 4 * b:4 * b + 4, :], xnb[:, :, :], ALU.add), [xm])
                xadd[b] = g
                for k in range(4):
                    for cc in range(2):
                        t = op(T, lambda e, k=k, cc=cc: nc.tensor.matmul(
                            M[:, k * 8:k * 8 + 8], xTb[:, cc, k * 128:(k + 1) * 128], CT[:, cc, :],
                            start=(cc == 0), stop=(cc == 1)), [xm, free["M"], mw], mark=(k == 3 and cc == 1))
                a = op(V, lambda e: nc.vector.tensor_copy(
                    AF[:, 4 * b:4 * b + 4, :], M[:, 0:32].rearrange("p (k e) -> p k e", k=4)), [t])
                free["M"] = a
                free["xnb"] = [g, xm, h0m[b]]
                afready.append(a)
                xt_ready[b] = xm
                yield
            yield from project(u, xTb, WQ, BQK, BV, mw, xt_ready[b])
            free["xTb"] = Q.last[T]

        xadd, afready = {}, []

        def maxp(u):
            qa, ka = QA[u.buf], KA[u.buf]
            for g in range(2):
                gi = cnt["mg"] % 2
                cnt["mg"] += 1
                r = None
                if u.causal:
                    packs = [(0, (0, 1, 2, 3))] + [(1, (0, 1)), (1, (2, 3))] + [(qb, (j,)) for j in range(4) for qb in (2, 3)]
                else:
                    packs = [(qb, (j,)) for j in range(4) for qb in range(4)]
                for qb, js in packs:
                    n = 128 * (qb + 1) if u.causal else 512
                    s = cnt["s1"] % 3
                    cnt["s1"] += 1
                    bank = S1[s][:, 0:len(js) * n].rearrange("p (j n) -> p j n", j=len(js))
                    for z, j in enumerate(js):
                        t = op(T, lambda e, bank=bank, z=z, h=4 * g + j, qb=qb, n=n: nc.tensor.matmul(
                            bank[:, z, :], qa[0:96, h, qb * 128:(qb + 1) * 128], ka[0:96, h, 0:n],
                            start=True, stop=not u.causal), [u.qready, u.kready, free["S1"][s]],
                            mark=not u.causal and j == js[-1])
                        if u.causal:
                            t = op(T, lambda e, bank=bank, z=z, n=n: nc.tensor.matmul(
                                bank[:, z, n - 128:n], identb[:, :], maskq[:, :], start=False, stop=True), [mconst],
                                mark=j == js[-1])
                    r = op(V, lambda e, bank=bank, i=4 * js[0] + qb, k=len(js), gi=gi: nc.vector.tensor_reduce(
                        mx[:, gi, i:i + 4 * k - 3:4], bank, AX.X, ALU.max), [t, free["mx"][gi]])
                    free["S1"][s] = r
                    yield
                t = op(T, lambda e, gi=gi: nc.tensor.transpose(M[0:16, 0:128], mx[:, gi, :], ident[:, :]),
                       [r, free["M"], mident])
                free["mx"][gi] = t
                a1 = op(V, lambda e, gi=gi: nc.vector.tensor_scalar(msp[:, 0, :], M[0:16, 0:128], -1.0, None, ALU.mult),
                        [t, free["msp"]])
                a2 = op(V, lambda e: nc.vector.scalar_tensor_tensor(
                    out=mrr[:, :], in0=M[0:16, 0:128], scalar=-1.0, in1=msp[:, 0, :],
                    op0=ALU.mult, op1=ALU.subtract), [a1])
                free["M"] = a2
                a3 = op(V, lambda e, gi=gi: nc.vector.tensor_copy(msp[:, 1, :], mrr[:, :]), [a2])
                a4 = op(V, lambda e, gi=gi: nc.vector.tensor_tensor(
                    msp[:, 2, :], mrr[:, :], msp[:, 1, :], ALU.subtract), [a3])
                i = 2 * u.n + g
                d1 = dma("d_m", lambda e, gi=gi, i=i: e.dma_start(msd[i], msp[:, :, :]), [a4])
                free["msp"] = d1
                u.mready[g] = dma(f"d_mq{u.buf}{g}", lambda e, g=g, i=i: e.dma_start(
                    qa[96:99, 4 * g:4 * g + 4, :], msd[i].rearrange("a s p -> s a p")), [d1, *free["QA"][u.buf]])
                yield

        def pv(u, g, kb, slot, e_ready):
            vt, _ = vtile(u)
            n0 = 128 * kb if u.causal else 0
            t = None
            for j in range(4):
                t = op(T, lambda e, j=j: nc.tensor.matmul(
                    PV[32 * j:32 * j + 17, n0:512], vt[:, kb, 4 * g + j, :], P[slot][:, j, 0:512 - n0],
                    start=(kb == 0), stop=(kb == 3), skip_group_check=True),
                    [e_ready, u.vready, free["PV"] if kb == 0 else None], mark=(j == 3))
            free["P"][slot] = t
            return t

        def expp(u):
            qa, ka = QA[u.buf], KA[u.buf]
            pend = None

            def close(g, t):
                if u.kind == 0:
                    a = op(V, lambda e: nc.vector.transpose(
                        O[:, :].rearrange("p (r d) -> p r d", r=16), PV[:, :].rearrange("p (n r) -> p r n", r=16)),
                        [t, free["O"]])
                    free["PV"] = a
                    yield
                    od = O[:, :].rearrange("p (r d) -> p r d", r=16)
                    r = op(V, lambda e: nc.vector.reciprocal(rc0[:, :], od[:, :, 16]), [a, free["on"]])
                    a = op(V, lambda e: nc.vector.tensor_tensor(
                        on0, od[:, :, 0:16], rc0[:, :].rearrange("p (r o) -> p r o", o=1).to_broadcast([128, 16, 16]),
                        ALU.mult), [r])
                    free["O"] = a
                    tgt = X[:, 4 * u.b + 2 * u.c + g, :].rearrange("p (r d) -> p r d", r=16)
                    free["on"] = op(G, lambda e: nc.gpsimd.tensor_tensor(tgt, tgt, on0, ALU.add), [a, xadd[u.b]])
                    return
                a = op(A, lambda e: nc.scalar.copy(O[:, :], PV[:, :]), [t, free["O"]])
                free["PV"] = a
                yield
                for k in range(4):
                    t = op(T, lambda e, k=k: nc.tensor.transpose(
                        M[:, k * 128:(k + 1) * 128], O[:, k * 128:(k + 1) * 128], ident[:, :]),
                        [a, free["M"], mident], mark=(k == 3))
                free["O"] = t
                mo = M[:, :].rearrange("p (k j d) -> p k j d", k=4, j=4)
                r = op(V, lambda e: nc.vector.reciprocal(rc[:, :, :], mo[:, :, :, 16]), [t, free["on"]])
                rb = rc[:, :, :].rearrange("p k (j o) -> p k j o", o=1).to_broadcast([128, 4, 4, 16])
                done1(u, g, mo[:, :, :, 0:16], rb, r)

            for g in range(2):
                for kb in range(4):
                    n0 = 128 * kb if u.causal else 0
                    n = 512 - n0
                    slot = cnt["p"] % 2
                    cnt["p"] += 1
                    ex = None
                    per = {512: 1, 384: 1, 256: 2, 128: 4}[n]
                    for j0 in range(0, 4, per):
                        s = cnt["s2"] % 3
                        cnt["s2"] += 1
                        bank = S2[s][:, 0:per * n].rearrange("p (j n) -> p j n", j=per)
                        for z in range(per):
                            t = op(T, lambda e, bank=bank, z=z, h=4 * g + j0 + z, n0=n0, kb=kb: nc.tensor.matmul(
                                bank[:, z, :], ka[0:99, h, kb * 128:(kb + 1) * 128], qa[0:99, h, n0:512],
                                start=True, stop=not u.causal),
                                [u.qready, u.kready, u.mready[g], free["S2"][s], mones[0]],
                                mark=(z == per - 1 and not u.causal))
                            if u.causal:
                                t = op(T, lambda e, bank=bank, z=z: nc.tensor.matmul(
                                    bank[:, z, 0:128], identb[:, :], maskk[:, :], start=False, stop=True),
                                    [mconst], mark=(z == per - 1))
                        ex = op(A, lambda e, bank=bank, j0=j0, per=per, n=n, slot=slot: nc.scalar.activation(
                            P[slot][:, j0:j0 + per, 0:n], bank, ACT.Exp,
                            scale=0.25 if u.causal else 1.0), [t, free["P"][slot]])
                        free["S2"][s] = ex
                        if pend is not None and j0 + per >= 2:
                            t = pv(*pend)
                            last = pend
                            pend = None
                            if last[2] == 3:
                                yield
                                yield from close(last[1], t)
                        yield
                    pend = (u, g, kb, slot, ex)
            t = pv(*pend)
            free["QA"][u.buf] = [t]
            free["KA"][u.buf] = [t]
            vt, key = vtile(u)
            if u.kind != 1:
                vfree[key] = t
            yield
            yield from close(1, t)

        def merge(lanes):
            live = [True] * len(lanes)
            k = 0
            while any(live):
                for z, (g, every) in enumerate(lanes):
                    if live[z] and k % every == 0:
                        try:
                            next(g)
                        except StopIteration:
                            live[z] = False
                k += 1

        def run(units, first, pre, extra):
            def gen(f, i):
                return f(units[i]) if 0 <= i < len(units) else iter(())
            for i in range(first, len(units) + 1):
                lanes = [(gen(maxp, i + 1), 1), (gen(expp, i), 1), (gen(pre, i + 2), 3)]
                merge(lanes + extra(i, gen))

        mones = [None]

        def init_attention(after, vt):
            for i in range(3):
                op(V, lambda e, i=i: nc.vector.memset(KA[i][96:99, :, :], 1.0), after)
            for t in vt:
                op(V, lambda e, t=t: nc.vector.memset(t[:, :, :, 16:17], 1.0), after)
            w = op(V, lambda e: nc.vector.memset(PV[:, :], 0.0), after)
            m = op(G, lambda e: nc.gpsimd.memset(rr[:, 0:1], 0.0), [Q.last[G], w])
            mones[0] = m
            free["rr"] = m

        init_attention([], V0)

        def barrier():
            return [Q.last[e] for e in (T, V, A, G)] + [(s, Q.count[s]) for s in Q.sems if s.startswith("d_")]

        B2 = R3[0:3, 0:1024].bitcast(BF).rearrange("p (e n) -> p e n", e=NE)
        cTv = cT[:, :, :].rearrange("p a n -> p (a n)")
        WQv = WQ[:, :, :].rearrange("p a n -> p (a n)")

        def wq8(i):
            return WQv[:, i * 256:(i + 1) * 256].rearrange("p (t e) -> p t e", e=NE)

        B1T = sb("B1T", [128, NE, 8])
        bd2 = nc.dram_tensor("bd2", (3, 2048), BF).ap()
        bt = sb("bt", [128, 16])
        br = sb("br", [128, 16])
        bs = sb("bs", [128, 3, 16], BF)
        ones3 = sb("ones3", [3, 128], BF)
        on3 = op(V, lambda e: nc.vector.memset(ones3[:, :], 1.0))
        mb1 = dma("d_b1", lambda e: e.dma_start(B1T[:, :, :], b1))
        m = dma("d_b", lambda e: e.dma_start(bt[:, :], b2.rearrange("(p n) -> p n", p=128)))
        m = op(V, lambda e: nc.vector.tensor_copy(bs[:, 0, :], bt[:, :]), [m])
        m = op(V, lambda e: nc.vector.tensor_tensor(br[:, :], bt[:, :], bs[:, 0, :], ALU.subtract), [m])
        m = op(V, lambda e: nc.vector.tensor_copy(bs[:, 1, :], br[:, :]), [m])
        m = op(V, lambda e: nc.vector.tensor_tensor(bs[:, 2, :], br[:, :], bs[:, 1, :], ALU.subtract), [m])
        m = dma("d_b", lambda e: e.dma_start(bd2.rearrange("s (p n) -> p s n", p=128), bs[:, :, :]), [m])
        mb2 = m

        tri = sb("tri", [128, 128])
        onesf = sb("onesf", [128, 128])
        io8 = sb("io8", [128, NE])
        ioT = sb("ioT", [128, TM])
        tok = sb("tok", [128, NT], I32)
        z39 = sb("z39", [128, TM], I32)
        g1 = op(G, lambda e: nc.gpsimd.memset(tri[:, :], 0.0))
        op(G, lambda e: nc.gpsimd.memset(onesf[:, :], 1.0))
        op(G, lambda e: nc.gpsimd.affine_select(out=tri[:, :], in_=tri[:, :], compare_op=ALU.is_ge, fill=1.0,
                                                base=0, pattern=[[-1, 128]], channel_multiplier=1), [g1])
        op(G, lambda e: nc.gpsimd.iota(io8[:, :], pattern=[[1, NE]], base=0, channel_multiplier=0,
                                       allow_small_or_imprecise_dtypes=True))
        op(G, lambda e: nc.gpsimd.iota(ioT[:, :], pattern=[[1, TM]], base=0, channel_multiplier=0,
                                       allow_small_or_imprecise_dtypes=True))
        op(G, lambda e: nc.gpsimd.iota(tok[:, :], pattern=[[128, NT]], base=0, channel_multiplier=1))
        mg = op(G, lambda e: nc.gpsimd.memset(z39[:, :], 0))
        mzid = dma("d_z", lambda e: e.dma_start(idd.rearrange("(p t) o -> p (t o)", p=128), z39[:, :]), [mg])

        def bc(ap, shape):
            return ap.to_broadcast(shape)

        amax = sb("amax", [128, NT])
        alpha = sb("alpha", [128, NT])
        eq = wq8(0)
        oh = wq8(1)
        emin = sb("emin", [128, NT])
        wi = wq8(2)
        tt = [wq8(3), wq8(4)]
        tot = wq8(5)
        te_ = [sb("tea", [128, NE]), sb("teb", [128, NE])]
        tl = sb("tl", [128, NE])
        tli = sb("tli", [128, NE], I32)
        slotf = sb("slotf", [128, NT])
        sloti = sb("sloti", [128, NT], I32)
        lo7 = sb("lo7", [128, NT], I32)
        hi7 = sb("hi7", [128, NT], I32)
        lof = sb("lof", [128, NT])
        hif = sb("hif", [128, NT])
        sidx = sb("sidx", [128, NT], I32)
        tcm = rr[:, 0:TM * NE].rearrange("p (t e) -> p t e", e=NE)
        texf = sb("texf", [128, TM])
        texp = sb("texp", [128, TM], I32)
        gidx = sb("gidx", [128, TM], I32)

        def v(f, *after):
            return op(V, f, list(after))

        rt = {}

        def route():
            start = [Q.last[T], Q.last[G], free["rr"], free["h0b"], *free["xnb"]]
            s8 = [128, NT, NE]
            m = v(lambda e: nc.vector.tensor_reduce(amax[:, :], AF[:, :, :], AX.X, ALU.max), afready[-1], *start)
            yield
            ma = op(A, lambda e: nc.scalar.activation(alpha[:, :], amax[:, :], ACT.Exp, scale=-1.0), [m])
            yield
            ma = v(lambda e: nc.vector.tensor_scalar(alpha[:, :], alpha[:, :], 1.0, None, ALU.add), ma)
            yield
            malpha = v(lambda e: nc.vector.reciprocal(alpha[:, :], alpha[:, :]), ma)
            yield
            m = v(lambda e: nc.vector.tensor_tensor(eq[:, :, :], AF[:, :, :],
                  bc(amax[:, :].rearrange("p (t o) -> p t o", o=1), s8), ALU.is_ge), m)
            yield
            m = v(lambda e: nc.vector.scalar_tensor_tensor(out=eq[:, :, :], in0=eq[:, :, :], scalar=-8.0,
                  in1=bc(io8[:, :].rearrange("p (o e) -> p o e", o=1), s8), op0=ALU.mult, op1=ALU.add), m, mg)
            yield
            m = v(lambda e: nc.vector.tensor_reduce(emin[:, :], eq[:, :, :], AX.X, ALU.min), m)
            yield
            m = v(lambda e: nc.vector.tensor_tensor(oh[:, :, :], eq[:, :, :],
                  bc(emin[:, :].rearrange("p (t o) -> p t o", o=1), s8), ALU.is_equal), m)
            yield
            ohf = oh[:, :, :].rearrange("p t e -> p (t e)")
            op(T, lambda e: nc.tensor.matmul(M[:, 0:256], tri[:, :], ohf, start=True, stop=True), [m, mg, free["M"]], mark=False)
            t = op(T, lambda e: nc.tensor.matmul(M[:, 256:512], onesf[:, :], ohf, start=True, stop=True))
            m1 = v(lambda e: nc.vector.tensor_copy(wi[:, :, :].rearrange("p t e -> p (t e)"), M[:, 0:256]), t)
            m = v(lambda e: nc.vector.tensor_copy(tot[:, :, :].rearrange("p t e -> p (t e)"), M[:, 256:512]), t)
            free["M"] = m
            yield
            src = tot
            for i, s in enumerate((1, 2, 4, 8, 16)):
                dst = tt[i % 2]
                m2 = v(lambda e, src=src, dst=dst, s=s: nc.vector.tensor_copy(dst[:, 0:s, :], src[:, 0:s, :]), m)
                yield
                m = v(lambda e, src=src, dst=dst, s=s: nc.vector.tensor_tensor(
                    dst[:, s:NT, :], src[:, s:NT, :], src[:, 0:NT - s, :], ALU.add), m2)
                yield
                src = dst
            inc = src
            m = v(lambda e: nc.vector.tensor_scalar(tl[:, :], inc[:, NT - 1, :], 127.0, None, ALU.add), m)
            yield
            m = v(lambda e: nc.vector.tensor_copy(tli[:, :], tl[:, :]), m)
            yield
            m = v(lambda e: nc.vector.tensor_scalar(tli[:, :], tli[:, :], 7, None, ALU.arith_shift_right), m)
            yield
            m = v(lambda e: nc.vector.tensor_copy(tl[:, :], tli[:, :]), m)
            yield
            src = tl
            for i, s in enumerate((1, 2, 4)):
                dst = te_[i % 2]
                m2 = v(lambda e, src=src, dst=dst, s=s: nc.vector.tensor_copy(dst[:, 0:s], src[:, 0:s]), m)
                yield
                m = v(lambda e, src=src, dst=dst, s=s: nc.vector.tensor_tensor(
                    dst[:, s:NE], src[:, s:NE], src[:, 0:NE - s], ALU.add), m2)
                yield
                src = dst
            ends, base = te_[0], te_[1]
            m2 = v(lambda e: nc.vector.tensor_tensor(base[:, :], ends[:, :], tl[:, :], ALU.subtract), m)
            yield
            m2 = v(lambda e: nc.vector.tensor_scalar(base[:, :], base[:, :], 128.0, None, ALU.mult), m2)
            yield
            m3 = v(lambda e: nc.vector.tensor_tensor(wi[:, :, :], wi[:, :, :], inc[:, :, :], ALU.add), m2, m1)
            yield
            m3 = v(lambda e: nc.vector.tensor_tensor(wi[:, :, :], wi[:, :, :], tot[:, :, :], ALU.subtract), m3)
            yield
            m3 = v(lambda e: nc.vector.tensor_tensor(wi[:, :, :], wi[:, :, :],
                   bc(base[:, :].rearrange("p (o e) -> p o e", o=1), s8), ALU.add), m3)
            yield
            m3 = v(lambda e: nc.vector.tensor_tensor(wi[:, :, :], wi[:, :, :], oh[:, :, :], ALU.mult), m3)
            yield
            m3 = v(lambda e: nc.vector.tensor_reduce(slotf[:, :], wi[:, :, :], AX.X, ALU.add), m3)
            yield
            m3 = v(lambda e: nc.vector.tensor_copy(sloti[:, :], slotf[:, :]), m3)
            yield
            mslot = m3
            m3 = v(lambda e: nc.vector.tensor_scalar(lo7[:, :], sloti[:, :], 127, None, ALU.bitwise_and), m3)
            yield
            m3 = v(lambda e: nc.vector.tensor_scalar(hi7[:, :], sloti[:, :], 7, None, ALU.arith_shift_right), m3)
            yield
            m3 = v(lambda e: nc.vector.tensor_copy(lof[:, :], lo7[:, :]), m3)
            yield
            m3 = v(lambda e: nc.vector.tensor_copy(hif[:, :], hi7[:, :]), m3)
            yield
            m3 = v(lambda e: nc.vector.scalar_tensor_tensor(out=lof[:, :], in0=lof[:, :], scalar=float(TM), in1=hif[:, :],
                   op0=ALU.mult, op1=ALU.add), m3)
            yield
            midx = v(lambda e: nc.vector.tensor_copy(sidx[:, :], lof[:, :]), m3)
            yield
            s39 = [128, TM, NE]
            m = v(lambda e: nc.vector.tensor_tensor(tcm[:, :, :], bc(ends[:, :].rearrange("p (o e) -> p o e", o=1), s39),
                  bc(ioT[:, :].rearrange("p (t o) -> p t o", o=1), s39), ALU.is_le), m)
            yield
            m = v(lambda e: nc.vector.tensor_reduce(texf[:, :], tcm[:, :, :], AX.X, ALU.add), m)
            yield
            m = v(lambda e: nc.vector.tensor_scalar(texf[:, :], texf[:, :], float(NE - 1), None, ALU.min), m)
            yield
            mtex = v(lambda e: nc.vector.tensor_copy(texp[:, :], texf[:, :]), m)

            yield
            m = None
            for t in range(NT):
                m = dma("d_sc", lambda e, t=t: nc.gpsimd.indirect_dma_start(
                    idd, bass.IndirectOffsetOnAxis(ap=sidx[:, t:t + 1].bitcast(U32), axis=0), tok[:, t:t + 1], None),
                    [midx, mzid, mg], eng=G)
                yield
            mgi = dma("d_gi", lambda e: e.dma_start(gidx[:, :], idd.rearrange("(p t) o -> p (t o)", p=128)), [m])
            rt.update(alpha=malpha, slot=mslot, tex=mtex, gi=mgi)
            gather(0)
            gather(1)

        spf = spl[:, :, :, :].rearrange("p a b n -> p (a b n)").bitcast(F32)
        hs = [spf[:, 1024:1280], spf[:, 1280:1536], on[:, :]]
        hT = [cTv[:, i * 256:(i + 1) * 256].rearrange("p (c n) -> p c n", c=2) for i in range(2)]
        AA = [xnb[:, :, :].rearrange("p a n -> p (a n)"), xTb[:, :, :].rearrange("p a n -> p (a n)")]
        AT = spf[:, 0:1024].rearrange("p (k n) -> p k n", k=8)
        Y = [cTv[:, 512 + i * 256:768 + i * 256] for i in range(2)]
        ef = {"hs": [None] * 3, "hT": [None] * 2, "AA": [None] * 2, "AT": [None, None], "Y": [None] * 2,
              "B": [None] * 2, "S1": [None, None], "PV": None}
        gath = {}
        bar_ = []
        regs = {}

        def gather(t):
            gath[t] = dma(f"d_hs{t % 3}", lambda e: nc.gpsimd.indirect_dma_start(
                hs[t % 3], None, h0d, bass.IndirectOffsetOnAxis(ap=gidx[:, t:t + 1].bitcast(U32), axis=0)),
                [rt["gi"], ef["hs"][t % 3], *(free["spl"] if t < 2 else bar_)], eng=G)

        def extra0(i, gen):
            lanes = [(gen(norm0, i + 3), 1)]
            if i == 14:
                lanes.append((route(), 1))
                load_w2((0, 1), free["QA"][1])
            if i == 15:
                load_w2((2, 3), free["QA"][2])
            if i == 16:
                load_w2((4, 5, 6, 7), [*free["QA"][0], *free["P"]])
            return lanes

        mw2 = []

        def load_w2(experts, after):
            for i in experts:
                mw2[:] = [dma("d_w2", lambda e, i=i: e.dma_start(W2[:, i, :], w2[:, i, :]), after)]

        units = [Unit(n, 0, n // 2, n % 2) for n in range(16)]
        for i in (-3,):
            merge([(norm0(units[0]), 1)])
        run(units, -2, pre0, extra0)

        bar = barrier()
        bar_ += bar
        mbias = dma("d_b2", lambda e: e.dma_start(B2.rearrange("s e n -> s (e n)"), bd2), [mb2, *bar])

        def expert(eng, t):
            def f(e):
                regs[(eng, t)] = e.value_load(texp[0:1, t:t + 1], min_val=0, max_val=NE - 1)
            return f

        aready = {}

        banks = [S2[0], S2[1], S2[2], S1[2]]

        def head(t):
            i = t % 2
            for eng in (T, V):
                Q._wait(eng, [rt["tex"]])
                Q.items[eng].append(("op", expert(eng, t), None, 0))
            for c in range(2):
                x_ = op(T, lambda e, c=c: nc.tensor.transpose(M[:, c * 128:(c + 1) * 128],
                        hs[t % 3][:, c * 128:(c + 1) * 128], ident[:, :]), [gath[t], free["M"]], mark=(c == 1))
            ef["hs"][t % 3] = x_
            for c in range(2):
                y_ = op(V, lambda e, c=c: nc.vector.tensor_scalar(
                    hT[i][:, c, :], M[:, c * 128:(c + 1) * 128],
                    GB[:, bass.ds(regs[(V, t)], 1), c:c + 1], GB[:, bass.ds(regs[(V, t)], 1), 2 + c:3 + c],
                    ALU.mult, ALU.add), [x_, ef["hT"][i], *bar])
            free["M"] = y_
            hready[t] = y_

        def up(t):
            i = t % 2
            for f in range(2):
                bank = banks[2 * i + f]
                for c in range(2):
                    z_ = op(T, lambda e, f=f, c=c, bank=bank: nc.tensor.matmul(
                        bank[:, :], hT[i][:, c, :],
                        W1[:, bass.ds(regs[(T, t)], 1), c * 1024 + f * 512:c * 1024 + f * 512 + 512],
                        start=(c == 0), stop=(c == 1)), [hready[t], ef["B"][i], mw1], mark=(c == 1))
                a_ = op(A, lambda e, f=f, bank=bank: nc.scalar.copy(AA[i][:, f * 512:(f + 1) * 512], bank[:, :]),
                        [z_, ef["AA"][i]])
            ef["hT"][i] = z_
            ef["B"][i] = a_
            aready[t] = a_

        def turn(t):
            i = t % 2
            for f in range(2):
                for k in range(4):
                    t_ = op(T, lambda e, f=f, k=k: nc.tensor.transpose(
                        S1[f][:, k * 128:(k + 1) * 128], AA[i][:, (4 * f + k) * 128:(4 * f + k + 1) * 128], ident[:, :]),
                        [aready[t], ef["S1"][f]], mark=(k == 3))
                for k in range(4):
                    cp[f] = op(V, lambda e, f=f, k=k: nc.vector.tensor_scalar(
                        AT[:, 4 * f + k, :], S1[f][:, k * 128:(k + 1) * 128],
                        B1T[:, bass.ds(regs[(V, t)], 1), 4 * f + k:4 * f + k + 1], 0.0, ALU.add, ALU.max),
                        [t_, ef["AT"][f], mb1])
                ef["S1"][f] = cp[f]
            ef["AA"][i] = t_

        def down(t):
            i = t % 2
            for k in range(8):
                t_ = op(T, lambda e, k=k: nc.tensor.matmul(
                    PV[:, 0:256], AT[:, k, :], W2[:, bass.ds(regs[(T, t)], 1), k * 256:k * 256 + 256],
                    start=(k == 0), stop=False), [cp[k // 4], ef["PV"], *mw2], mark=(k in (3, 7)))
                if k in (3, 7):
                    ef["AT"][k // 4] = t_
            t_ = op(T, lambda e: nc.tensor.matmul(
                PV[:, 0:256], ones3[:, :], B2[:, bass.ds(regs[(T, t)], 1), :], start=False, stop=True), [mbias, on3])
            a_ = op(A, lambda e: nc.scalar.copy(Y[i], PV[:, 0:256]), [t_, ef["Y"][i]])
            ef["PV"] = a_
            ef["Y"][i] = dma(f"d_y{i}", lambda e: e.dma_start(ysd[t * 128:(t + 1) * 128, :], Y[i]), [a_])

        hready = {}
        cp = [None, None]
        head(0)
        gather(2)
        up(0)
        head(1)
        for t in range(TM):
            turn(t)
            if t + 3 < TM:
                gather(t + 3)
            if t + 1 < TM:
                up(t + 1)
            if t + 2 < TM:
                head(t + 2)
            down(t)

        bar = barrier()
        gy = [R2[:, 14336 + i * 256:14592 + i * 256] for i in range(8)]
        gyf = [None] * 8
        WQ1 = WQ

        def loadl(view, src):
            return dma("d_l1", lambda e: e.dma_start(view, src), bar)

        CW = R1[:, 12544:14080].rearrange("p (a n) -> p a n", a=6)
        OB = R3[:, 512:768]
        FB = R3[:, 768:1024]
        CB = sb("CB", [128, 2])
        U1 = R3[:, 1024:1280].rearrange("p (c n) -> p c n", c=2)
        r2c = R2[:, :].bitcast(BF)
        V1f, V1r = R2[:, 0:1024], R2[:, 1024:2048]
        V1a, V1b, V1c = r2c[:, 4096:5120], r2c[:, 5120:6144], r2c[:, 6144:7168]
        VA, VB = r2c[:, 16384:17408], r2c[:, 17408:18432]
        U2 = R2[:, 9216:9728].rearrange("p (k n) -> p k n", k=8)
        V2 = R2[:, 9728:9984]
        Pr = R2[:, 9984:10496]
        PT = [r2c[:, 20992 + i * 1536:22528 + i * 1536].rearrange("p (a n) -> p a n", a=3) for i in range(2)]
        QS = [R2[:, 12032 + i * 512:12544 + i * 512] for i in range(2)]
        HT = [R1[:, 14080 + i * 512:14592 + i * 512] for i in range(4)]
        FBI = sb("FBI", [128, 8])
        loadl(U1, u1)
        loadl(V1f[0:64], v1)
        loadl(V1f[64:128], v1)
        loadl(U2, u2)
        loadl(V2[0:64], v2)
        loadl(V2[64:128], v2)
        loadl(OB, outb.rearrange("(o n) -> o n", o=1).to_broadcast([128, 256]))
        loadl(FB, fb2.rearrange("(o n) -> o n", o=1).to_broadcast([128, 256]))
        ml1 = loadl(FBI[:], fb1)

        def loadm(view, src):
            return dma("d_l2", lambda e: e.dma_start(view, src), bar)

        loadm(WQ1[:], wqkv1)
        loadm(BQK[:], bqk1)
        loadm(BV[:], bv1.rearrange("(o n) -> o n", o=1).to_broadcast([128, 256]))
        loadm(CW, convw)
        loadm(OW, outw)
        ml2 = loadm(CB[:], convb)

        def gathers(b):
            for k in range(4):
                t = 4 * b + k
                gm[t] = dma(f"d_gy{t % 8}", lambda e, t=t: nc.gpsimd.indirect_dma_start(
                    gy[t % 8], None, ysd, bass.IndirectOffsetOnAxis(ap=sloti[:, t:t + 1].bitcast(U32), axis=0)),
                    [gyf[t % 8], rt["slot"], *bar], eng=G)
                yield

        gm = {}
        ff = {"PT": [None] * 2, "HT": [None] * 4, "QS": [None] * 2, "hb": [None] * 3, "qb": [None, None],
              "yb": [None, None], "Pr": None}
        pready = {}
        free["xnb"] = bar

        def near(b):
            yield from gathers(b)
            a = None
            for k in range(4):
                t = 4 * b + k
                a = v(lambda e, t=t: nc.vector.scalar_tensor_tensor(
                    out=X[:, t, :], in0=gy[t % 8], scalar=alpha[:, t:t + 1], in1=X[:, t, :], op0=ALU.mult, op1=ALU.add),
                    gm[t], rt["alpha"], *bar)
                gyf[t % 8] = a
                yield
            yield from norm(b, a)
            xm = None
            for xm in transposes(xnb, XT[:, :, 512 * b:512 * b + 512], xnm[b], None):
                yield
            free["xnb"] = [Q.last[T]]
            xt_ready[("l1", b)] = xm
            p = PT[b % 2]
            for cc in range(2):
                t = op(T, lambda e, cc=cc, b=b: nc.tensor.matmul(
                    M[:, :], U1[:, cc, :], XT[:, cc, 512 * b:512 * b + 512], start=(cc == 0), stop=(cc == 1)),
                    [xm, free["M"], ml1], mark=(cc == 1))
            a1 = op(A, lambda e: nc.scalar.copy(p[:, 0, :], M[:, :]), [t, ff["PT"][b % 2]])
            a2 = v(lambda e: nc.vector.tensor_tensor(Pr, M[:, :], p[:, 0, :], ALU.subtract), a1, ff["Pr"])
            free["M"] = a2
            yield
            a3 = v(lambda e: nc.vector.tensor_copy(p[:, 1, :], Pr), a2)
            yield
            a4 = v(lambda e: nc.vector.tensor_tensor(p[0:64, 2, :], Pr[0:64], p[0:64, 1, :], ALU.subtract), a3)
            a5 = op(A, lambda e: nc.scalar.copy(p[64:128, 2, :], p[64:128, 0, :]), [a1])
            ff["Pr"] = a4
            pready[b] = [a4, a5]

        hc = [0]

        def far(b):
            p = PT[b % 2]
            qb = (PV, S1[0])[b % 2]

            def u2mm(j):
                q = None
                for f, (ready, hi) in j:
                    h = f % 2
                    q = op(T, lambda e, f=f, h=h, hi=hi: nc.tensor.matmul(
                        qb[64 * h:64 * h + 64, :], U2[:, f, :], HT[hi], start=(f < 2), stop=(f >= 6),
                        skip_group_check=True), [ready, ff["qb"][b % 2]])
                    ff["HT"][hi] = q
                return q

            pend = []
            for f in range(8):
                bi, hi = hc[0] % 3, hc[0] % 4
                hc[0] += 1
                hb = S2[bi]
                for z, (vv, pp) in enumerate(((VA, 0), (VA, 1), (VB, 2))):
                    t = op(T, lambda e, z=z, vv=vv, pp=pp, f=f, hb=hb: nc.tensor.matmul(
                        hb[:, :], vv[:, f * 128:(f + 1) * 128], p[:, pp, :], start=(z == 0), stop=(z == 2)),
                        [*pready[b], mva, ff["hb"][bi]], mark=(z == 2))
                g_ = op(A, lambda e, f=f, hb=hb, hi=hi: nc.scalar.activation(
                    HT[hi], hb[:, :], ACT.Gelu_apprx_tanh, bias=FBI[:, f:f + 1]), [t, ff["HT"][hi]])
                ff["hb"][bi] = g_
                pend.append((f, (g_, hi)))
                if f % 2 == 1 and f >= 3:
                    u2mm(pend[:2])
                    pend = pend[2:]
                yield
            ff["PT"][b % 2] = t
            qm = u2mm(pend)
            a = op(A, lambda e: nc.scalar.copy(QS[b % 2], qb[:, :]), [qm, ff["QS"][b % 2]])
            ff["qb"][b % 2] = a
            yield
            for h in range(2):
                yb = S1[1 + h]
                for k in range(2):
                    t = op(T, lambda e, h=h, k=k, yb=yb: nc.tensor.matmul(
                        yb[:, k * 256:(k + 1) * 256], QS[b % 2][:, (2 * h + k) * 128:(2 * h + k + 1) * 128], V2,
                        start=True, stop=True), [a, ff["yb"][h]], mark=(k == 1))
                tg = X[:, 4 * b + 2 * h:4 * b + 2 * h + 2, :]
                y_ = v(lambda e, tg=tg, yb=yb: nc.vector.tensor_tensor(
                    tg, tg, yb[:, :].rearrange("p (k n) -> p k n", k=2), ALU.add), t, xnm[b])
                ff["yb"][h] = y_
                yield
            ff["QS"][b % 2] = t
            tb = X[:, 4 * b:4 * b + 4, :]
            xadd[b] = op(G, lambda e: nc.gpsimd.tensor_tensor(
                tb, tb, OB.rearrange("p (o n) -> p o n", o=1).to_broadcast([128, 4, 256]), ALU.add), [y_, mbb])

        def parts():
            m = v(lambda e: nc.vector.tensor_copy(V1a, V1f), ml1)
            m = v(lambda e: nc.vector.tensor_tensor(V1r, V1f, V1a, ALU.subtract), m)
            m = v(lambda e: nc.vector.tensor_copy(V1b, V1r), m)
            m = v(lambda e: nc.vector.tensor_tensor(V1c, V1r, V1b, ALU.subtract), m)
            v(lambda e: nc.vector.tensor_copy(VA[0:64], V1a[0:64]), m)
            v(lambda e: nc.vector.tensor_copy(VA[64:128], V1b[64:128]), m)
            v(lambda e: nc.vector.tensor_copy(VB[0:64], V1a[0:64]), m)
            return v(lambda e: nc.vector.tensor_copy(VB[64:128], V1c[64:128]), m)

        merge([(near(0), 1)])
        mbb = op(G, lambda e: nc.gpsimd.tensor_tensor(OB, OB, FB, ALU.add), [ml1])
        mva = parts()
        for b in range(NB - 1):
            merge([(near(b + 1), 1), (far(b), 3)])

        CTX = [R1[:, 14080:15104].rearrange("p (k n) -> p k n", k=4),
               R1[:, 15104:16128].rearrange("p (k n) -> p k n", k=4), xnb]
        c2T = xTb
        for t in V1S:
            op(V, lambda e, t=t: nc.vector.memset(t[:, :, :, 16:17], 1.0), bar)
        for k in (0, 513):
            mpad = op(V, lambda e, k=k: nc.vector.memset(cT[:, :, k:k + 1], 0.0))
        free["QA"] = [[], [mva], [mva]]
        free["KA"] = [[], [mva], [mva]]
        vfree.clear()

        ctxm = {}
        ctxf = [None] * 3

        def cslot(kind, b):
            return b % 2 if kind == 1 else 2

        cTf = [None]

        def pre1(u):
            b, c = u.b, u.c
            if u.kind == 1:
                yield from project(u, XT[:, :, 512 * b:512 * b + 512], WQ1, BQK, BV, ml2, xt_ready[("l1", b)])
                return
            if c == 0:
                cx = CTX[cslot(1, b)]
                for m in transposes(cx, cT[:, :, 1:513], ctxm[(1, b)], cTf[0]):
                    yield
                ctxf[cslot(1, b)] = Q.last[T]
                ctxT_ready[b] = m
            for i in range(6):
                k, cc = i // 2, i % 2
                t = op(T, lambda e, i=i, k=k, cc=cc: nc.tensor.matmul(
                    M[:, :], CW[:, i, c * 128:c * 128 + 128], cT[:, cc, k:k + 512], start=(i == 0), stop=(i == 5)),
                    [ctxT_ready[b], mpad, ml2, free["M"]], mark=(i == 5))
            cTf[0] = t
            d = split_out(0, CB[:, c:c + 1], t, "d_sp0", qs[u.n], ml2)
            u.qready = fan(QA[u.buf], qs[u.n], QP, f"d_f0{u.buf}", [d, *free["QA"][u.buf]])
            yield
            u.kready = fan(KA[u.buf], kdram[(1, b, c)], KP, f"d_f1{u.buf}", [*free["KA"][u.buf]])
            u.vready = vready[(1, b, c)]
            yield

        def done1(u, g, vals, rb, r):
            key = (u.kind, u.b)
            s = cslot(*key)
            lo = u.c * 128 + g * 64
            tg = CTX[s][:, :, lo:lo + 64].rearrange("p k (j d) -> p k j d", j=4)
            a = op(V, lambda e: nc.vector.tensor_tensor(tg, vals, rb, ALU.mult), [r, ctxf[s]])
            free["M"] = a
            free["on"] = a
            ctxm[key] = a

        def fin1(u):
            if u.kind != 2 or u.c != 1:
                return
            b = u.b
            cx = CTX[cslot(2, b)]
            for m in transposes(cx, c2T, ctxm[(2, b)], free["xTb"]):
                yield
            ctxf[cslot(2, b)] = Q.last[T]
            for h in range(2):
                for k in range(2):
                    for cc in range(2):
                        t = op(T, lambda e, h=h, k=k, cc=cc: nc.tensor.matmul(
                            M[:, k * 256:(k + 1) * 256], c2T[:, cc, (2 * h + k) * 128:(2 * h + k + 1) * 128],
                            OW[:, cc, :], start=(cc == 0), stop=(cc == 1)), [m, free["M"], ml2], mark=(k == 1 and cc == 1))
                tg = X[:, 4 * b + 2 * h:4 * b + 2 * h + 2, :]
                y_ = v(lambda e, tg=tg: nc.vector.tensor_tensor(
                    tg, tg, M[:, :].rearrange("p (k n) -> p k n", k=2), ALU.add), t, xadd[b])
                free["M"] = y_
                yield
            free["xTb"] = t
            dma("d_out", lambda e: e.dma_start(ov[:, 4 * b:4 * b + 4, :], X[:, 4 * b:4 * b + 4, :]), [y_])

        order, a1, a2 = [], 0, 0
        while a2 < NB:
            if a1 < NB and a1 < a2 + 2:
                order += [(1, a1, 0), (1, a1, 1)]
                a1 += 1
            else:
                order += [(2, a2, 0), (2, a2, 1)]
                a2 += 1
        units = [Unit(n, kind, b, c) for n, (kind, b, c) in enumerate(order, 16)]
        merge([(far(NB - 1), 1), (pre1(units[0]), 3), (pre1(units[1]), 3)])
        bar = barrier()
        init_attention(bar, [])
        for key in ("M", "PV", "O", "on", "xTb"):
            free[key] = mones[0]
        free["xnb"] = [mones[0]]
        free["S1"] = [mones[0]] * 3
        free["S2"] = [mones[0]] * 3
        free["P"] = [mones[0]] * 2
        free["QA"][0] = [mones[0]]
        free["KA"][0] = [mones[0]]
        ctxf[:] = [mones[0]] * 3
        run(units, -1, pre1, lambda i, gen: [(gen(fin1, i - 1), 3)])

        ends_ = [(s, Q.count[s]) for s in Q.sems if s.startswith("d_")]
        Q._wait("sync", ends_)
        block = ctx.enter_context(nc.Block())
        Q.emit(block)


_ARGS = ["x", "wqkv0", "bqk0", "bv0", "cent", "gb", "w1", "b1", "w2", "b2", "wqkv1", "bqk1", "bv1", "convw", "convb",
         "outw", "outb", "u1", "v1", "fb1", "u2", "v2", "fb2"]


def kernel(**inputs):
    import numpy as np
    import concourse.bacc as bacc
    from concourse.bass_utils import run_bass_kernel_spmd

    i = {k: np.asarray(v) for k, v in inputs.items()}

    def rows(w):
        return w.reshape(2, 128, -1).transpose(1, 0, 2)

    g, b = i["L0_ffn_ln_g"].reshape(8, 2, 128), i["L0_ffn_ln_b"].reshape(8, 2, 128)
    a = {
        "x": i["L0_attn_x"].reshape(4096, 256),
        "wqkv0": rows(i["L0_attn_W_qkv"]),
        "bqk0": i["L0_attn_b_qkv"][0:512].reshape(4, 128).T,
        "bv0": i["L0_attn_b_qkv"][512:768],
        "cent": rows(i["L0_ffn_centroids"].T),
        "gb": np.concatenate([g, b], axis=1).transpose(2, 0, 1),
        "w1": i["L0_ffn_w1"].transpose(0, 2, 1).reshape(8, 2, 128, 1024).transpose(2, 0, 1, 3).reshape(128, 8, 2048),
        "b1": i["L0_ffn_b1"].reshape(8, 8, 128).transpose(2, 0, 1),
        "w2": i["L0_ffn_w2"].transpose(0, 2, 1).reshape(8, 8, 128, 256).transpose(2, 0, 1, 3).reshape(128, 8, 2048),
        "b2": i["L0_ffn_b2"].reshape(-1),
        "wqkv1": rows(i["L1_attn_Wqkv_w"].T),
        "bqk1": i["L1_attn_Wqkv_b"][0:512].reshape(4, 128).T,
        "bv1": i["L1_attn_Wqkv_b"][512:768],
        "convw": i["L1_attn_conv_w"].transpose(2, 1, 0).reshape(3, 2, 128, 256).transpose(2, 0, 1, 3).reshape(128, 6, 256),
        "convb": i["L1_attn_conv_b"].reshape(2, 128).T,
        "outw": rows(i["L1_attn_out_w"].T),
        "outb": i["L1_attn_out_b"],
        "u1": np.concatenate([rows(i["L1_ffn_U1"])] * 2, axis=2),
        "v1": i["L1_ffn_V1"],
        "fb1": i["L1_ffn_b1"].reshape(8, 128).T,
        "u2": i["L1_ffn_U2"].reshape(8, 128, 64).transpose(1, 0, 2),
        "v2": i["L1_ffn_V2"],
        "fb2": i["L1_ffn_b2"],
    }
    nc = bacc.Bacc("TRN2", target_bir_lowering=False, num_devices=1)
    arrays, args = {}, []
    for name in _ARGS:
        arrays[f"in_{name}"] = np.ascontiguousarray(a[name])
        args.append(nc.dram_tensor(f"in_{name}", a[name].shape, F32, kind="ExternalInput").ap())
    args.append(nc.dram_tensor("out", (4096, 256), F32, kind="ExternalOutput").ap())
    build(nc, *args)
    r = run_bass_kernel_spmd(nc, [arrays], core_ids=[0])
    return r.results[0]["out"].reshape(8, 512, 256)
```

```python
import concourse.bass as bass
from concourse import mybir
from contextlib import ExitStack

F32 = mybir.dt.float32
BF = mybir.dt.bfloat16
I32 = mybir.dt.int32
U32 = mybir.dt.uint32
ALU = mybir.AluOpType
ACT = mybir.ActivationFunctionType
AX = mybir.AxisListType

NB = 8
NT = 32
NE = 8
TM = 39
EPS = 1e-5
NEG = -(2.0 ** 127)
ENGINES = ("tensor", "vector", "scalar", "gpsimd", "sync")


class Queues:

    def __init__(self, nc, ctx):
        self.nc, self.ctx = nc, ctx
        self.items = {e: [] for e in ENGINES}
        self.sems, self.count = {}, {}
        self.seen = {e: {} for e in ENGINES}
        self.last = {}

    def sem(self, name):
        if name not in self.sems:
            self.sems[name] = self.ctx.enter_context(self.nc.semaphore(name))
            self.count[name] = 0
        return name

    def _wait(self, eng, after):
        need = {}
        for m in after:
            if m is not None and m[1] > self.seen[eng].get(m[0], 0):
                need[m[0]] = max(need.get(m[0], 0), m[1])
        for s, v in need.items():
            self.seen[eng][s] = v
            self.items[eng].append(("wait", s, v))

    def op(self, eng, fn, after=(), mark=True):
        self._wait(eng, after)
        if mark:
            s = self.sem("s_" + eng)
            self.count[s] += 1
            self.items[eng].append(("op", fn, s, 1))
            self.last[eng] = (s, self.count[s])
            return self.last[eng]
        self.items[eng].append(("op", fn, None, 0))
        return None

    def dma(self, name, fn, after=(), eng="sync"):
        self._wait(eng, after)
        s = self.sem(name)
        self.count[s] += 16
        self.items[eng].append(("op", fn, s, 16))
        return (s, self.count[s])

    def emit(self, block):
        for e in ENGINES:
            def body(handle, e=e):
                for it in self.items[e]:
                    if it[0] == "wait":
                        handle.wait_ge(self.sems[it[1]], it[2])
                    else:
                        r = it[1](handle)
                        if it[2] is not None:
                            r.then_inc(self.sems[it[2]], it[3])
            register = {"tensor": block.tensor, "vector": block.vector, "scalar": block.scalar,
                            "gpsimd": block.gpsimd, "sync": block.sync}
            register[e](body)


def build(nc, x, wqkv0, bqk0, bv0, cent, gb, w1, b1, w2, b2, wqkv1, bqk1, bv1, convw, convb,
          outw, outb, u1, v1, fb1, u2, v2, fb2, out):
    ctx = ExitStack()
    with ctx:
        Q = Queues(nc, ctx)
        op, dma = Q.op, Q.dma

        def sb(name, shape, dt=F32):
            return ctx.enter_context(nc.sbuf_tensor("t_" + name, shape, dt))

        def ps(name, shape):
            return ctx.enter_context(nc.psum_tensor("p_" + name, shape, F32))

        X = sb("X", [128, NT, 256])
        R1 = sb("R1", [128, 16384])
        R2 = sb("R2", [128, 16384])
        R3 = sb("R3", [128, 1632])
        r2b = R2[:, :].bitcast(BF)
        QA = [r2b[:, i * 4096:(i + 1) * 4096].rearrange("p (h n) -> p h n", h=8) for i in (4, 0, 2)]
        KA = [r2b[:, i * 4096:(i + 1) * 4096].rearrange("p (h n) -> p h n", h=8) for i in (5, 1, 3)]
        P = [R2[:, 12288 + i * 2048:12288 + (i + 1) * 2048].rearrange("p (h n) -> p h n", h=4) for i in range(2)]
        V0 = [R3[:, i * 544:(i + 1) * 544].rearrange("p (k h d) -> p k h d", k=4, h=8) for i in range(3)]
        W1 = R1[:, :].rearrange("p (e n) -> p e n", e=NE)
        W2 = R2[:, 0:16384].rearrange("p (e n) -> p e n", e=NE)
        XT = R1[:, 0:8192].rearrange("p (c n) -> p c n", c=2)
        V1S = [R1[:, 8192 + i * 544:8192 + (i + 1) * 544].rearrange("p (k h d) -> p k h d", k=4, h=8)
               for i in range(8)]

        S1 = [ps(f"S1{i}", [128, 512]) for i in range(3)]
        S2 = [ps(f"S2{i}", [128, 512]) for i in range(2)]
        PV = ps("PV", [128, 512])
        MB = [ps("Ma", [128, 512]), ps("Mb", [128, 512])]

        ident = sb("ident", [128, 128])
        identb = sb("identb", [128, 128], BF)
        maskq = sb("maskq", [128, 128], BF)
        maskk = sb("maskk", [128, 128], BF)
        G = "gpsimd"
        V = "vector"
        A = "scalar"
        T = "tensor"

        zi = op(G, lambda e: nc.gpsimd.memset(ident[:, :], 0.0))
        zb = op(G, lambda e: nc.gpsimd.memset(identb[:, :], 0.0))
        zq = op(G, lambda e: nc.gpsimd.memset(maskq[:, :], 0.0))
        zk = op(G, lambda e: nc.gpsimd.memset(maskk[:, :], 0.0))
        mident = op(G, lambda e: nc.gpsimd.affine_select(out=ident[:, :], in_=ident[:, :], compare_op=ALU.not_equal,
                    fill=1.0, base=0, pattern=[[-1, 128]], channel_multiplier=1), [zi])
        op(G, lambda e: nc.gpsimd.affine_select(out=identb[:, :], in_=identb[:, :], compare_op=ALU.not_equal,
                    fill=1.0, base=0, pattern=[[-1, 128]], channel_multiplier=1), [zb])
        mconst = op(G, lambda e: nc.gpsimd.affine_select(out=maskq[:, :], in_=maskq[:, :], compare_op=ALU.is_ge,
                    fill=1.0, base=0, pattern=[[-1, 128]], channel_multiplier=1), [zq])
        mconst = op(G, lambda e: nc.gpsimd.affine_select(out=maskk[:, :], in_=maskk[:, :], compare_op=ALU.is_ge,
                    fill=1.0, base=0, pattern=[[1, 128]], channel_multiplier=-1), [zk])
        mconst = op(V, lambda e: nc.vector.tensor_scalar(maskk[:, :], maskk[:, :], NEG, None, ALU.mult), [mconst])
        mconst = op(V, lambda e: nc.vector.tensor_scalar(maskq[:, :], maskq[:, :], NEG, None, ALU.mult), [mconst])

        xv = x.rearrange("(t p) d -> p t d", p=128)
        ov = out.rearrange("(t p) d -> p t d", p=128)
        mx_in = [dma(f"d_x{b}", lambda e, b=b: e.dma_start(X[:, 4 * b:4 * b + 4, :], xv[:, 4 * b:4 * b + 4, :]))
                 for b in (0,)]

        def load(name, shape, src, dt=F32):
            t = sb(name, shape, dt)
            m = dma("d_w", lambda e: e.dma_start(t[:], src))
            return t, m

        WQ, _ = load("WQ", [128, 2, 768], wqkv0)
        BQK, _ = load("BQK", [128, 4], bqk0)
        BV, _ = load("BV", [128, 256], bv0.rearrange("(o n) -> o n", o=1).to_broadcast([128, 256]))
        CT, _ = load("CT", [128, 2, NE], cent)
        GB, mw = load("GB", [128, NE, 4], gb)

        def load_x(b):
            mx_in.append(dma(f"d_x{b}", lambda e: e.dma_start(X[:, 4 * b:4 * b + 4, :], xv[:, 4 * b:4 * b + 4, :])))

        load_x(1)
        mw1 = []

        st = sb("st", [128, 4, 6])
        mv = sb("mv", [128, NT, 2])
        rs = sb("rs", [128, NT])
        mv2 = sb("mv2", [128, NT, 2])
        rs2 = sb("rs2", [128, NT])
        nt_ = sb("nt_", [128, NT])
        nu_ = sb("nu_", [128, NT])
        nw_ = sb("nw_", [128, NT])
        xnb = sb("xnb", [128, 4, 256])
        cT = sb("cT", [128, 2, 514])
        h0b = cT[:, :, :].rearrange("p a n -> p (a n)")[:, 0:1024].rearrange("p (k n) -> p k n", k=4)
        xTb = sb("xTb", [128, 2, 512])
        AF = sb("AF", [128, NT, NE])
        spl = sb("spl", [128, 2, 3, 512], BF)
        rr = sb("rr", [128, 512])
        mx = sb("mx", [128, 2, 16])
        msp = sb("msp", [16, 3, 128], BF)
        mrr = sb("mrr", [16, 128])
        O = sb("O", [128, 512])
        OW = R3[:, 0:512].rearrange("p (c n) -> p c n", c=2)
        rc = sb("rc", [128, 4, 4])
        rc0 = sb("rc0", [128, 16])
        on = sb("on", [128, 256])
        on0 = on[:, :].rearrange("p (r d) -> p r d", r=16)

        qs = nc.dram_tensor("qs", (48, 128, 3, 512), BF).ap()
        ks = nc.dram_tensor("ks", (32, 128, 3, 512), BF).ap()
        msd = nc.dram_tensor("msd", (96, 16, 3, 128), BF).ap()
        h0d = nc.dram_tensor("h0d", (4096, 256), F32).ap()
        ysd = nc.dram_tensor("ysd", (TM * 128, 256), F32).ap()
        idd = nc.dram_tensor("idd", (TM * 128, 1), I32).ap()

        free = {"M": [None, None], "rr": None, "S1": [None] * 3, "S2": [None] * 2, "PV": None, "P": [None, None],
                "O": None, "on": None, "spl": [None, None], "xnb": [], "h0b": None, "xTb": None,
                "mx": [None, None], "msp": None, "QA": [[], [], []], "KA": [[], [], []]}

        def rstd(var, dst, lo, hi, after):
            a = slice(lo, hi)
            nu, y, w, w2 = nu_[:, a], dst, nt_[:, a], nw_[:, a]
            m = op(V, lambda e: nc.vector.tensor_scalar(nu, var, EPS, None, ALU.add), after)
            yield
            m = op(V, lambda e: nc.vector.tensor_scalar(w.bitcast(I32), nu.bitcast(I32), 1, None,
                                                        ALU.arith_shift_right), [m])
            yield
            m = op(V, lambda e: nc.vector.tensor_scalar(y.bitcast(I32), w.bitcast(I32), -1.0, 1597463007.0,
                                                        ALU.mult, ALU.add), [m])
            yield
            for _ in range(3):
                m = op(G, lambda e: nc.gpsimd.tensor_tensor(w, y, y, ALU.mult), [m])
                m = op(G, lambda e: nc.gpsimd.tensor_tensor(w2, w, nu, ALU.mult), [m])
                m = op(G, lambda e: nc.gpsimd.tensor_scalar(w, w2, -0.5, 1.5, ALU.mult, ALU.add), [m])
                m = op(G, lambda e: nc.gpsimd.tensor_tensor(y, y, w, ALU.mult), [m])
                yield
            rsm[0] = m

        rsm = [None]
        sts = sb("sts", [128, NT, 6])

        def stats(t, src, m, after):
            s = op(V, lambda e: nc.vector.bn_stats(sts[:, t, :], src), after)
            return op(V, lambda e: nc.vector.bn_aggr(m[:, t, :], sts[:, t, :]), [s])

        xnm, h0m = {}, {}

        def norm(b, ready, xnb, xfree):
            ms = None
            for k in range(4):
                t = 4 * b + k
                ms = stats(t, X[:, t, :], mv, [ready])
                yield
            yield from rstd(mv[:, 4 * b:4 * b + 4, 1], rs[:, 4 * b:4 * b + 4], 4 * b, 4 * b + 4, [ms])
            mr, m = rsm[0], None
            for k in range(4):
                t = 4 * b + k
                m = op(V, lambda e, t=t, k=k: nc.vector.tensor_scalar(
                    xnb[:, k, :], X[:, t, :], mv[:, t, 0:1], rs[:, t:t + 1], ALU.subtract, ALU.mult),
                    [mr, *xfree()])
                yield
            xnm[b] = m

        def norm0(u):
            b = u.b
            if u.c:
                return
            yield from norm(b, mx_in[b], xnb, lambda: free["xnb"])
            ms = None
            for k in range(4):
                ms = stats(4 * b + k, xnb[:, k, :], mv2, [xnm[b]])
                yield
            yield from rstd(mv2[:, 4 * b:4 * b + 4, 1], rs2[:, 4 * b:4 * b + 4], 4 * b, 4 * b + 4, [ms])
            mr = rsm[0]
            for k in range(4):
                t = 4 * b + k
                mh = op(G, lambda e, t=t, k=k: nc.gpsimd.tensor_scalar(
                    h0b[:, k, :], xnb[:, k, :], mv2[:, t, 0:1], rs2[:, t:t + 1], ALU.subtract, ALU.mult),
                    [mr, free["h0b"]])
            d = dma("d_h0", lambda e: e.dma_start(
                h0d.rearrange("(t p) d -> p t d", p=128)[:, 4 * b:4 * b + 4, :], h0b[:, :, :]), [mh])
            free["h0b"] = d
            h0m[b] = mh

        def mbank():
            cnt["m"] += 1
            return MB[cnt["m"] % 2], cnt["m"] % 2

        def transposes(src, dst, src_ready, dst_free, eng=A):
            m = None
            for c in range(2):
                M, mi = mbank()
                for k in range(4):
                    t = op(T, lambda e, M=M, c=c, k=k: nc.tensor.transpose(
                        M[:, k * 128:(k + 1) * 128], src[:, k, c * 128:(c + 1) * 128], ident[:, :]),
                        [src_ready, free["M"][mi], mident], mark=(k == 3))
                m = op(A, lambda e, M=M, c=c: nc.scalar.copy(dst[:, c, :], M[:, :]), [t, dst_free])
                free["M"][mi] = m
                yield m

        def split_out(M, mi, z, bias, after_mm, name, dram, bw):
            a1 = op(A, lambda e, M=M: nc.scalar.activation(spl[:, z, 0, :], M[:, :], ACT.Identity, bias=bias),
                    [after_mm, free["spl"][z], bw])
            a2 = op(V, lambda e, M=M: nc.vector.scalar_tensor_tensor(out=rr[:, :], in0=M[:, :], scalar=bias,
                    in1=spl[:, z, 0, :], op0=ALU.add, op1=ALU.subtract), [a1, free["rr"]])
            free["M"][mi] = a2
            a3 = op(G, lambda e: nc.gpsimd.tensor_copy(spl[:, z, 1, :], rr[:, :]), [a2])
            a4 = op(G, lambda e: nc.gpsimd.tensor_tensor(spl[:, z, 2, :], rr[:, :], spl[:, z, 1, :], ALU.subtract), [a3])
            free["rr"] = a4
            d = dma(name, lambda e: e.dma_start(dram, spl[:, z, :, :]), [a4])
            free["spl"][z] = d
            return d

        def fan(dst, dram, parts, name, after):
            m = None
            for j, s in enumerate(parts):
                m = dma(name, lambda e, j=j, s=s: e.dma_start(
                    dst[16 * j:16 * j + 16, :, :], dram[:, s, :].rearrange("(h d) n -> d h n", d=16)), after)
            return m

        QP, KP = (0, 0, 0, 1, 1, 2), (0, 1, 2, 0, 1, 0)

        class Unit:

            def __init__(self, n, kind, b, c):
                self.n, self.kind, self.b, self.c = n, kind, b, c
                self.causal = kind > 0
                self.buf = n % 3
                self.qready = self.kready = self.vready = None
                self.mready = [None, None]
                self.tail = None

        xt_ready = {}
        kdram = {}
        vready = {}
        vfree = {}
        ctxT_ready = {}
        cnt = {"m": 0, "s1": 0, "s2": 0, "p": 0, "mg": 0}

        def vtile(u):
            if u.kind == 0:
                return V0[u.n % 3], ("v0", u.n % 3)
            i = (2 * u.b + u.c) % 8
            return V1S[i], ("v1", i)

        def project(u, xT, wt, bt, bvt, wm, xm):
            c = u.c
            for z, (off, parts) in enumerate(((0, QP), (256, KP))):
                M, mi = mbank()
                for cc in range(2):
                    t = op(T, lambda e, M=M, cc=cc, off=off: nc.tensor.matmul(
                        M[:, :], wt[:, cc, off + c * 128:off + c * 128 + 128], xT[:, cc, :],
                        start=(cc == 0), stop=(cc == 1)), [xm, free["M"][mi], wm], mark=(cc == 1))
                dram = qs[u.n] if z == 0 else ks[(0 if u.kind == 0 else 16) + 2 * u.b + c]
                d = split_out(M, mi, z, bt[:, 2 * z + c:2 * z + c + 1], t, f"d_sp{z}", dram, wm)
                buf = (QA if z == 0 else KA)[u.buf]
                fr = free["QA" if z == 0 else "KA"][u.buf]
                m = fan(buf, dram, parts, f"d_f{z}{u.buf}", [d, *fr])
                if z == 0:
                    u.qready = m
                else:
                    u.kready = m
                    kdram[(u.kind, u.b, c)] = dram
                yield
            vt, key = vtile(u)
            M, mi = mbank()
            for k in range(4):
                for cc in range(2):
                    t = op(T, lambda e, M=M, cc=cc, k=k: nc.tensor.matmul(
                        M[:, k * 128:(k + 1) * 128], xT[:, cc, k * 128:(k + 1) * 128],
                        wt[:, cc, 512 + c * 128:512 + c * 128 + 128], start=(cc == 0), stop=(cc == 1)),
                        [xm, free["M"][mi], wm], mark=(k == 3 and cc == 1))
            a = op(V, lambda e, M=M: nc.vector.tensor_tensor(
                vt[:, :, :, 0:16], M[:, :].rearrange("p (k h d) -> p k h d", k=4, h=8),
                bvt[:, c * 128:c * 128 + 128].rearrange("p (o h d) -> p o h d", o=1, h=8).to_broadcast([128, 4, 8, 16]),
                ALU.add), [t, vfree.get(key), wm])
            free["M"][mi] = a
            u.vready = vready[(u.kind, u.b, c)] = a
            yield

        def pre0(u):
            b = u.b
            if u.c == 0:
                for xm in transposes(xnb, xTb, xnm[b], free["xTb"]):
                    yield
                g = op(G, lambda e: nc.gpsimd.tensor_tensor(
                    X[:, 4 * b:4 * b + 4, :], X[:, 4 * b:4 * b + 4, :], xnb[:, :, :], ALU.add), [xm])
                xadd[b] = g
                M, mi = mbank()
                for k in range(4):
                    for cc in range(2):
                        t = op(T, lambda e, M=M, k=k, cc=cc: nc.tensor.matmul(
                            M[:, k * 8:k * 8 + 8], xTb[:, cc, k * 128:(k + 1) * 128], CT[:, cc, :],
                            start=(cc == 0), stop=(cc == 1)), [xm, free["M"][mi], mw], mark=(k == 3 and cc == 1))
                a = op(V, lambda e, M=M: nc.vector.tensor_copy(
                    AF[:, 4 * b:4 * b + 4, :], M[:, 0:32].rearrange("p (k e) -> p k e", k=4)), [t])
                free["M"][mi] = a
                while b not in h0m:
                    yield
                free["xnb"] = [g, xm, h0m[b]]
                afready.append(a)
                xt_ready[b] = xm
                yield
            yield from project(u, xTb, WQ, BQK, BV, mw, xt_ready[b])
            free["xTb"] = Q.last[T]

        xadd, afready = {}, []

        def maxp(u):
            qa, ka = QA[u.buf], KA[u.buf]
            for g in range(2):
                gi = cnt["mg"] % 2
                cnt["mg"] += 1
                r = None
                if u.causal:
                    packs = [(0, (0, 1, 2, 3))] + [(1, (0, 1)), (1, (2, 3))] + [(qb, (j,)) for j in range(4) for qb in (2, 3)]
                else:
                    packs = [(qb, (j,)) for j in range(4) for qb in range(4)]
                for qb, js in packs:
                    n = 128 * (qb + 1) if u.causal else 512
                    s = cnt["s1"] % 3
                    cnt["s1"] += 1
                    bank = S1[s][:, 0:len(js) * n].rearrange("p (j n) -> p j n", j=len(js))
                    for z, j in enumerate(js):
                        t = op(T, lambda e, bank=bank, z=z, h=4 * g + j, qb=qb, n=n: nc.tensor.matmul(
                            bank[:, z, :], qa[0:96, h, qb * 128:(qb + 1) * 128], ka[0:96, h, 0:n],
                            start=True, stop=not u.causal), [u.qready, u.kready, free["S1"][s]],
                            mark=not u.causal and j == js[-1])
                        if u.causal:
                            t = op(T, lambda e, bank=bank, z=z, n=n: nc.tensor.matmul(
                                bank[:, z, n - 128:n], identb[:, :], maskq[:, :], start=False, stop=True), [mconst],
                                mark=j == js[-1])
                    r = op(V, lambda e, bank=bank, i=4 * js[0] + qb, k=len(js), gi=gi: nc.vector.tensor_reduce(
                        mx[:, gi, i:i + 4 * k - 3:4], bank, AX.X, ALU.max), [t, free["mx"][gi]])
                    free["S1"][s] = r
                    yield
                M, mi = mbank()
                t = op(T, lambda e, M=M, gi=gi: nc.tensor.transpose(M[0:16, 0:128], mx[:, gi, :], ident[:, :]),
                       [r, free["M"][mi], mident])
                free["mx"][gi] = t
                a1 = op(V, lambda e, M=M, gi=gi: nc.vector.tensor_scalar(msp[:, 0, :], M[0:16, 0:128], -1.0, None, ALU.mult),
                        [t, free["msp"]])
                a2 = op(V, lambda e, M=M: nc.vector.scalar_tensor_tensor(
                    out=mrr[:, :], in0=M[0:16, 0:128], scalar=-1.0, in1=msp[:, 0, :],
                    op0=ALU.mult, op1=ALU.subtract), [a1])
                free["M"][mi] = a2
                a3 = op(V, lambda e, gi=gi: nc.vector.tensor_copy(msp[:, 1, :], mrr[:, :]), [a2])
                a4 = op(V, lambda e, gi=gi: nc.vector.tensor_tensor(
                    msp[:, 2, :], mrr[:, :], msp[:, 1, :], ALU.subtract), [a3])
                i = 2 * u.n + g
                d1 = dma("d_m", lambda e, gi=gi, i=i: e.dma_start(msd[i], msp[:, :, :]), [a4])
                free["msp"] = d1
                u.mready[g] = dma(f"d_mq{u.buf}{g}", lambda e, g=g, i=i: e.dma_start(
                    qa[96:99, 4 * g:4 * g + 4, :], msd[i].rearrange("a s p -> s a p")), [d1, *free["QA"][u.buf]])
                yield

        def pv(u, g, kb, slot, e_ready):
            vt, _ = vtile(u)
            n0 = 128 * kb if u.causal else 0
            t = None
            for j in range(4):
                t = op(T, lambda e, j=j: nc.tensor.matmul(
                    PV[32 * j:32 * j + 17, n0:512], vt[:, kb, 4 * g + j, :], P[slot][:, j, 0:512 - n0],
                    start=(kb == 0), stop=(kb == 3), skip_group_check=True),
                    [e_ready, u.vready, free["PV"] if kb == 0 else None], mark=(j == 3))
            free["P"][slot] = t
            return t

        def expp(u):
            qa, ka = QA[u.buf], KA[u.buf]
            pend = None

            def close(g, t):
                if u.kind == 0:
                    a = op(V, lambda e: nc.vector.transpose(
                        O[:, :].rearrange("p (r d) -> p r d", r=16), PV[:, :].rearrange("p (n r) -> p r n", r=16)),
                        [t, free["O"]])
                    free["PV"] = a
                    yield
                    od = O[:, :].rearrange("p (r d) -> p r d", r=16)
                    r = op(V, lambda e: nc.vector.reciprocal(rc0[:, :], od[:, :, 16]), [a, free["on"]])
                    a = op(V, lambda e: nc.vector.tensor_tensor(
                        on0, od[:, :, 0:16], rc0[:, :].rearrange("p (r o) -> p r o", o=1).to_broadcast([128, 16, 16]),
                        ALU.mult), [r])
                    free["O"] = a
                    tgt = X[:, 4 * u.b + 2 * u.c + g, :].rearrange("p (r d) -> p r d", r=16)
                    free["on"] = op(G, lambda e: nc.gpsimd.tensor_tensor(tgt, tgt, on0, ALU.add), [a, xadd[u.b]])
                    return
                a = op(A, lambda e: nc.scalar.copy(O[:, :], PV[:, :]), [t, free["O"]])
                free["PV"] = a
                yield
                M, mi = mbank()
                for k in range(4):
                    t = op(T, lambda e, M=M, k=k: nc.tensor.transpose(
                        M[:, k * 128:(k + 1) * 128], O[:, k * 128:(k + 1) * 128], ident[:, :]),
                        [a, free["M"][mi], mident], mark=(k == 3))
                free["O"] = t
                mo = M[:, :].rearrange("p (k j d) -> p k j d", k=4, j=4)
                r = op(V, lambda e: nc.vector.reciprocal(rc[:, :, :], mo[:, :, :, 16]), [t, free["on"]])
                rb = rc[:, :, :].rearrange("p k (j o) -> p k j o", o=1).to_broadcast([128, 4, 4, 16])
                done1(u, g, mi, mo[:, :, :, 0:16], rb, r)

            for g in range(2):
                for kb in range(4):
                    n0 = 128 * kb if u.causal else 0
                    n = 512 - n0
                    slot = cnt["p"] % 2
                    cnt["p"] += 1
                    ex = None
                    per = {512: 1, 384: 1, 256: 2, 128: 4}[n]
                    for j0 in range(0, 4, per):
                        s = cnt["s2"] % 2
                        cnt["s2"] += 1
                        bank = S2[s][:, 0:per * n].rearrange("p (j n) -> p j n", j=per)
                        for z in range(per):
                            t = op(T, lambda e, bank=bank, z=z, h=4 * g + j0 + z, n0=n0, kb=kb: nc.tensor.matmul(
                                bank[:, z, :], ka[0:99, h, kb * 128:(kb + 1) * 128], qa[0:99, h, n0:512],
                                start=True, stop=not u.causal),
                                [u.qready, u.kready, u.mready[g], free["S2"][s], mones[0]],
                                mark=(z == per - 1 and not u.causal))
                            if u.causal:
                                t = op(T, lambda e, bank=bank, z=z: nc.tensor.matmul(
                                    bank[:, z, 0:128], identb[:, :], maskk[:, :], start=False, stop=True),
                                    [mconst], mark=(z == per - 1))
                        ex = op(A, lambda e, bank=bank, j0=j0, per=per, n=n, slot=slot: nc.scalar.activation(
                            P[slot][:, j0:j0 + per, 0:n], bank, ACT.Exp,
                            scale=0.25 if u.causal else 1.0), [t, free["P"][slot]])
                        free["S2"][s] = ex
                        if pend is not None and j0 + per >= 2:
                            t = pv(*pend)
                            last = pend
                            pend = None
                            if last[2] == 3:
                                yield
                                yield from close(last[1], t)
                        yield
                    pend = (u, g, kb, slot, ex)
            t = pv(*pend)
            free["QA"][u.buf] = [t]
            free["KA"][u.buf] = [t]
            vt, key = vtile(u)
            if u.kind != 1:
                vfree[key] = t
            yield
            yield from close(1, t)

        def merge(lanes):
            live = [True] * len(lanes)
            k = 0
            while any(live):
                for z, (g, every) in enumerate(lanes):
                    if live[z] and k % every == 0:
                        try:
                            next(g)
                        except StopIteration:
                            live[z] = False
                k += 1

        def run(units, first, pre, extra):
            def gen(f, i):
                return f(units[i]) if 0 <= i < len(units) else iter(())
            for i in range(first, len(units) + 1):
                every = 3 if units[0].kind == 0 else 2
                lanes = [(gen(expp, i), 1), (gen(maxp, i + 1), 1), (gen(pre, i + 2), every)]
                merge(lanes + extra(i, gen))

        mones = [None]

        def init_attention(after, vt):
            for i in range(3):
                op(V, lambda e, i=i: nc.vector.memset(KA[i][96:99, :, :], 1.0), after)
            for t in vt:
                op(V, lambda e, t=t: nc.vector.memset(t[:, :, :, 16:17], 1.0), after)
            w = op(V, lambda e: nc.vector.memset(PV[:, :], 0.0), after)
            m = op(G, lambda e: nc.gpsimd.memset(on[:, 0:1], 0.0), [Q.last[G], w])
            mones[0] = m

        def barrier():
            return [Q.last[e] for e in (T, V, A, G)] + [(s, Q.count[s]) for s in Q.sems if s.startswith("d_")]

        B2 = R3[0:3, 0:1024].bitcast(BF).rearrange("p (e n) -> p e n", e=NE)
        cTv = cT[:, :, :].rearrange("p a n -> p (a n)")
        xnv = xnb[:, :, :].rearrange("p a n -> p (a n)")

        def room(i):
            w = cTv[:, i * 256:(i + 1) * 256] if i < 4 else xnv[:, (i - 4) * 256:(i - 3) * 256]
            return w.rearrange("p (t e) -> p t e", e=NE)

        B1T = sb("B1T", [128, NE, 8])
        bd2 = nc.dram_tensor("bd2", (3, 2048), BF).ap()
        bt = sb("bt", [128, 16])
        br = sb("br", [128, 16])
        bs = sb("bs", [128, 3, 16], BF)
        ones3 = sb("ones3", [3, 128], BF)
        on3 = op(V, lambda e: nc.vector.memset(ones3[:, :], 1.0))
        mb1 = dma("d_b1", lambda e: e.dma_start(B1T[:, :, :], b1))

        tri = sb("tri", [128, 128])
        onesf = sb("onesf", [128, 128])
        io8 = sb("io8", [128, NE])
        ioT = sb("ioT", [128, TM])
        tok = sb("tok", [128, NT], I32)
        z39 = sb("z39", [128, TM], I32)
        g1 = op(G, lambda e: nc.gpsimd.memset(tri[:, :], 0.0))
        op(G, lambda e: nc.gpsimd.memset(onesf[:, :], 1.0))
        op(G, lambda e: nc.gpsimd.affine_select(out=tri[:, :], in_=tri[:, :], compare_op=ALU.is_ge, fill=1.0,
                                                base=0, pattern=[[-1, 128]], channel_multiplier=1), [g1])
        op(G, lambda e: nc.gpsimd.iota(io8[:, :], pattern=[[1, NE]], base=0, channel_multiplier=0,
                                       allow_small_or_imprecise_dtypes=True))
        op(G, lambda e: nc.gpsimd.iota(ioT[:, :], pattern=[[1, TM]], base=0, channel_multiplier=0,
                                       allow_small_or_imprecise_dtypes=True))
        op(G, lambda e: nc.gpsimd.iota(tok[:, :], pattern=[[128, NT]], base=0, channel_multiplier=1))
        mg = op(G, lambda e: nc.gpsimd.memset(z39[:, :], 0))
        mzid = dma("d_z", lambda e: e.dma_start(idd.rearrange("(p t) o -> p (t o)", p=128), z39[:, :]), [mg])

        def bc(ap, shape):
            return ap.to_broadcast(shape)

        amax = sb("amax", [128, NT])
        alpha = sb("alpha", [128, NT])
        eq = room(0)
        oh = room(1)
        emin = sb("emin", [128, NT])
        wi = room(2)
        tt = [room(3), room(4)]
        tot = room(5)
        te_ = [sb("tea", [128, NE]), sb("teb", [128, NE])]
        tl = sb("tl", [128, NE])
        tli = sb("tli", [128, NE], I32)
        slotf = sb("slotf", [128, NT])
        sloti = sb("sloti", [128, NT], I32)
        lo7 = sb("lo7", [128, NT], I32)
        hi7 = sb("hi7", [128, NT], I32)
        lof = sb("lof", [128, NT])
        hif = sb("hif", [128, NT])
        sidx = sb("sidx", [128, NT], I32)
        tcm = xnv[:, 512:512 + TM * NE].rearrange("p (t e) -> p t e", e=NE)
        texf = sb("texf", [128, TM])
        texp = sb("texp", [128, TM], I32)
        gidx = sb("gidx", [128, TM], I32)

        def v(f, *after):
            return op(V, f, list(after))

        rt = {}

        def route():
            start = [Q.last[T], Q.last[G], free["h0b"], *free["xnb"]]
            s8 = [128, NT, NE]
            m = v(lambda e: nc.vector.tensor_reduce(amax[:, :], AF[:, :, :], AX.X, ALU.max), afready[-1], *start)
            yield
            ma = op(A, lambda e: nc.scalar.activation(alpha[:, :], amax[:, :], ACT.Exp, scale=-1.0), [m])
            yield
            ma = v(lambda e: nc.vector.tensor_scalar(alpha[:, :], alpha[:, :], 1.0, None, ALU.add), ma)
            yield
            malpha = v(lambda e: nc.vector.reciprocal(alpha[:, :], alpha[:, :]), ma)
            yield
            m = v(lambda e: nc.vector.tensor_tensor(eq[:, :, :], AF[:, :, :],
                  bc(amax[:, :].rearrange("p (t o) -> p t o", o=1), s8), ALU.is_ge), m)
            yield
            m = v(lambda e: nc.vector.scalar_tensor_tensor(out=eq[:, :, :], in0=eq[:, :, :], scalar=-8.0,
                  in1=bc(io8[:, :].rearrange("p (o e) -> p o e", o=1), s8), op0=ALU.mult, op1=ALU.add), m, mg)
            yield
            m = v(lambda e: nc.vector.tensor_reduce(emin[:, :], eq[:, :, :], AX.X, ALU.min), m)
            yield
            m = v(lambda e: nc.vector.tensor_tensor(oh[:, :, :], eq[:, :, :],
                  bc(emin[:, :].rearrange("p (t o) -> p t o", o=1), s8), ALU.is_equal), m)
            yield
            M, mi = mbank()
            ohf = oh[:, :, :].rearrange("p t e -> p (t e)")
            op(T, lambda e, M=M: nc.tensor.matmul(M[:, 0:256], tri[:, :], ohf, start=True, stop=True), [m, mg, free["M"][mi]], mark=False)
            t = op(T, lambda e, M=M: nc.tensor.matmul(M[:, 256:512], onesf[:, :], ohf, start=True, stop=True))
            m1 = v(lambda e, M=M: nc.vector.tensor_copy(wi[:, :, :].rearrange("p t e -> p (t e)"), M[:, 0:256]), t)
            m = v(lambda e, M=M: nc.vector.tensor_copy(tot[:, :, :].rearrange("p t e -> p (t e)"), M[:, 256:512]), t)
            free["M"][mi] = m
            yield
            src = tot
            for i, s in enumerate((1, 2, 4, 8, 16)):
                dst = tt[i % 2]
                m2 = v(lambda e, src=src, dst=dst, s=s: nc.vector.tensor_copy(dst[:, 0:s, :], src[:, 0:s, :]), m)
                yield
                m = v(lambda e, src=src, dst=dst, s=s: nc.vector.tensor_tensor(
                    dst[:, s:NT, :], src[:, s:NT, :], src[:, 0:NT - s, :], ALU.add), m2)
                yield
                src = dst
            inc = src
            m = v(lambda e: nc.vector.tensor_scalar(tl[:, :], inc[:, NT - 1, :], 127.0, None, ALU.add), m)
            yield
            m = v(lambda e: nc.vector.tensor_copy(tli[:, :], tl[:, :]), m)
            yield
            m = v(lambda e: nc.vector.tensor_scalar(tli[:, :], tli[:, :], 7, None, ALU.arith_shift_right), m)
            yield
            m = v(lambda e: nc.vector.tensor_copy(tl[:, :], tli[:, :]), m)
            yield
            src = tl
            for i, s in enumerate((1, 2, 4)):
                dst = te_[i % 2]
                m2 = v(lambda e, src=src, dst=dst, s=s: nc.vector.tensor_copy(dst[:, 0:s], src[:, 0:s]), m)
                yield
                m = v(lambda e, src=src, dst=dst, s=s: nc.vector.tensor_tensor(
                    dst[:, s:NE], src[:, s:NE], src[:, 0:NE - s], ALU.add), m2)
                yield
                src = dst
            ends, base = te_[0], te_[1]
            m2 = v(lambda e: nc.vector.tensor_tensor(base[:, :], ends[:, :], tl[:, :], ALU.subtract), m)
            yield
            m2 = v(lambda e: nc.vector.tensor_scalar(base[:, :], base[:, :], 128.0, None, ALU.mult), m2)
            yield
            m3 = v(lambda e: nc.vector.tensor_tensor(wi[:, :, :], wi[:, :, :], inc[:, :, :], ALU.add), m2, m1)
            yield
            m3 = v(lambda e: nc.vector.tensor_tensor(wi[:, :, :], wi[:, :, :], tot[:, :, :], ALU.subtract), m3)
            yield
            m3 = v(lambda e: nc.vector.tensor_tensor(wi[:, :, :], wi[:, :, :],
                   bc(base[:, :].rearrange("p (o e) -> p o e", o=1), s8), ALU.add), m3)
            yield
            m3 = v(lambda e: nc.vector.tensor_tensor(wi[:, :, :], wi[:, :, :], oh[:, :, :], ALU.mult), m3)
            yield
            m3 = v(lambda e: nc.vector.tensor_reduce(slotf[:, :], wi[:, :, :], AX.X, ALU.add), m3)
            yield
            m3 = v(lambda e: nc.vector.tensor_copy(sloti[:, :], slotf[:, :]), m3)
            yield
            mslot = m3
            m3 = v(lambda e: nc.vector.tensor_scalar(lo7[:, :], sloti[:, :], 127, None, ALU.bitwise_and), m3)
            yield
            m3 = v(lambda e: nc.vector.tensor_scalar(hi7[:, :], sloti[:, :], 7, None, ALU.arith_shift_right), m3)
            yield
            m3 = v(lambda e: nc.vector.tensor_copy(lof[:, :], lo7[:, :]), m3)
            yield
            m3 = v(lambda e: nc.vector.tensor_copy(hif[:, :], hi7[:, :]), m3)
            yield
            m3 = v(lambda e: nc.vector.scalar_tensor_tensor(out=lof[:, :], in0=lof[:, :], scalar=float(TM), in1=hif[:, :],
                   op0=ALU.mult, op1=ALU.add), m3)
            yield
            midx = v(lambda e: nc.vector.tensor_copy(sidx[:, :], lof[:, :]), m3)
            yield
            s39 = [128, TM, NE]
            m = v(lambda e: nc.vector.tensor_tensor(tcm[:, :, :], bc(ends[:, :].rearrange("p (o e) -> p o e", o=1), s39),
                  bc(ioT[:, :].rearrange("p (t o) -> p t o", o=1), s39), ALU.is_le), m)
            yield
            m = v(lambda e: nc.vector.tensor_reduce(texf[:, :], tcm[:, :, :], AX.X, ALU.add), m)
            yield
            m = v(lambda e: nc.vector.tensor_scalar(texf[:, :], texf[:, :], float(NE - 1), None, ALU.min), m)
            yield
            mtex = v(lambda e: nc.vector.tensor_copy(texp[:, :], texf[:, :]), m)
            rt.update(alpha=malpha, slot=mslot, tex=mtex, idx=midx)

        def scatter():
            m = None
            for t in range(NT):
                m = dma("d_sc", lambda e, t=t: nc.gpsimd.indirect_dma_start(
                    idd, bass.IndirectOffsetOnAxis(ap=sidx[:, t:t + 1].bitcast(U32), axis=0), tok[:, t:t + 1], None),
                    [rt["idx"], mzid, mg], eng=G)
                yield
            mgi = dma("d_gi", lambda e: e.dma_start(gidx[:, :], idd.rearrange("(p t) o -> p (t o)", p=128)), [m])
            rt["gi"] = mgi
            gather(0)
            gather(1)

        spf = spl[:, :, :, :].rearrange("p a b n -> p (a b n)").bitcast(F32)
        hs = [spf[:, 1024:1280], spf[:, 1280:1536], on[:, :]]
        hT = [cTv[:, i * 256:(i + 1) * 256].rearrange("p (c n) -> p c n", c=2) for i in range(2)]
        AA = [xnb[:, :, :].rearrange("p a n -> p (a n)"), xTb[:, :, :].rearrange("p a n -> p (a n)")]
        AT = spf[:, 0:1024].rearrange("p (k n) -> p k n", k=8)
        Y = [cTv[:, 512 + i * 256:768 + i * 256] for i in range(2)]
        ef = {"hs": [None] * 3, "hT": [None] * 2, "AA": [None] * 2, "AT": [None, None], "Y": [None] * 2,
              "B": [None] * 2, "S1": [None, None], "PV": None}
        gath = {}
        bar_ = []
        regs = {}

        def gather(t):
            gath[t] = dma(f"d_hs{t % 3}", lambda e: nc.gpsimd.indirect_dma_start(
                hs[t % 3], None, h0d, bass.IndirectOffsetOnAxis(ap=gidx[:, t:t + 1].bitcast(U32), axis=0)),
                [rt["gi"], ef["hs"][t % 3], *(free["spl"] if t < 2 else bar_)], eng=G)

        def extra0(i, gen):
            if i == -1:
                init_attention([], V0)
            lanes = [(first, 6) if i == -2 else (gen(norm0, i + 3), 1)]
            if i % 2 and (i + 5) // 2 < NB and i < 12:
                load_x((i + 5) // 2)
            if 0 <= i < NE:
                mw1[:] = [dma("d_w1", lambda e, i=i: e.dma_start(W1[:, i, :], w1[:, i, :]))]
            if i == NE:
                lanes.append((bias2(), 1))
            if i == 13:
                lanes.append((route(), 1))
            if i == 14:
                lanes.append((scatter(), 1))
                load_w2((0, 1), free["QA"][1])
            if i == 15:
                load_w2((2, 3), free["QA"][2])
            if i == 16:
                load_w2((4, 5, 6, 7), [*free["QA"][0], *free["P"]])
            return lanes

        mw2 = []
        mb2 = []

        def bias2():
            m = dma("d_b", lambda e: e.dma_start(bt[:, :], b2.rearrange("(p n) -> p n", p=128)))
            yield
            yield
            m = op(V, lambda e: nc.vector.tensor_copy(bs[:, 0, :], bt[:, :]), [m])
            m = op(V, lambda e: nc.vector.tensor_tensor(br[:, :], bt[:, :], bs[:, 0, :], ALU.subtract), [m])
            m = op(V, lambda e: nc.vector.tensor_copy(bs[:, 1, :], br[:, :]), [m])
            m = op(V, lambda e: nc.vector.tensor_tensor(bs[:, 2, :], br[:, :], bs[:, 1, :], ALU.subtract), [m])
            m = dma("d_b", lambda e: e.dma_start(bd2.rearrange("s (p n) -> p s n", p=128), bs[:, :, :]), [m])
            mb2.append(m)
            yield

        def load_w2(experts, after):
            for i in experts:
                mw2[:] = [dma("d_w2", lambda e, i=i: e.dma_start(W2[:, i, :], w2[:, i, :]), after)]

        units = [Unit(n, 0, n // 2, n % 2) for n in range(16)]
        first = norm0(units[0])
        while 0 not in xnm:
            next(first)
        run(units, -2, pre0, extra0)

        bar = barrier()
        bar_ += bar
        mbias = dma("d_b2", lambda e: e.dma_start(B2.rearrange("s e n -> s (e n)"), bd2), [*mb2, *bar])

        def expert(eng, t):
            def f(e):
                regs[(eng, t)] = e.value_load(texp[0:1, t:t + 1], min_val=0, max_val=NE - 1)
            return f

        aready = {}

        banks = [S2[0], S2[1], MB[1], S1[2]]

        def head(t):
            i = t % 2
            for eng in (T, V):
                Q._wait(eng, [rt["tex"]])
                Q.items[eng].append(("op", expert(eng, t), None, 0))
            M, mi = MB[0], 0
            for c in range(2):
                x_ = op(T, lambda e, M=M, c=c: nc.tensor.transpose(M[:, c * 128:(c + 1) * 128],
                        hs[t % 3][:, c * 128:(c + 1) * 128], ident[:, :]), [gath[t], free["M"][mi]], mark=(c == 1))
            ef["hs"][t % 3] = x_
            for c in range(2):
                y_ = op(V, lambda e, M=M, c=c: nc.vector.tensor_scalar(
                    hT[i][:, c, :], M[:, c * 128:(c + 1) * 128],
                    GB[:, bass.ds(regs[(V, t)], 1), c:c + 1], GB[:, bass.ds(regs[(V, t)], 1), 2 + c:3 + c],
                    ALU.mult, ALU.add), [x_, ef["hT"][i], *bar])
            free["M"][mi] = y_
            hready[t] = y_

        def up(t):
            i = t % 2
            for f in range(2):
                bank = banks[2 * i + f]
                for c in range(2):
                    z_ = op(T, lambda e, f=f, c=c, bank=bank: nc.tensor.matmul(
                        bank[:, :], hT[i][:, c, :],
                        W1[:, bass.ds(regs[(T, t)], 1), c * 1024 + f * 512:c * 1024 + f * 512 + 512],
                        start=(c == 0), stop=(c == 1)), [hready[t], ef["B"][i], *mw1], mark=(c == 1))
                a_ = op(A, lambda e, f=f, bank=bank: nc.scalar.copy(AA[i][:, f * 512:(f + 1) * 512], bank[:, :]),
                        [z_, ef["AA"][i]])
            ef["hT"][i] = z_
            ef["B"][i] = a_
            aready[t] = a_

        def turn(t):
            i = t % 2
            for f in range(2):
                for k in range(4):
                    t_ = op(T, lambda e, f=f, k=k: nc.tensor.transpose(
                        S1[f][:, k * 128:(k + 1) * 128], AA[i][:, (4 * f + k) * 128:(4 * f + k + 1) * 128], ident[:, :]),
                        [aready[t], ef["S1"][f]], mark=(k == 3))
                for k in range(4):
                    cp[f] = op(V, lambda e, f=f, k=k: nc.vector.tensor_scalar(
                        AT[:, 4 * f + k, :], S1[f][:, k * 128:(k + 1) * 128],
                        B1T[:, bass.ds(regs[(V, t)], 1), 4 * f + k:4 * f + k + 1], 0.0, ALU.add, ALU.max),
                        [t_, ef["AT"][f], mb1])
                ef["S1"][f] = cp[f]
            ef["AA"][i] = t_

        def down(t):
            i = t % 2
            for k in range(8):
                t_ = op(T, lambda e, k=k: nc.tensor.matmul(
                    PV[:, 0:256], AT[:, k, :], W2[:, bass.ds(regs[(T, t)], 1), k * 256:k * 256 + 256],
                    start=(k == 0), stop=False), [cp[k // 4], ef["PV"], *mw2], mark=(k in (3, 7)))
                if k in (3, 7):
                    ef["AT"][k // 4] = t_
            t_ = op(T, lambda e: nc.tensor.matmul(
                PV[:, 0:256], ones3[:, :], B2[:, bass.ds(regs[(T, t)], 1), :], start=False, stop=True), [mbias, on3])
            a_ = op(A, lambda e: nc.scalar.copy(Y[i], PV[:, 0:256]), [t_, ef["Y"][i]])
            ef["PV"] = a_
            ef["Y"][i] = dma(f"d_y{i}", lambda e: e.dma_start(ysd[t * 128:(t + 1) * 128, :], Y[i]), [a_])

        hready = {}
        cp = [None, None]
        head(0)
        gather(2)
        up(0)
        head(1)
        for t in range(TM):
            turn(t)
            if t + 3 < TM:
                gather(t + 3)
            if t + 1 < TM:
                up(t + 1)
            if t + 2 < TM:
                head(t + 2)
            down(t)

        bar = barrier()
        gy = [R2[:, 14336 + i * 256:14592 + i * 256] for i in range(8)]
        gyf = [None] * 8
        WQ1 = WQ

        def loadl(view, src):
            return dma("d_l1", lambda e: e.dma_start(view, src), bar)

        CW = R1[:, 12544:14080].rearrange("p (a n) -> p a n", a=6)
        OB = R3[:, 512:768]
        FB = R3[:, 768:1024]
        CB = sb("CB", [128, 2])
        U1 = R3[:, 1024:1280].rearrange("p (c n) -> p c n", c=2)
        r2c = R2[:, :].bitcast(BF)
        V1f, V1r = R2[:, 0:1024], R2[:, 1024:2048]
        V1a, V1b, V1c = r2c[:, 4096:5120], r2c[:, 5120:6144], r2c[:, 6144:7168]
        VA, VB = r2c[:, 16384:17408], r2c[:, 17408:18432]
        U2 = R2[:, 9216:9728].rearrange("p (k n) -> p k n", k=8)
        V2 = R2[:, 9728:9984]
        Pr = R2[:, 9984:10496]
        PT = [r2c[:, 20992 + i * 1536:22528 + i * 1536].rearrange("p (a n) -> p a n", a=3) for i in range(2)]
        QS = [R2[:, 12032 + i * 512:12544 + i * 512] for i in range(2)]
        HT = [R1[:, 14080 + i * 512:14592 + i * 512] for i in range(4)]
        FBI = sb("FBI", [128, 8])
        loadl(U1, u1)
        loadl(V1f[0:64], v1)
        loadl(V1f[64:128], v1)
        loadl(U2, u2)
        loadl(V2[0:64], v2)
        loadl(V2[64:128], v2)
        loadl(OB, outb.rearrange("(o n) -> o n", o=1).to_broadcast([128, 256]))
        loadl(FB, fb2.rearrange("(o n) -> o n", o=1).to_broadcast([128, 256]))
        ml1 = loadl(FBI[:], fb1)

        def loadm(view, src):
            return dma("d_l2", lambda e: e.dma_start(view, src), bar)

        loadm(WQ1[:], wqkv1)
        loadm(BQK[:], bqk1)
        loadm(BV[:], bv1.rearrange("(o n) -> o n", o=1).to_broadcast([128, 256]))
        loadm(CW, convw)
        loadm(OW, outw)
        ml2 = loadm(CB[:], convb)

        def gathers(b):
            for k in range(4):
                t = 4 * b + k
                gm[t] = dma(f"d_gy{t % 8}", lambda e, t=t: nc.gpsimd.indirect_dma_start(
                    gy[t % 8], None, ysd, bass.IndirectOffsetOnAxis(ap=sloti[:, t:t + 1].bitcast(U32), axis=0)),
                    [gyf[t % 8], rt["slot"], *bar], eng=G)
                yield

        gm = {}
        XN = [xnb, R2[:, 13056:14080].rearrange("p (k n) -> p k n", k=4)]
        xnf = [bar, bar]
        ff = {"PT": [None] * 2, "HT": [None] * 4, "QS": [None] * 2, "hb": [None] * 3, "qb": [None, None],
              "Pr": None}
        pready = {}
        def joined(b):
            a = None
            for k in range(4):
                t = 4 * b + k
                a = v(lambda e, t=t: nc.vector.scalar_tensor_tensor(
                    out=X[:, t, :], in0=gy[t % 8], scalar=alpha[:, t:t + 1], in1=X[:, t, :], op0=ALU.mult, op1=ALU.add),
                    gm[t], rt["alpha"], *bar)
                gyf[t % 8] = a
                yield
            yield from norm(b, a, XN[b % 2], lambda: xnf[b % 2])

        def near(b):
            xm = None
            for xm in transposes(XN[b % 2], XT[:, :, 512 * b:512 * b + 512], xnm[b], None):
                yield
            xnf[b % 2] = [Q.last[T]]
            xt_ready[("l1", b)] = xm
            p = PT[b % 2]
            M, mi = mbank()
            for cc in range(2):
                t = op(T, lambda e, M=M, cc=cc, b=b: nc.tensor.matmul(
                    M[:, :], U1[:, cc, :], XT[:, cc, 512 * b:512 * b + 512], start=(cc == 0), stop=(cc == 1)),
                    [xm, free["M"][mi], ml1], mark=(cc == 1))
            a1 = op(A, lambda e, M=M: nc.scalar.copy(p[:, 0, :], M[:, :]), [t, ff["PT"][b % 2]])
            a2 = v(lambda e, M=M: nc.vector.tensor_tensor(Pr, M[:, :], p[:, 0, :], ALU.subtract), a1, ff["Pr"])
            free["M"][mi] = a2
            yield
            a3 = v(lambda e: nc.vector.tensor_copy(p[:, 1, :], Pr), a2)
            yield
            a4 = v(lambda e: nc.vector.tensor_tensor(p[0:64, 2, :], Pr[0:64], p[0:64, 1, :], ALU.subtract), a3)
            a5 = op(A, lambda e: nc.scalar.copy(p[64:128, 2, :], p[64:128, 0, :]), [a1])
            ff["Pr"] = a4
            pready[b] = [a4, a5]

        hc = [0]

        def far(b):
            p = PT[b % 2]
            qb = (PV, S1[0])[b % 2]

            def u2mm(j):
                q = None
                for f, (ready, hi) in j:
                    h = f % 2
                    q = op(T, lambda e, f=f, h=h, hi=hi: nc.tensor.matmul(
                        qb[64 * h:64 * h + 64, :], U2[:, f, :], HT[hi], start=(f < 2), stop=(f >= 6),
                        skip_group_check=True), [ready, ff["qb"][b % 2]])
                    ff["HT"][hi] = q
                return q

            pend = []
            for f in range(8):
                bi, hi = hc[0] % 3, hc[0] % 4
                hc[0] += 1
                hb = (S2[0], S2[1], S1[1])[bi]
                for z, (vv, pp) in enumerate(((VA, 0), (VA, 1), (VB, 2))):
                    t = op(T, lambda e, z=z, vv=vv, pp=pp, f=f, hb=hb: nc.tensor.matmul(
                        hb[:, :], vv[:, f * 128:(f + 1) * 128], p[:, pp, :], start=(z == 0), stop=(z == 2)),
                        [*pready[b], mva, ff["hb"][bi]], mark=(z == 2))
                g_ = op(A, lambda e, f=f, hb=hb, hi=hi: nc.scalar.activation(
                    HT[hi], hb[:, :], ACT.Gelu_apprx_tanh, bias=FBI[:, f:f + 1]), [t, ff["HT"][hi]])
                ff["hb"][bi] = g_
                pend.append((f, (g_, hi)))
                if f % 2 == 1 and f >= 3:
                    u2mm(pend[:2])
                    pend = pend[2:]
                yield
            ff["PT"][b % 2] = t
            rest[b] = (u2mm, pend)

        rest = {}

        def tail(b):
            u2mm, pend = rest[b]
            qb = (PV, S1[0])[b % 2]
            qm = u2mm(pend)
            a = op(A, lambda e: nc.scalar.copy(QS[b % 2], qb[:, :]), [qm, ff["QS"][b % 2]])
            ff["qb"][b % 2] = a
            yield
            yield
            for h in range(2):
                yb, mi = mbank()
                for k in range(2):
                    t = op(T, lambda e, h=h, k=k, yb=yb: nc.tensor.matmul(
                        yb[:, k * 256:(k + 1) * 256], QS[b % 2][:, (2 * h + k) * 128:(2 * h + k + 1) * 128], V2,
                        start=True, stop=True), [a, free["M"][mi]], mark=(k == 1))
                tg = X[:, 4 * b + 2 * h:4 * b + 2 * h + 2, :]
                y_ = v(lambda e, tg=tg, yb=yb: nc.vector.tensor_tensor(
                    tg, tg, yb[:, :].rearrange("p (k n) -> p k n", k=2), ALU.add), t, xnm[b])
                free["M"][mi] = y_
                yield
            ff["QS"][b % 2] = t
            tb = X[:, 4 * b:4 * b + 4, :]
            xadd[b] = op(G, lambda e: nc.gpsimd.tensor_tensor(
                tb, tb, OB.rearrange("p (o n) -> p o n", o=1).to_broadcast([128, 4, 256]), ALU.add), [y_, mbb])

        def parts():
            m = v(lambda e: nc.vector.tensor_copy(V1a, V1f), ml1)
            m = v(lambda e: nc.vector.tensor_tensor(V1r, V1f, V1a, ALU.subtract), m)
            m = v(lambda e: nc.vector.tensor_copy(V1b, V1r), m)
            m = v(lambda e: nc.vector.tensor_tensor(V1c, V1r, V1b, ALU.subtract), m)
            v(lambda e: nc.vector.tensor_copy(VA[0:64], V1a[0:64]), m)
            v(lambda e: nc.vector.tensor_copy(VA[64:128], V1b[64:128]), m)
            v(lambda e: nc.vector.tensor_copy(VB[0:64], V1a[0:64]), m)
            return v(lambda e: nc.vector.tensor_copy(VB[64:128], V1c[64:128]), m)

        merge([(gathers(0), 1)])
        merge([(gathers(1), 1), (joined(0), 1)])
        mva = parts()
        mbb = op(G, lambda e: nc.gpsimd.tensor_tensor(OB, OB, FB, ALU.add), [ml1])

        CTX = [R1[:, 14080:15104].rearrange("p (k n) -> p k n", k=4),
               R1[:, 15104:16128].rearrange("p (k n) -> p k n", k=4), xnb]
        c2T = xTb
        for t in V1S:
            op(V, lambda e, t=t: nc.vector.memset(t[:, :, :, 16:17], 1.0), bar)
        for k in (0, 513):
            mpad = op(V, lambda e, k=k: nc.vector.memset(cT[:, :, k:k + 1], 0.0))
        vfree.clear()

        ctxm = {}
        ctxf = [None] * 3

        def cslot(kind, b):
            return b % 2 if kind == 1 else 2

        cTf = [None]

        def pre1(u):
            b, c = u.b, u.c
            if u.kind == 1:
                yield from project(u, XT[:, :, 512 * b:512 * b + 512], WQ1, BQK, BV, ml2, xt_ready[("l1", b)])
                return
            if c == 0:
                cx = CTX[cslot(1, b)]
                for m in transposes(cx, cT[:, :, 1:513], ctxm[(1, b)], cTf[0]):
                    yield
                ctxf[cslot(1, b)] = Q.last[T]
                ctxT_ready[b] = m
            M, mi = mbank()
            for i in range(6):
                k, cc = i // 2, i % 2
                t = op(T, lambda e, M=M, i=i, k=k, cc=cc: nc.tensor.matmul(
                    M[:, :], CW[:, i, c * 128:c * 128 + 128], cT[:, cc, k:k + 512], start=(i == 0), stop=(i == 5)),
                    [ctxT_ready[b], mpad, ml2, free["M"][mi]], mark=(i == 5))
            cTf[0] = t
            d = split_out(M, mi, 0, CB[:, c:c + 1], t, "d_sp0", qs[u.n], ml2)
            u.qready = fan(QA[u.buf], qs[u.n], QP, f"d_f0{u.buf}", [d, *free["QA"][u.buf]])
            yield
            u.kready = fan(KA[u.buf], kdram[(1, b, c)], KP, f"d_f1{u.buf}", [*free["KA"][u.buf]])
            u.vready = vready[(1, b, c)]
            yield

        def done1(u, g, mi, vals, rb, r):
            key = (u.kind, u.b)
            s = cslot(*key)
            lo = u.c * 128 + g * 64
            tg = CTX[s][:, :, lo:lo + 64].rearrange("p k (j d) -> p k j d", j=4)
            a = op(V, lambda e: nc.vector.tensor_tensor(tg, vals, rb, ALU.mult), [r, ctxf[s]])
            free["M"][mi] = a
            free["on"] = a
            ctxm[key] = a

        def fin1(u):
            if u.kind != 2 or u.c != 1:
                return
            b = u.b
            cx = CTX[cslot(2, b)]
            for m in transposes(cx, c2T, ctxm[(2, b)], free["xTb"]):
                yield
            ctxf[cslot(2, b)] = Q.last[T]
            for h in range(2):
                M, mi = mbank()
                for k in range(2):
                    for cc in range(2):
                        t = op(T, lambda e, M=M, h=h, k=k, cc=cc: nc.tensor.matmul(
                            M[:, k * 256:(k + 1) * 256], c2T[:, cc, (2 * h + k) * 128:(2 * h + k + 1) * 128],
                            OW[:, cc, :], start=(cc == 0), stop=(cc == 1)), [m, free["M"][mi], ml2], mark=(k == 1 and cc == 1))
                tg = X[:, 4 * b + 2 * h:4 * b + 2 * h + 2, :]
                y_ = v(lambda e, M=M, tg=tg: nc.vector.tensor_tensor(
                    tg, tg, M[:, :].rearrange("p (k n) -> p k n", k=2), ALU.add), t, xadd[b])
                free["M"][mi] = y_
                yield
            free["xTb"] = t
            dma("d_out", lambda e: e.dma_start(ov[:, 4 * b:4 * b + 4, :], X[:, 4 * b:4 * b + 4, :]), [y_])

        order, a1, a2 = [], 0, 0
        while a2 < NB:
            if a1 < NB and a1 < a2 + 2:
                order += [(1, a1, 0), (1, a1, 1)]
                a1 += 1
            else:
                order += [(2, a2, 0), (2, a2, 1)]
                a2 += 1
        units = [Unit(n, kind, b, c) for n, (kind, b, c) in enumerate(order, 16)]
        mka_ = [None]

        def ones_rows(b):
            if b < 4:
                for i in (1, 2):
                    mka_[0] = v(lambda e, i=i: nc.vector.memset(KA[i][96:99, 2 * b:2 * b + 2, :], 1.0), mva)
                    yield

        for b in range(-1, NB - 2):
            lanes = [(far(b), 1)] if b >= 0 else []
            if b >= 1:
                lanes.append((tail(b - 1), 1))
            lanes.append((near(b + 1), 2))
            if b < 1:
                lanes.append((gathers(b + 3), 1))
            for z in {-1: (1,), 0: (2, 3)}.get(b, (b + 3,)):
                if z < NB:
                    lanes.append((joined(z), 1))
            if 0 <= b and b + 4 < NB:
                lanes.append((gathers(b + 4), 1))
            if b >= 0:
                lanes.append((ones_rows(b), 4))
            if b == NB - 3:
                mka = mka_[0]
                free["QA"] = [[], [mka], [mka]]
                free["KA"] = [[], [mka], [mka]]
            if b == NB - 3:
                lanes.append((pre1(units[0]), 3))
            merge(lanes)
        merge([(far(NB - 2), 1), (tail(NB - 3), 1), (near(NB - 1), 2), (pre1(units[1]), 3)])
        merge([(far(NB - 1), 1), (tail(NB - 2), 1)])

        def start1():
            yield from tail(NB - 1)
            bar = barrier()
            op(V, lambda e: nc.vector.memset(KA[0][96:99, :, :], 1.0), bar)
            w = op(V, lambda e: nc.vector.memset(PV[:, :], 0.0), bar)
            mones[0] = op(G, lambda e: nc.gpsimd.memset(on[:, 0:1], 0.0), [*bar, w])
            for key in ("PV", "O", "on", "xTb"):
                free[key] = mones[0]
            free["P"] = [mones[0]] * 2
            free["QA"][0] = [mones[0]]
            free["KA"][0] = [mones[0]]
            ctxf[:] = [mones[0]] * 3

        g1 = start1()
        next(g1)
        free["S1"] = [ff["qb"][1], ff["hb"][2], None]
        free["S2"] = ff["hb"][0:2]
        merge([(maxp(units[0]), 1), (g1, 1)])
        run(units, 0, pre1, lambda i, gen: [(gen(fin1, i - 1), 3)])

        ends_ = [(s, Q.count[s]) for s in Q.sems if s.startswith("d_")]
        Q._wait("sync", ends_)
        block = ctx.enter_context(nc.Block())
        Q.emit(block)


_ARGS = ["x", "wqkv0", "bqk0", "bv0", "cent", "gb", "w1", "b1", "w2", "b2", "wqkv1", "bqk1", "bv1", "convw", "convb",
         "outw", "outb", "u1", "v1", "fb1", "u2", "v2", "fb2"]


def kernel(**inputs):
    import numpy as np
    import concourse.bacc as bacc
    from concourse.bass_utils import run_bass_kernel_spmd

    i = {k: np.asarray(v) for k, v in inputs.items()}

    def rows(w):
        return w.reshape(2, 128, -1).transpose(1, 0, 2)

    g, b = i["L0_ffn_ln_g"].reshape(8, 2, 128), i["L0_ffn_ln_b"].reshape(8, 2, 128)
    a = {
        "x": i["L0_attn_x"].reshape(4096, 256),
        "wqkv0": rows(i["L0_attn_W_qkv"]),
        "bqk0": i["L0_attn_b_qkv"][0:512].reshape(4, 128).T,
        "bv0": i["L0_attn_b_qkv"][512:768],
        "cent": rows(i["L0_ffn_centroids"].T),
        "gb": np.concatenate([g, b], axis=1).transpose(2, 0, 1),
        "w1": i["L0_ffn_w1"].transpose(0, 2, 1).reshape(8, 2, 128, 1024).transpose(2, 0, 1, 3).reshape(128, 8, 2048),
        "b1": i["L0_ffn_b1"].reshape(8, 8, 128).transpose(2, 0, 1),
        "w2": i["L0_ffn_w2"].transpose(0, 2, 1).reshape(8, 8, 128, 256).transpose(2, 0, 1, 3).reshape(128, 8, 2048),
        "b2": i["L0_ffn_b2"].reshape(-1),
        "wqkv1": rows(i["L1_attn_Wqkv_w"].T),
        "bqk1": i["L1_attn_Wqkv_b"][0:512].reshape(4, 128).T,
        "bv1": i["L1_attn_Wqkv_b"][512:768],
        "convw": i["L1_attn_conv_w"].transpose(2, 1, 0).reshape(3, 2, 128, 256).transpose(2, 0, 1, 3).reshape(128, 6, 256),
        "convb": i["L1_attn_conv_b"].reshape(2, 128).T,
        "outw": rows(i["L1_attn_out_w"].T),
        "outb": i["L1_attn_out_b"],
        "u1": np.concatenate([rows(i["L1_ffn_U1"])] * 2, axis=2),
        "v1": i["L1_ffn_V1"],
        "fb1": i["L1_ffn_b1"].reshape(8, 128).T,
        "u2": i["L1_ffn_U2"].reshape(8, 128, 64).transpose(1, 0, 2),
        "v2": i["L1_ffn_V2"],
        "fb2": i["L1_ffn_b2"],
    }
    nc = bacc.Bacc("TRN2", target_bir_lowering=False, num_devices=1)
    arrays, args = {}, []
    for name in _ARGS:
        arrays[f"in_{name}"] = np.ascontiguousarray(a[name])
        args.append(nc.dram_tensor(f"in_{name}", a[name].shape, F32, kind="ExternalInput").ap())
    args.append(nc.dram_tensor("out", (4096, 256), F32, kind="ExternalOutput").ap())
    build(nc, *args)
    r = run_bass_kernel_spmd(nc, [arrays], core_ids=[0])
    return r.results[0]["out"].reshape(8, 512, 256)
```
